# Optimizing a Trainium2 kernel written in Bass

```python
import numpy as np
import jax
import jax.numpy as jnp

def _softmax(x, axis=-1):
    return jax.nn.softmax(x, axis=axis)

def _gelu(x):
    return jax.nn.gelu(x, approximate=True)

def _silu(x):
    return jax.nn.silu(x)

def _sigmoid(x):
    return jax.nn.sigmoid(x)

def _layernorm(x, axis=-1, eps=1e-05):
    m = jnp.mean(x, axis=axis, keepdims=True)
    v = jnp.var(x, axis=axis, keepdims=True)
    return (x - m) / jnp.sqrt(v + eps)

def _scatter_add(tgt, idx, src, axis=0):
    return tgt.at[idx].add(src)

def _segment_sum(src, seg, n):
    return jax.ops.segment_sum(src, seg, n)
kernel_name = 'mk_sandwich_d4_jaxref_r8_118db4'

def setup_inputs(seed: int=0):
    np.random.seed(seed)
    _w = jnp.asarray

    def _L0_attn_setup():
        import jax, jax.numpy as jnp
        import numpy as np
        DIM = 128
        HID = 512
        NUM_HEADS = 4
        WINDOW = 64
        NUM_PM = 64
        NEG = -1e+30

        def _swa(x_in, wq, wk, wv, wo):
            B, S, D = x_in.shape
            h, dh = (NUM_HEADS, D // NUM_HEADS)
            q = (x_in @ wq.T).reshape(B, S, h, dh).transpose(0, 2, 1, 3)
            k = (x_in @ wk.T).reshape(B, S, h, dh).transpose(0, 2, 1, 3)
            v = (x_in @ wv.T).reshape(B, S, h, dh).transpose(0, 2, 1, 3)
            i = jnp.arange(S)[:, None]
            j = jnp.arange(S)[None, :]
            mask = (j <= i) & (j > i - WINDOW)
            logits = jnp.einsum('bhqd,bhkd->bhqk', q, k) / np.sqrt(dh).astype(np.float32)
            logits = jnp.where(mask, logits, NEG)
            attn = jax.nn.softmax(logits, axis=-1)
            out = jnp.einsum('bhqk,bhkd->bhqd', attn, v)
            out = out.transpose(0, 2, 1, 3).reshape(B, S, D)
            return out @ wo.T

        def _mlp(w1, b1, w2, b2, x):
            return jax.nn.silu(x @ w1.T + b1) @ w2.T + b2
        key = jax.random.key(seed)
        ks = jax.random.split(key, 12)
        B, S = (2, 256)
        sc = 0.02
        n = lambda k, shape, s=sc: jax.random.normal(k, shape, jnp.float32) * s
        return {'x': n(ks[0], (B, S, DIM), 1.0), 'mem': n(ks[1], (NUM_PM, DIM), 1.0), 'wq': n(ks[2], (DIM, DIM)), 'wk': n(ks[3], (DIM, DIM)), 'wv': n(ks[4], (DIM, DIM)), 'wo': n(ks[5], (DIM, DIM)), 'w1': n(ks[6], (HID, DIM)), 'b1': jnp.zeros((HID,), jnp.float32), 'w2': n(ks[7], (DIM, HID)), 'b2': jnp.zeros((DIM,), jnp.float32), 'lin1': n(ks[8], (DIM, DIM)), 'lin2': n(ks[9], (DIM, DIM)), 'alpha': jnp.float32(0.0001), 'theta': jnp.float32(0.0001)}
    _L0_attn_in = _L0_attn_setup()

    def _L0_ffn_setup():
        import jax, jax.numpy as jnp
        import numpy as np
        B, N, C, H, REG = (1, 2309, 128, 16, 5)
        D = C // H
        key = jax.random.key(seed)
        k0, k1, k2, k3 = jax.random.split(key, 4)
        x = jax.random.normal(k0, (B, N, C), dtype=jnp.float32)
        g_info = jax.random.normal(k1, (12, 2, C), dtype=jnp.float32)
        W_qkv = jax.random.normal(k2, (C, 3 * C), dtype=jnp.float32) * 0.02
        W_proj = jax.random.normal(k3, (C, C), dtype=jnp.float32) * 0.02
        b_proj = jnp.zeros((C,), dtype=jnp.float32)
        return {'x': x, 'g_info': g_info, 'W_qkv': W_qkv, 'W_proj': W_proj, 'b_proj': b_proj}
    _L0_ffn_in = _L0_ffn_setup()

    def _L1_attn_setup():
        import jax, jax.numpy as jnp
        import numpy as np
        DIM = 128
        HEADS = 16
        HEAD_DIM = DIM // HEADS
        B, N = (4, 512)

        def _reference_tuple_inner(x, Wq, bq, Wk, bk, Wv, bv, Wo, bo, stdp):
            b, n, d = x.shape
            h, dh = (HEADS, HEAD_DIM)

            def proj(W, bias):
                return (x @ W.T + bias).reshape(b, n, h, dh).transpose(0, 2, 1, 3)
            Q = jax.nn.elu(proj(Wq, bq)) + 1.0
            K = jax.nn.elu(proj(Wk, bk)) + 1.0
            V = proj(Wv, bv)
            stdp_w = jax.nn.sigmoid(stdp).reshape(1, h, 1, 1)
            KV = jnp.einsum('bhnd,bhnv->bhdv', K, V)
            K_sum = K.sum(axis=2)
            numerator = jnp.einsum('bhnd,bhdv->bhnv', Q, KV)
            denominator = jnp.einsum('bhnd,bhd->bhn', Q, K_sum)[..., None] + 1e-06
            attn_out = numerator / denominator * stdp_w
            out = attn_out.transpose(0, 2, 1, 3).reshape(b, n, d)
            out = out @ Wo.T + bo
            return (out, jax.lax.stop_gradient(stdp))
        key = jax.random.key(seed)
        ks = jax.random.split(key, 10)
        s = 1.0 / np.sqrt(DIM)
        return {'x': jax.random.normal(ks[0], (B, N, DIM), dtype=jnp.float32), 'Wq': jax.random.uniform(ks[1], (DIM, DIM), jnp.float32, -s, s), 'bq': jax.random.uniform(ks[2], (DIM,), jnp.float32, -s, s), 'Wk': jax.random.uniform(ks[3], (DIM, DIM), jnp.float32, -s, s), 'bk': jax.random.uniform(ks[4], (DIM,), jnp.float32, -s, s), 'Wv': jax.random.uniform(ks[5], (DIM, DIM), jnp.float32, -s, s), 'bv': jax.random.uniform(ks[6], (DIM,), jnp.float32, -s, s), 'Wo': jax.random.uniform(ks[7], (DIM, DIM), jnp.float32, -s, s), 'bo': jax.random.uniform(ks[8], (DIM,), jnp.float32, -s, s), 'stdp': jnp.ones((HEADS,), dtype=jnp.float32)}
    _L1_attn_in = _L1_attn_setup()

    def _L1_ffn_setup():
        import jax, jax.numpy as jnp
        import numpy as np
        E, D, F = (16, 128, 256)
        B, N = (2, 256)
        LN_EPS = 1e-05
        key = jax.random.key(seed)
        ks = jax.random.split(key, 8)
        s = 0.02
        return {'x': jax.random.normal(ks[0], (B, N, D), dtype=jnp.float32), 'router_w': jax.random.normal(ks[1], (E, D), dtype=jnp.float32) * s, 'router_b': jnp.zeros((E,), dtype=jnp.float32), 'w1': jax.random.normal(ks[2], (E, F, D), dtype=jnp.float32) * s, 'w2': jax.random.normal(ks[3], (E, D, F), dtype=jnp.float32) * s, 'w3': jax.random.normal(ks[4], (E, F, D), dtype=jnp.float32) * s, 'ln_g': jnp.ones((E, D), dtype=jnp.float32), 'ln_b': jnp.zeros((E, D), dtype=jnp.float32)}
    _L1_ffn_in = _L1_ffn_setup()

    def _L2_attn_setup():
        import jax, jax.numpy as jnp
        import numpy as np
        D_MODEL = 128
        D_STATE = 16
        D_CONV = 3
        D_INNER = 2 * D_MODEL
        B, S = (4, 256)

        def _mamba_forward(x, in_proj_w, conv_w, conv_b, x_proj_w, dt_proj_w, dt_proj_b, out_proj_w, A_log, D_param):
            combined = x @ in_proj_w
            u, x_gate = jnp.split(combined, 2, axis=-1)
            u_c = jax.lax.conv_general_dilated(u.transpose(0, 2, 1), conv_w, window_strides=(1,), padding='SAME', feature_group_count=D_INNER, dimension_numbers=('NCW', 'OIW', 'NCW'))
            u = jax.nn.silu((u_c + conv_b[None, :, None]).transpose(0, 2, 1))
            x_dbl = u @ x_proj_w
            delta, b, c = jnp.split(x_dbl, [D_INNER, D_INNER + D_STATE], axis=-1)
            delta = jax.nn.softplus(delta @ dt_proj_w + dt_proj_b)
            a = -jnp.exp(A_log)

            def step(h, inp):
                u_t, d_t, b_t, c_t = inp
                h = jnp.exp(d_t[:, :, None] * a) * h + d_t[:, :, None] * b_t[:, None, :] * u_t[:, :, None]
                y_t = jnp.einsum('bds,bs->bd', h, c_t)
                return (h, y_t)
            h0 = jnp.zeros((x.shape[0], D_INNER, D_STATE), x.dtype)
            xs = (u.transpose(1, 0, 2), delta.transpose(1, 0, 2), b.transpose(1, 0, 2), c.transpose(1, 0, 2))
            _, ys = jax.lax.scan(step, h0, xs)
            y = ys.transpose(1, 0, 2)
            y = y + u * D_param
            y = y * jax.nn.silu(x_gate)
            return y @ out_proj_w
        key = jax.random.key(seed)
        ks = jax.random.split(key, 9)
        s = 0.02
        x = jax.random.normal(ks[0], (B, S, D_MODEL), jnp.float32)
        in_proj_w = jax.random.normal(ks[1], (D_MODEL, 2 * D_INNER), jnp.float32) * s
        conv_w = jax.random.normal(ks[2], (D_INNER, 1, D_CONV), jnp.float32) * s
        conv_b = jax.random.normal(ks[3], (D_INNER,), jnp.float32) * s
        x_proj_w = jax.random.normal(ks[4], (D_INNER, D_INNER + 2 * D_STATE), jnp.float32) * s
        dt_proj_w = jax.random.normal(ks[5], (D_INNER, D_INNER), jnp.float32) * s
        dt_proj_b = jax.random.normal(ks[6], (D_INNER,), jnp.float32) * s
        out_proj_w = jax.random.normal(ks[7], (D_INNER, D_MODEL), jnp.float32) * s
        A_log = jnp.tile(jnp.log(jnp.arange(1, D_STATE + 1, dtype=jnp.float32))[None, :], (D_INNER, 1))
        D_param = jnp.ones((D_INNER,), jnp.float32)
        return {'x': x, 'in_proj_w': in_proj_w, 'conv_w': conv_w, 'conv_b': conv_b, 'x_proj_w': x_proj_w, 'dt_proj_w': dt_proj_w, 'dt_proj_b': dt_proj_b, 'out_proj_w': out_proj_w, 'A_log': A_log, 'D_param': D_param}
    _L2_attn_in = _L2_attn_setup()

    def _L2_ffn_setup():
        import jax, jax.numpy as jnp
        import numpy as np
        B, S, D = (2, 256, 128)
        H, HKV = (16, 4)
        HD = D // H
        F, E, K = (256, 8, 2)
        THETA = 10000.0
        EPS = 1e-05

        def _rmsnorm(x, w):
            return x * jax.lax.rsqrt(jnp.mean(x * x, axis=-1, keepdims=True) + EPS) * w

        def _rope_cos_sin(seq_len, head_dim, theta):
            inv_freq = 1.0 / theta ** (jnp.arange(0, head_dim, 2, dtype=jnp.float32) / head_dim)
            freqs = jnp.arange(seq_len, dtype=jnp.float32)[:, None] * inv_freq
            return (jnp.cos(freqs), jnp.sin(freqs))

        def _apply_rope(x, cos, sin):
            x1, x2 = jnp.split(x, 2, axis=-1)
            c = cos[None, :, None, :]
            s = sin[None, :, None, :]
            return jnp.concatenate([x1 * c - x2 * s, x2 * c + x1 * s], axis=-1)
        key = jax.random.key(seed)
        ks = jax.random.split(key, 12)
        s = 0.02
        return {'hidden_states': jax.random.normal(ks[0], (B, S, D), jnp.float32), 'ln1_w': 1.0 + 0.1 * jax.random.normal(ks[1], (D,), jnp.float32), 'ln2_w': 1.0 + 0.1 * jax.random.normal(ks[2], (D,), jnp.float32), 'Wq': s * jax.random.normal(ks[3], (D, H * HD), jnp.float32), 'Wk': s * jax.random.normal(ks[4], (D, HKV * HD), jnp.float32), 'Wv': s * jax.random.normal(ks[5], (D, HKV * HD), jnp.float32), 'Wo': s * jax.random.normal(ks[6], (H * HD, D), jnp.float32), 'Wr': s * jax.random.normal(ks[7], (D, E), jnp.float32), 'Wg': s * jax.random.normal(ks[8], (E, D, F), jnp.float32), 'Wu': s * jax.random.normal(ks[9], (E, D, F), jnp.float32), 'Wd': s * jax.random.normal(ks[10], (E, F, D), jnp.float32)}
    _L2_ffn_in = _L2_ffn_setup()

    def _L3_attn_setup():
        import jax, jax.numpy as jnp
        import numpy as np
        D_MODEL = 128
        N_HEADS = 16
        HEAD_DIM = D_MODEL // N_HEADS
        D_LATENT = 32
        LAMBDA_DECAY = 0.01
        TIME_STEP = 0.01
        CLAMP = 10000.0

        def _reference_tuple_inner(x, Wq, Wk, Wv, Wo, W_down_kv, W_up_k, W_up_v):
            B, S, _ = x.shape
            q = x @ Wq
            k = x @ Wk
            v = x @ Wv
            latent_kv = (k + v) @ W_down_kv
            k_rec = latent_kv @ W_up_k
            v_rec = latent_kv @ W_up_v

            def heads(t):
                return t.reshape(B, S, N_HEADS, HEAD_DIM).transpose(0, 2, 1, 3)
            qh, kh, vh = (heads(q), heads(k_rec), heads(v_rec))
            scale = 1.0 / (jnp.sqrt(jnp.float32(D_MODEL)) + 1e-08)
            scores = jnp.einsum('bhqd,bhkd->bhqk', qh, kh) * scale
            scores = jnp.clip(jnp.nan_to_num(scores, nan=-1000000000.0), -CLAMP, CLAMP)
            idx = jnp.arange(S, dtype=jnp.float32)
            decay = jnp.exp(-LAMBDA_DECAY * TIME_STEP * jnp.abs(idx[:, None] - idx[None, :]))
            scores = scores * decay[None, None, :, :]
            scores = jnp.clip(jnp.nan_to_num(scores, nan=-1000000000.0), -CLAMP, CLAMP)
            attn = jax.nn.softmax(scores, axis=-1)
            out = jnp.einsum('bhqk,bhkd->bhqd', attn, vh)
            out = out.transpose(0, 2, 1, 3).reshape(B, S, D_MODEL)
            return (out @ Wo, latent_kv)
        key = jax.random.key(seed)
        ks = jax.random.split(key, 8)
        B, S = (2, 256)

        def w(k, i, o):
            return jax.random.normal(k, (i, o), dtype=jnp.float32) * 0.02
        return {'x': jax.random.normal(ks[0], (B, S, D_MODEL), dtype=jnp.float32), 'Wq': w(ks[1], D_MODEL, D_MODEL), 'Wk': w(ks[2], D_MODEL, D_MODEL), 'Wv': w(ks[3], D_MODEL, D_MODEL), 'Wo': w(ks[4], D_MODEL, D_MODEL), 'W_down_kv': w(ks[5], D_MODEL, D_LATENT), 'W_up_k': w(ks[6], D_LATENT, D_MODEL), 'W_up_v': w(ks[7], D_LATENT, D_MODEL)}
    _L3_attn_in = _L3_attn_setup()

    def _L3_ffn_setup():
        import jax, jax.numpy as jnp
        import numpy as np
        DIM = 128
        DEPTH = 6
        HEADS = 16
        DIM_HEAD = 64
        WINDOW = 32
        INNER = HEADS * DIM_HEAD
        DIM_INNER = int(DIM * 4 * 2 / 3)
        QK_SCALE = 8.0

        def shift_tokens(t):
            a, s = jnp.split(t, 2, -1)
            s = jnp.pad(s, ((0, 0), (1, 0), (0, 0)))[:, :-1]
            return jnp.concatenate([a, s], -1)

        def l2norm(t):
            return t / jnp.maximum(jnp.linalg.norm(t, axis=-1, keepdims=True), 1e-12)

        def rotate_half(x):
            x1, x2 = jnp.split(x, 2, -1)
            return jnp.concatenate([-x2, x1], -1)

        def rotary_tables(n):
            half = jnp.arange(0, DIM_HEAD, 2, dtype=jnp.float32)
            inv_freq = 1.0 / 10000.0 ** (half / DIM_HEAD)
            t = jnp.arange(n, dtype=jnp.float32)
            freqs = t[:, None] * inv_freq[None, :]
            freqs = jnp.concatenate([freqs, freqs], -1)
            base_scale = (half + 0.4 * DIM_HEAD) / (1.4 * DIM_HEAD)
            power = (t - n // 2) / (WINDOW // 2)
            scale = base_scale[None, :] ** power[:, None]
            scale = jnp.concatenate([scale, scale], -1)
            return (freqs, scale)

        def local_attention(q, k, v):
            b, h, n, d = q.shape
            w = WINDOW
            nw = n // w
            bq = q.reshape(b, h, nw, w, d)
            bk = k.reshape(b, h, nw, w, d)
            bv = v.reshape(b, h, nw, w, d)

            def look(t):
                p = jnp.pad(t, ((0, 0), (0, 0), (1, 0), (0, 0), (0, 0)))
                return jnp.concatenate([p[:, :, :nw], p[:, :, 1:]], axis=3)
            bk2, bv2 = (look(bk), look(bv))
            seq = jnp.arange(n).reshape(nw, w)
            seq_p = jnp.pad(seq, ((1, 0), (0, 0)), constant_values=-1)
            jt = jnp.concatenate([seq_p[:nw], seq_p[1:]], axis=1)
            it = seq[:, :, None]
            jb = jt[:, None, :]
            mask = (it < jb) | (it > jb + w) | (jb == -1)
            sim = jnp.einsum('bhwie,bhwje->bhwij', bq, bk2) * QK_SCALE
            sim = jnp.where(mask, -jnp.finfo(sim.dtype).max, sim)
            attn = jax.nn.softmax(sim, -1)
            out = jnp.einsum('bhwij,bhwje->bhwie', attn, bv2)
            return out.reshape(b, h, n, d)

        def attn_layer(x, Wqkv, qs, ksc, Wo):
            b, n, _ = x.shape
            qkv = x @ Wqkv
            q, k, v = jnp.split(qkv, 3, -1)
            sh = lambda t: t.reshape(b, n, HEADS, DIM_HEAD).transpose(0, 2, 1, 3)
            q, k, v = (sh(q), sh(k), sh(v))
            q = l2norm(q) * qs
            k = l2norm(k) * ksc
            freqs, scale = rotary_tables(n)
            cos, sin = (jnp.cos(freqs), jnp.sin(freqs))
            q = q * cos * scale + rotate_half(q) * sin * scale
            inv = 1.0 / scale
            k = k * cos * inv + rotate_half(k) * sin * inv
            out = local_attention(q, k, v)
            out = out.transpose(0, 2, 1, 3).reshape(b, n, INNER)
            return out @ Wo

        def ffn_layer(x, g, bln, W1, b1, W2, b2):
            mu = x.mean(-1, keepdims=True)
            var = ((x - mu) ** 2).mean(-1, keepdims=True)
            xn = (x - mu) / jnp.sqrt(var + 1e-05) * g + bln
            hg = xn @ W1 + b1
            a, gate = jnp.split(hg, 2, -1)
            return a * jax.nn.gelu(gate, approximate=False) @ W2 + b2
        key = jax.random.key(seed)
        ks = jax.random.split(key, 8)
        B, N = (2, 256)
        init = lambda k, shape: jax.random.normal(k, shape, jnp.float32) * 0.02
        return {'x': jax.random.normal(ks[0], (B, N, DIM), jnp.float32), 'Wqkv': init(ks[1], (DEPTH, DIM, 3 * INNER)), 'q_scale': jnp.ones((DEPTH, DIM_HEAD), jnp.float32), 'k_scale': jnp.ones((DEPTH, DIM_HEAD), jnp.float32), 'Wo': init(ks[2], (DEPTH, INNER, DIM)), 'ln_g': jnp.ones((DEPTH, DIM), jnp.float32), 'ln_b': jnp.zeros((DEPTH, DIM), jnp.float32), 'W1': init(ks[3], (DEPTH, DIM, 2 * DIM_INNER)), 'b1': jnp.zeros((DEPTH, 2 * DIM_INNER), jnp.float32), 'W2': init(ks[4], (DEPTH, DIM_INNER, DIM)), 'b2': jnp.zeros((DEPTH, DIM), jnp.float32)}
    _L3_ffn_in = _L3_ffn_setup()
    _d = {'L0_attn_x': _L0_attn_in['x'], 'L0_attn_mem': _L0_attn_in['mem'], 'L0_attn_wq': _L0_attn_in['wq'], 'L0_attn_wk': _L0_attn_in['wk'], 'L0_attn_wv': _L0_attn_in['wv'], 'L0_attn_wo': _L0_attn_in['wo'], 'L0_attn_w1': _L0_attn_in['w1'], 'L0_attn_b1': _L0_attn_in['b1'], 'L0_attn_w2': _L0_attn_in['w2'], 'L0_attn_b2': _L0_attn_in['b2'], 'L0_attn_lin1': _L0_attn_in['lin1'], 'L0_attn_lin2': _L0_attn_in['lin2'], 'L0_attn_alpha': _L0_attn_in['alpha'], 'L0_attn_theta': _L0_attn_in['theta'], 'L0_ffn_g_info': _L0_ffn_in['g_info'], 'L0_ffn_W_qkv': _L0_ffn_in['W_qkv'], 'L0_ffn_W_proj': _L0_ffn_in['W_proj'], 'L0_ffn_b_proj': _L0_ffn_in['b_proj'], 'L1_attn_Wq': _L1_attn_in['Wq'], 'L1_attn_bq': _L1_attn_in['bq'], 'L1_attn_Wk': _L1_attn_in['Wk'], 'L1_attn_bk': _L1_attn_in['bk'], 'L1_attn_Wv': _L1_attn_in['Wv'], 'L1_attn_bv': _L1_attn_in['bv'], 'L1_attn_Wo': _L1_attn_in['Wo'], 'L1_attn_bo': _L1_attn_in['bo'], 'L1_attn_stdp': _L1_attn_in['stdp'], 'L1_ffn_router_w': _L1_ffn_in['router_w'], 'L1_ffn_router_b': _L1_ffn_in['router_b'], 'L1_ffn_w1': _L1_ffn_in['w1'], 'L1_ffn_w2': _L1_ffn_in['w2'], 'L1_ffn_w3': _L1_ffn_in['w3'], 'L1_ffn_ln_g': _L1_ffn_in['ln_g'], 'L1_ffn_ln_b': _L1_ffn_in['ln_b'], 'L2_attn_in_proj_w': _L2_attn_in['in_proj_w'], 'L2_attn_conv_w': _L2_attn_in['conv_w'], 'L2_attn_conv_b': _L2_attn_in['conv_b'], 'L2_attn_x_proj_w': _L2_attn_in['x_proj_w'], 'L2_attn_dt_proj_w': _L2_attn_in['dt_proj_w'], 'L2_attn_dt_proj_b': _L2_attn_in['dt_proj_b'], 'L2_attn_out_proj_w': _L2_attn_in['out_proj_w'], 'L2_attn_A_log': _L2_attn_in['A_log'], 'L2_attn_D_param': _L2_attn_in['D_param'], 'L2_ffn_ln1_w': _L2_ffn_in['ln1_w'], 'L2_ffn_ln2_w': _L2_ffn_in['ln2_w'], 'L2_ffn_Wq': _L2_ffn_in['Wq'], 'L2_ffn_Wk': _L2_ffn_in['Wk'], 'L2_ffn_Wv': _L2_ffn_in['Wv'], 'L2_ffn_Wo': _L2_ffn_in['Wo'], 'L2_ffn_Wr': _L2_ffn_in['Wr'], 'L2_ffn_Wg': _L2_ffn_in['Wg'], 'L2_ffn_Wu': _L2_ffn_in['Wu'], 'L2_ffn_Wd': _L2_ffn_in['Wd'], 'L3_attn_Wq': _L3_attn_in['Wq'], 'L3_attn_Wk': _L3_attn_in['Wk'], 'L3_attn_Wv': _L3_attn_in['Wv'], 'L3_attn_Wo': _L3_attn_in['Wo'], 'L3_attn_W_down_kv': _L3_attn_in['W_down_kv'], 'L3_attn_W_up_k': _L3_attn_in['W_up_k'], 'L3_attn_W_up_v': _L3_attn_in['W_up_v'], 'L3_ffn_Wqkv': _L3_ffn_in['Wqkv'], 'L3_ffn_q_scale': _L3_ffn_in['q_scale'], 'L3_ffn_k_scale': _L3_ffn_in['k_scale'], 'L3_ffn_Wo': _L3_ffn_in['Wo'], 'L3_ffn_ln_g': _L3_ffn_in['ln_g'], 'L3_ffn_ln_b': _L3_ffn_in['ln_b'], 'L3_ffn_W1': _L3_ffn_in['W1'], 'L3_ffn_b1': _L3_ffn_in['b1'], 'L3_ffn_W2': _L3_ffn_in['W2'], 'L3_ffn_b2': _L3_ffn_in['b2']}
    _x0 = _d['L0_attn_x']
    _d['L0_attn_x'] = jax.random.normal(jax.random.fold_in(jax.random.key(seed), 1), (8, 256, 128), dtype=_x0.dtype)
    del _x0
    return _d

def reference(L0_attn_x, L0_attn_mem, L0_attn_wq, L0_attn_wk, L0_attn_wv, L0_attn_wo, L0_attn_w1, L0_attn_b1, L0_attn_w2, L0_attn_b2, L0_attn_lin1, L0_attn_lin2, L0_attn_alpha, L0_attn_theta, L0_ffn_g_info, L0_ffn_W_qkv, L0_ffn_W_proj, L0_ffn_b_proj, L1_attn_Wq, L1_attn_bq, L1_attn_Wk, L1_attn_bk, L1_attn_Wv, L1_attn_bv, L1_attn_Wo, L1_attn_bo, L1_attn_stdp, L1_ffn_router_w, L1_ffn_router_b, L1_ffn_w1, L1_ffn_w2, L1_ffn_w3, L1_ffn_ln_g, L1_ffn_ln_b, L2_attn_in_proj_w, L2_attn_conv_w, L2_attn_conv_b, L2_attn_x_proj_w, L2_attn_dt_proj_w, L2_attn_dt_proj_b, L2_attn_out_proj_w, L2_attn_A_log, L2_attn_D_param, L2_ffn_ln1_w, L2_ffn_ln2_w, L2_ffn_Wq, L2_ffn_Wk, L2_ffn_Wv, L2_ffn_Wo, L2_ffn_Wr, L2_ffn_Wg, L2_ffn_Wu, L2_ffn_Wd, L3_attn_Wq, L3_attn_Wk, L3_attn_Wv, L3_attn_Wo, L3_attn_W_down_kv, L3_attn_W_up_k, L3_attn_W_up_v, L3_ffn_Wqkv, L3_ffn_q_scale, L3_ffn_k_scale, L3_ffn_Wo, L3_ffn_ln_g, L3_ffn_ln_b, L3_ffn_W1, L3_ffn_b1, L3_ffn_W2, L3_ffn_b2):

    def _L0_attn_ref(x, mem, wq, wk, wv, wo, w1, b1, w2, b2, lin1, lin2, alpha, theta):
        import jax, jax.numpy as jnp
        import numpy as np
        DIM = 128
        HID = 512
        NUM_HEADS = 4
        WINDOW = 64
        NUM_PM = 64
        NEG = -1e+30

        def _swa(x_in, wq, wk, wv, wo):
            B, S, D = x_in.shape
            h, dh = (NUM_HEADS, D // NUM_HEADS)
            q = (x_in @ wq.T).reshape(B, S, h, dh).transpose(0, 2, 1, 3)
            k = (x_in @ wk.T).reshape(B, S, h, dh).transpose(0, 2, 1, 3)
            v = (x_in @ wv.T).reshape(B, S, h, dh).transpose(0, 2, 1, 3)
            i = jnp.arange(S)[:, None]
            j = jnp.arange(S)[None, :]
            mask = (j <= i) & (j > i - WINDOW)
            logits = jnp.einsum('bhqd,bhkd->bhqk', q, k) / np.sqrt(dh).astype(np.float32)
            logits = jnp.where(mask, logits, NEG)
            attn = jax.nn.softmax(logits, axis=-1)
            out = jnp.einsum('bhqk,bhkd->bhqd', attn, v)
            out = out.transpose(0, 2, 1, 3).reshape(B, S, D)
            return out @ wo.T

        def _mlp(w1, b1, w2, b2, x):
            return jax.nn.silu(x @ w1.T + b1) @ w2.T + b2
        B, S, D = x.shape
        pm = jnp.broadcast_to(mem[None], (B, NUM_PM, D))
        x_in = jnp.concatenate([pm, x], axis=1)
        out_swa = _swa(x_in, wq, wk, wv, wo)
        k_flat = x_in.reshape(-1, D)
        v_flat = out_swa.reshape(-1, D)

        def loss_fn(params):
            pred = _mlp(*params, k_flat)
            return 0.5 * jnp.sum((pred - v_flat) ** 2)
        grads = jax.grad(loss_fn)((w1, b1, w2, b2))
        upd = jax.tree_util.tree_map(lambda p, g: (1.0 - alpha) * p - theta * g, (w1, b1, w2, b2), grads)
        out_mem = _mlp(*upd, k_flat).reshape(x_in.shape)
        g1 = jax.nn.sigmoid(out_swa @ lin1.T)
        g2 = jax.nn.sigmoid(out_mem @ lin2.T)
        out_merged = g1 * out_swa + g2 * out_mem
        return out_merged[:, NUM_PM:, :]

    def _L0_ffn_ref(x, g_info, W_qkv, W_proj, b_proj):
        import jax, jax.numpy as jnp
        import numpy as np
        B, N, C, H, REG = (1, 2309, 128, 16, 5)
        D = C // H
        Bx, Nx, Cx = x.shape
        scale = D ** (-0.5)
        qkv = (x @ W_qkv).reshape(Bx, Nx, 3, H, D)
        q, k, v = (qkv[:, :, 0], qkv[:, :, 1], qkv[:, :, 2])
        g_layer = g_info[0].reshape(-1, H, D)
        q_g = g_layer[0]
        q_pure = q[:, REG:]
        q_n = q_pure / jnp.linalg.norm(q_pure, axis=-1, keepdims=True)
        qg_n = q_g / jnp.linalg.norm(q_g, axis=-1, keepdims=True)
        sim = (qg_n[None, None] * q_n).sum(-1).mean(-1)
        sim = (sim - sim.min()) / (sim.max() - sim.min())
        pos = sim > 0.9
        logits = jnp.einsum('bqhd,bkhd->bhqk', q * scale, k)

        def masked_attn(tok_mask):
            key_mask = jnp.concatenate([jnp.ones((Bx, REG), bool), tok_mask], axis=1)
            l = jnp.where(key_mask[:, None, None, :], logits, -jnp.inf)
            a = jax.nn.softmax(l, axis=-1)
            return jnp.einsum('bhqk,bkhd->bqhd', a, v)
        x_pos = masked_attn(pos)
        x_neg = masked_attn(~pos)
        reg_out = (x_pos[:, :REG] + x_neg[:, :REG]) * 0.5
        tok_out = jnp.where(pos[:, :, None, None], x_pos[:, REG:], x_neg[:, REG:])
        out = jnp.concatenate([reg_out, tok_out], axis=1).reshape(Bx, Nx, Cx)
        return out @ W_proj + b_proj

    def _L1_attn_ref(x, Wq, bq, Wk, bk, Wv, bv, Wo, bo, stdp):
        import jax, jax.numpy as jnp
        import numpy as np
        DIM = 128
        HEADS = 16
        HEAD_DIM = DIM // HEADS
        B, N = (4, 512)

        def _reference_tuple_inner(x, Wq, bq, Wk, bk, Wv, bv, Wo, bo, stdp):
            b, n, d = x.shape
            h, dh = (HEADS, HEAD_DIM)

            def proj(W, bias):
                return (x @ W.T + bias).reshape(b, n, h, dh).transpose(0, 2, 1, 3)
            Q = jax.nn.elu(proj(Wq, bq)) + 1.0
            K = jax.nn.elu(proj(Wk, bk)) + 1.0
            V = proj(Wv, bv)
            stdp_w = jax.nn.sigmoid(stdp).reshape(1, h, 1, 1)
            KV = jnp.einsum('bhnd,bhnv->bhdv', K, V)
            K_sum = K.sum(axis=2)
            numerator = jnp.einsum('bhnd,bhdv->bhnv', Q, KV)
            denominator = jnp.einsum('bhnd,bhd->bhn', Q, K_sum)[..., None] + 1e-06
            attn_out = numerator / denominator * stdp_w
            out = attn_out.transpose(0, 2, 1, 3).reshape(b, n, d)
            out = out @ Wo.T + bo
            return (out, jax.lax.stop_gradient(stdp))
        return _reference_tuple_inner(x, Wq, bq, Wk, bk, Wv, bv, Wo, bo, stdp)[0]

    def _L1_ffn_ref(x, router_w, router_b, w1, w2, w3, ln_g, ln_b):
        import jax, jax.numpy as jnp
        import numpy as np
        E, D, F = (16, 128, 256)
        B, N = (2, 256)
        LN_EPS = 1e-05
        'SparseMixtureOfExperts.forward (eval mode: no router noise, dropout=0).\n\n            Top-2 routing over softmax(router logits), renormalized; each selected\n            expert applies LayerNorm(SwiGLU(x)). Exact math of the torch masked loop,\n            expressed as a scan over experts with zero coefficients for unrouted tokens.\n            '
        Bx, Nx, Dx = x.shape
        xf = x.reshape(-1, Dx)
        logits = xf @ router_w.T + router_b
        probs = jax.nn.softmax(logits, axis=-1)
        top_w, top_e = jax.lax.top_k(probs, 2)
        top_w = top_w / jnp.sum(top_w, axis=-1, keepdims=True)

        def body(acc, params):
            W1, W2, W3, gm, bt, eid = params
            h = jax.nn.silu(xf @ W1.T) * (xf @ W3.T)
            y = h @ W2.T
            mu = jnp.mean(y, axis=-1, keepdims=True)
            var = jnp.var(y, axis=-1, keepdims=True)
            yn = (y - mu) / jnp.sqrt(var + LN_EPS) * gm + bt
            coeff = jnp.sum(jnp.where(top_e == eid, top_w, 0.0), axis=-1)
            return (acc + coeff[:, None] * yn, None)
        eids = jnp.arange(router_w.shape[0], dtype=top_e.dtype)
        out, _ = jax.lax.scan(body, jnp.zeros_like(xf), (w1, w2, w3, ln_g, ln_b, eids))
        return out.reshape(Bx, Nx, Dx)

    def _L2_attn_ref(x, in_proj_w, conv_w, conv_b, x_proj_w, dt_proj_w, dt_proj_b, out_proj_w, A_log, D_param):
        import jax, jax.numpy as jnp
        import numpy as np
        D_MODEL = 128
        D_STATE = 16
        D_CONV = 3
        D_INNER = 2 * D_MODEL
        B, S = (4, 256)

        def _mamba_forward(x, in_proj_w, conv_w, conv_b, x_proj_w, dt_proj_w, dt_proj_b, out_proj_w, A_log, D_param):
            combined = x @ in_proj_w
            u, x_gate = jnp.split(combined, 2, axis=-1)
            u_c = jax.lax.conv_general_dilated(u.transpose(0, 2, 1), conv_w, window_strides=(1,), padding='SAME', feature_group_count=D_INNER, dimension_numbers=('NCW', 'OIW', 'NCW'))
            u = jax.nn.silu((u_c + conv_b[None, :, None]).transpose(0, 2, 1))
            x_dbl = u @ x_proj_w
            delta, b, c = jnp.split(x_dbl, [D_INNER, D_INNER + D_STATE], axis=-1)
            delta = jax.nn.softplus(delta @ dt_proj_w + dt_proj_b)
            a = -jnp.exp(A_log)

            def step(h, inp):
                u_t, d_t, b_t, c_t = inp
                h = jnp.exp(d_t[:, :, None] * a) * h + d_t[:, :, None] * b_t[:, None, :] * u_t[:, :, None]
                y_t = jnp.einsum('bds,bs->bd', h, c_t)
                return (h, y_t)
            h0 = jnp.zeros((x.shape[0], D_INNER, D_STATE), x.dtype)
            xs = (u.transpose(1, 0, 2), delta.transpose(1, 0, 2), b.transpose(1, 0, 2), c.transpose(1, 0, 2))
            _, ys = jax.lax.scan(step, h0, xs)
            y = ys.transpose(1, 0, 2)
            y = y + u * D_param
            y = y * jax.nn.silu(x_gate)
            return y @ out_proj_w
        return _mamba_forward(x, in_proj_w, conv_w, conv_b, x_proj_w, dt_proj_w, dt_proj_b, out_proj_w, A_log, D_param)

    def _L2_ffn_ref(hidden_states, ln1_w, ln2_w, Wq, Wk, Wv, Wo, Wr, Wg, Wu, Wd):
        import jax, jax.numpy as jnp
        import numpy as np
        B, S, D = (2, 256, 128)
        H, HKV = (16, 4)
        HD = D // H
        F, E, K = (256, 8, 2)
        THETA = 10000.0
        EPS = 1e-05

        def _rmsnorm(x, w):
            return x * jax.lax.rsqrt(jnp.mean(x * x, axis=-1, keepdims=True) + EPS) * w

        def _rope_cos_sin(seq_len, head_dim, theta):
            inv_freq = 1.0 / theta ** (jnp.arange(0, head_dim, 2, dtype=jnp.float32) / head_dim)
            freqs = jnp.arange(seq_len, dtype=jnp.float32)[:, None] * inv_freq
            return (jnp.cos(freqs), jnp.sin(freqs))

        def _apply_rope(x, cos, sin):
            x1, x2 = jnp.split(x, 2, axis=-1)
            c = cos[None, :, None, :]
            s = sin[None, :, None, :]
            return jnp.concatenate([x1 * c - x2 * s, x2 * c + x1 * s], axis=-1)
        b, s, d = hidden_states.shape
        residual = hidden_states
        h = _rmsnorm(hidden_states, ln1_w)
        q = (h @ Wq).reshape(b, s, H, HD)
        k = (h @ Wk).reshape(b, s, HKV, HD)
        v = (h @ Wv).reshape(b, s, HKV, HD)
        cos, sin = _rope_cos_sin(s, HD, THETA)
        q = _apply_rope(q, cos, sin)
        k = _apply_rope(k, cos, sin)
        rep = H // HKV
        k = jnp.repeat(k, rep, axis=2)
        v = jnp.repeat(v, rep, axis=2)
        scores = jnp.einsum('bqhd,bkhd->bhqk', q, k) / np.sqrt(HD).astype(np.float32)
        causal = jnp.tril(jnp.ones((s, s), dtype=bool))
        scores = jnp.where(causal[None, None], scores, jnp.finfo(scores.dtype).min)
        attn = jax.nn.softmax(scores, axis=-1)
        ctx = jnp.einsum('bhqk,bkhd->bqhd', attn, v).reshape(b, s, H * HD)
        attn_out = ctx @ Wo
        h = jnp.clip(residual + attn_out, -100.0, 100.0)
        residual = h
        hn = _rmsnorm(h, ln2_w)
        flat = hn.reshape(b * s, d)
        logits = flat @ Wr
        probs = jax.nn.softmax(logits, axis=-1)
        topv, topi = jax.lax.top_k(probs, K)
        topv = topv / jnp.sum(topv, axis=-1, keepdims=True)
        w = jnp.sum(jax.nn.one_hot(topi, E, dtype=flat.dtype) * topv[..., None], axis=1)
        g = jnp.einsum('td,edf->etf', flat, Wg)
        u = jnp.einsum('td,edf->etf', flat, Wu)
        a = jax.nn.silu(g) * u
        o = jnp.einsum('etf,efd->etd', a, Wd)
        moe_out = jnp.einsum('te,etd->td', w, o).reshape(b, s, d)
        out = jnp.clip(residual + moe_out, -100.0, 100.0)
        return out

    def _L3_attn_ref(x, Wq, Wk, Wv, Wo, W_down_kv, W_up_k, W_up_v):
        import jax, jax.numpy as jnp
        import numpy as np
        D_MODEL = 128
        N_HEADS = 16
        HEAD_DIM = D_MODEL // N_HEADS
        D_LATENT = 32
        LAMBDA_DECAY = 0.01
        TIME_STEP = 0.01
        CLAMP = 10000.0

        def _reference_tuple_inner(x, Wq, Wk, Wv, Wo, W_down_kv, W_up_k, W_up_v):
            B, S, _ = x.shape
            q = x @ Wq
            k = x @ Wk
            v = x @ Wv
            latent_kv = (k + v) @ W_down_kv
            k_rec = latent_kv @ W_up_k
            v_rec = latent_kv @ W_up_v

            def heads(t):
                return t.reshape(B, S, N_HEADS, HEAD_DIM).transpose(0, 2, 1, 3)
            qh, kh, vh = (heads(q), heads(k_rec), heads(v_rec))
            scale = 1.0 / (jnp.sqrt(jnp.float32(D_MODEL)) + 1e-08)
            scores = jnp.einsum('bhqd,bhkd->bhqk', qh, kh) * scale
            scores = jnp.clip(jnp.nan_to_num(scores, nan=-1000000000.0), -CLAMP, CLAMP)
            idx = jnp.arange(S, dtype=jnp.float32)
            decay = jnp.exp(-LAMBDA_DECAY * TIME_STEP * jnp.abs(idx[:, None] - idx[None, :]))
            scores = scores * decay[None, None, :, :]
            scores = jnp.clip(jnp.nan_to_num(scores, nan=-1000000000.0), -CLAMP, CLAMP)
            attn = jax.nn.softmax(scores, axis=-1)
            out = jnp.einsum('bhqk,bhkd->bhqd', attn, vh)
            out = out.transpose(0, 2, 1, 3).reshape(B, S, D_MODEL)
            return (out @ Wo, latent_kv)
        return _reference_tuple_inner(x, Wq, Wk, Wv, Wo, W_down_kv, W_up_k, W_up_v)[0]

    def _L3_ffn_ref(x, Wqkv, q_scale, k_scale, Wo, ln_g, ln_b, W1, b1, W2, b2):
        import jax, jax.numpy as jnp
        import numpy as np
        DIM = 128
        DEPTH = 6
        HEADS = 16
        DIM_HEAD = 64
        WINDOW = 32
        INNER = HEADS * DIM_HEAD
        DIM_INNER = int(DIM * 4 * 2 / 3)
        QK_SCALE = 8.0

        def shift_tokens(t):
            a, s = jnp.split(t, 2, -1)
            s = jnp.pad(s, ((0, 0), (1, 0), (0, 0)))[:, :-1]
            return jnp.concatenate([a, s], -1)

        def l2norm(t):
            return t / jnp.maximum(jnp.linalg.norm(t, axis=-1, keepdims=True), 1e-12)

        def rotate_half(x):
            x1, x2 = jnp.split(x, 2, -1)
            return jnp.concatenate([-x2, x1], -1)

        def rotary_tables(n):
            half = jnp.arange(0, DIM_HEAD, 2, dtype=jnp.float32)
            inv_freq = 1.0 / 10000.0 ** (half / DIM_HEAD)
            t = jnp.arange(n, dtype=jnp.float32)
            freqs = t[:, None] * inv_freq[None, :]
            freqs = jnp.concatenate([freqs, freqs], -1)
            base_scale = (half + 0.4 * DIM_HEAD) / (1.4 * DIM_HEAD)
            power = (t - n // 2) / (WINDOW // 2)
            scale = base_scale[None, :] ** power[:, None]
            scale = jnp.concatenate([scale, scale], -1)
            return (freqs, scale)

        def local_attention(q, k, v):
            b, h, n, d = q.shape
            w = WINDOW
            nw = n // w
            bq = q.reshape(b, h, nw, w, d)
            bk = k.reshape(b, h, nw, w, d)
            bv = v.reshape(b, h, nw, w, d)

            def look(t):
                p = jnp.pad(t, ((0, 0), (0, 0), (1, 0), (0, 0), (0, 0)))
                return jnp.concatenate([p[:, :, :nw], p[:, :, 1:]], axis=3)
            bk2, bv2 = (look(bk), look(bv))
            seq = jnp.arange(n).reshape(nw, w)
            seq_p = jnp.pad(seq, ((1, 0), (0, 0)), constant_values=-1)
            jt = jnp.concatenate([seq_p[:nw], seq_p[1:]], axis=1)
            it = seq[:, :, None]
            jb = jt[:, None, :]
            mask = (it < jb) | (it > jb + w) | (jb == -1)
            sim = jnp.einsum('bhwie,bhwje->bhwij', bq, bk2) * QK_SCALE
            sim = jnp.where(mask, -jnp.finfo(sim.dtype).max, sim)
            attn = jax.nn.softmax(sim, -1)
            out = jnp.einsum('bhwij,bhwje->bhwie', attn, bv2)
            return out.reshape(b, h, n, d)

        def attn_layer(x, Wqkv, qs, ksc, Wo):
            b, n, _ = x.shape
            qkv = x @ Wqkv
            q, k, v = jnp.split(qkv, 3, -1)
            sh = lambda t: t.reshape(b, n, HEADS, DIM_HEAD).transpose(0, 2, 1, 3)
            q, k, v = (sh(q), sh(k), sh(v))
            q = l2norm(q) * qs
            k = l2norm(k) * ksc
            freqs, scale = rotary_tables(n)
            cos, sin = (jnp.cos(freqs), jnp.sin(freqs))
            q = q * cos * scale + rotate_half(q) * sin * scale
            inv = 1.0 / scale
            k = k * cos * inv + rotate_half(k) * sin * inv
            out = local_attention(q, k, v)
            out = out.transpose(0, 2, 1, 3).reshape(b, n, INNER)
            return out @ Wo

        def ffn_layer(x, g, bln, W1, b1, W2, b2):
            mu = x.mean(-1, keepdims=True)
            var = ((x - mu) ** 2).mean(-1, keepdims=True)
            xn = (x - mu) / jnp.sqrt(var + 1e-05) * g + bln
            hg = xn @ W1 + b1
            a, gate = jnp.split(hg, 2, -1)
            return a * jax.nn.gelu(gate, approximate=False) @ W2 + b2
        for i in range(DEPTH):
            x = attn_layer(shift_tokens(x), Wqkv[i], q_scale[i], k_scale[i], Wo[i]) + x
            x = ffn_layer(shift_tokens(x), ln_g[i], ln_b[i], W1[i], b1[i], W2[i], b2[i]) + x
        return x
    x = L0_attn_x
    x = x + _layernorm(_L0_attn_ref(_layernorm(x, axis=-1), L0_attn_mem, L0_attn_wq, L0_attn_wk, L0_attn_wv, L0_attn_wo, L0_attn_w1, L0_attn_b1, L0_attn_w2, L0_attn_b2, L0_attn_lin1, L0_attn_lin2, L0_attn_alpha, L0_attn_theta), axis=-1)
    x = x + _layernorm(_L0_ffn_ref(_layernorm(x, axis=-1), L0_ffn_g_info, L0_ffn_W_qkv, L0_ffn_W_proj, L0_ffn_b_proj), axis=-1)
    x = x + _layernorm(_L1_attn_ref(_layernorm(x, axis=-1), L1_attn_Wq, L1_attn_bq, L1_attn_Wk, L1_attn_bk, L1_attn_Wv, L1_attn_bv, L1_attn_Wo, L1_attn_bo, L1_attn_stdp), axis=-1)
    x = x + _layernorm(_L1_ffn_ref(_layernorm(x, axis=-1), L1_ffn_router_w, L1_ffn_router_b, L1_ffn_w1, L1_ffn_w2, L1_ffn_w3, L1_ffn_ln_g, L1_ffn_ln_b), axis=-1)
    x = x + _layernorm(_L2_attn_ref(_layernorm(x, axis=-1), L2_attn_in_proj_w, L2_attn_conv_w, L2_attn_conv_b, L2_attn_x_proj_w, L2_attn_dt_proj_w, L2_attn_dt_proj_b, L2_attn_out_proj_w, L2_attn_A_log, L2_attn_D_param), axis=-1)
    x = x + _layernorm(_L2_ffn_ref(_layernorm(x, axis=-1), L2_ffn_ln1_w, L2_ffn_ln2_w, L2_ffn_Wq, L2_ffn_Wk, L2_ffn_Wv, L2_ffn_Wo, L2_ffn_Wr, L2_ffn_Wg, L2_ffn_Wu, L2_ffn_Wd), axis=-1)
    x = x + _layernorm(_L3_attn_ref(_layernorm(x, axis=-1), L3_attn_Wq, L3_attn_Wk, L3_attn_Wv, L3_attn_Wo, L3_attn_W_down_kv, L3_attn_W_up_k, L3_attn_W_up_v), axis=-1)
    x = x + _layernorm(_L3_ffn_ref(_layernorm(x, axis=-1), L3_ffn_Wqkv, L3_ffn_q_scale, L3_ffn_k_scale, L3_ffn_Wo, L3_ffn_ln_g, L3_ffn_ln_b, L3_ffn_W1, L3_ffn_b1, L3_ffn_W2, L3_ffn_b2), axis=-1)
    return x

_drawn_inputs = setup_inputs


def setup_inputs(seed=0):
    import zlib

    import numpy as np

    out = dict(_drawn_inputs(seed))
    spreads = {'L0_attn_b1': (0.0, 0.1),
     'L0_attn_b2': (0.0, 0.1),
     'L0_ffn_b_proj': (0.0, 0.1),
     'L1_attn_stdp': (1.0, 0.2),
     'L1_ffn_router_b': (0.0, 0.1),
     'L1_ffn_ln_g': (1.0, 0.2),
     'L1_ffn_ln_b': (0.0, 0.1),
     'L2_attn_D_param': (1.0, 0.6),
     'L3_ffn_q_scale': (1.0, 0.6),
     'L3_ffn_k_scale': (1.0, 0.6),
     'L3_ffn_ln_g': (1.0, 0.6),
     'L3_ffn_ln_b': (0.0, 0.8),
     'L3_ffn_b1': (0.0, 0.8),
     'L3_ffn_b2': (0.0, 0.8)}
    factors = {'L0_attn_wk': 3.26,
     'L0_attn_lin1': 27.978,
     'L0_attn_lin2': 3.149,
     'L0_ffn_g_info': 5.473,
     'L1_attn_Wq': 3.297,
     'L1_attn_bq': 8.0,
     'L1_attn_bk': 6.0,
     'L2_attn_conv_w': 2.741,
     'L2_attn_x_proj_w': 64.0,
     'L2_attn_dt_proj_w': 64.0,
     'L2_attn_dt_proj_b': 64.0,
     'L2_attn_A_log': 64.0,
     'L2_ffn_ln1_w': 8.0,
     'L2_ffn_ln2_w': 8.0,
     'L2_ffn_Wq': 8.0,
     'L2_ffn_Wk': 8.0,
     'L2_ffn_Wv': 4.34,
     'L2_ffn_Wo': 4.366,
     'L2_ffn_Wr': 8.0,
     'L2_ffn_Wg': 8.0,
     'L2_ffn_Wu': 8.0,
     'L2_ffn_Wd': 8.0,
     'L3_attn_Wq': 64.0,
     'L3_attn_W_up_k': 64.0,
     'L3_ffn_W1': 7.915,
     'L3_ffn_W2': 7.658}
    for name, (base, spread) in spreads.items():
        noise = np.random.default_rng([zlib.crc32(name.encode()), seed]).standard_normal(out[name].shape)
        drawn = base * np.exp(spread * noise) if base else spread * noise
        out[name] = jnp.asarray(drawn.astype(out[name].dtype))
    for name, factor in factors.items():
        out[name] = (out[name] * factor).astype(out[name].dtype)
    return out
```

```python
from contextlib import ExitStack

import numpy as np

import concourse.bass as bass
from concourse import mybir

P = 128
F32 = mybir.dt.float32
U32 = mybir.dt.uint32
I32 = mybir.dt.int32
ALU = mybir.AluOpType
ACT = mybir.ActivationFunctionType
AX = mybir.AxisListType.X

BATCH, SEQ, DIM = 8, 256, 128
TOKENS = BATCH * SEQ
TILES = TOKENS // P
GROUP = 512
GROUPS = TOKENS // GROUP
NEG = -1.0e30
EPS = 1e-5
MAGIC = 0x5F3759DF

HID0, HEADS0, WIN0, MEM0 = 512, 4, 64, 64
HEADS, HDIM = 16, 8
CHUNKS = HEADS // 4
REG = 5
EXP1, EXP2, FF = 16, 8, 256
INNER, STATE, CONV = 256, 16, 3
LATENT = 32
CLAMP = 10000.0
DEPTH, LHEADS, LDIM, LWIN = 6, 16, 64, 32
LIN = LHEADS * LDIM
GLU = int(DIM * 4 * 2 / 3)
GLU_PARTS = [(0, 128), (128, 128), (256, GLU - 256)]



def rows(v):
    v = np.asarray(v).reshape(1, -1)
    return np.broadcast_to(v, (P, v.shape[1]))


def cols(v):
    return np.asarray(v).reshape(-1, P).T


def chunks(w):
    w = np.asarray(w)
    return w.reshape(-1, P, w.shape[1]).transpose(1, 0, 2).reshape(P, -1)


def spread_heads(w, head_of=None):
    w = np.asarray(w)
    out = np.zeros((w.shape[0], CHUNKS, 4, 32), np.float32)
    for c in range(CHUNKS):
        for g in range(4):
            h = 4 * c + g if head_of is None else head_of(4 * c + g)
            out[:, c, g, :HDIM] = w[:, h * HDIM:(h + 1) * HDIM]
    return out.reshape(w.shape[0], CHUNKS * P)


def spread_rows(w):
    return chunks(spread_heads(np.asarray(w).T).T)


def tall(a):
    a = np.asarray(a)
    out = np.zeros((P, a.shape[1]), np.float32)
    out[:a.shape[0]] = a
    return out


def rotate_columns(w, half):
    w = np.asarray(w)
    k, n = w.shape
    return w.reshape(k, n // (2 * half), 2, half)[:, :, ::-1, :].reshape(k, n)


def pack(parts):
    place, at = {}, 0
    for name, a in parts:
        place[name] = (at, a.shape[1])
        at += a.shape[1]
    return np.ascontiguousarray(np.concatenate([a for _, a in parts], axis=1)), place


def expert_weights(up, gate, down):
    return [piece for e in range(up.shape[0])
            for piece in ((f"gate{e}", np.asarray(gate[e])), (f"up{e}", np.asarray(up[e])),
                          (f"down{e}", chunks(down[e])))]


def layout(i):
    a = {k: np.asarray(v) for k, v in i.items()}
    T = np.transpose
    out = {}
    mem = np.zeros((P, DIM), np.float32)
    mem[P - MEM0:] = a["L0_attn_mem"]
    out["titan"] = [(n, T(a["L0_attn_" + n])) for n in ("wq", "wk", "wv", "wo", "lin1", "lin2", "w1")] + [
        ("w2", a["L0_attn_w2"]), ("w2T", chunks(T(a["L0_attn_w2"]))), ("b1", rows(a["L0_attn_b1"])),
        ("b2", rows(a["L0_attn_b2"])), ("b2col", cols(a["L0_attn_b2"])), ("mem", mem), ("memT", T(mem)),
        ("alpha", rows(a["L0_attn_alpha"])), ("theta", rows(a["L0_attn_theta"]))]
    w = a["L0_ffn_W_qkv"]
    out["split"] = [("wq", w[:, :DIM]), ("wqs", spread_heads(w[:, :DIM])), ("wks", spread_heads(w[:, DIM:2 * DIM])),
                    ("wv", w[:, 2 * DIM:]), ("wo", spread_rows(a["L0_ffn_W_proj"])), ("bo", rows(a["L0_ffn_b_proj"])),
                    ("g", rows(a["L0_ffn_g_info"][0, 0]))]
    out["linear"] = [(n, T(a["L1_attn_" + n])) for n in ("Wq", "Wk", "Wv", "Wo")] + [
        ("bq", cols(a["L1_attn_bq"]))] + [(n, rows(a["L1_attn_" + n])) for n in ("bk", "bv", "bo", "stdp")]
    out["moe1"] = [("router", T(a["L1_ffn_router_w"])), ("rb", rows(a["L1_ffn_router_b"])),
                   ("lng", rows(a["L1_ffn_ln_g"])), ("lnb", tall(a["L1_ffn_ln_b"]))] + expert_weights(
        T(a["L1_ffn_w3"], (0, 2, 1)), T(a["L1_ffn_w1"], (0, 2, 1)), T(a["L1_ffn_w2"], (0, 2, 1)))
    m = "L2_attn_"
    out["mamba"] = [("in", a[m + "in_proj_w"]), ("conv", chunks(a[m + "conv_w"][:, 0, :])),
                    ("convb", cols(a[m + "conv_b"])), ("xp", chunks(a[m + "x_proj_w"])),
                    ("dt", chunks(a[m + "dt_proj_w"])), ("dtb", cols(a[m + "dt_proj_b"])),
                    ("out", chunks(a[m + "out_proj_w"])), ("alog", chunks(a[m + "A_log"])),
                    ("dp", cols(a[m + "D_param"]))]
    m = "L2_ffn_"
    q, k = a[m + "Wq"], a[m + "Wk"]
    kv = lambda h: h // 4
    out["gqa"] = [("ln1", cols(a[m + "ln1_w"])), ("ln2", cols(a[m + "ln2_w"])),
                  ("wqs", spread_heads(q)), ("wqr", spread_heads(rotate_columns(q, 4))),
                  ("wks", spread_heads(k, kv)), ("wkr", spread_heads(rotate_columns(k, 4), kv)),
                  ("wv", a[m + "Wv"]), ("wo", spread_rows(a[m + "Wo"])), ("wr", a[m + "Wr"])] + expert_weights(
        a[m + "Wu"], a[m + "Wg"], a[m + "Wd"])
    m = "L3_attn_"
    out["mla"] = [(n, a[m + n]) for n in ("Wk", "Wv")] + [("Wo", spread_rows(a[m + "Wo"])),
        ("wqs", spread_heads(a[m + "Wq"])), ("down", a[m + "W_down_kv"]),
        ("upk", tall(spread_heads(a[m + "W_up_k"]))), ("upv", tall(a[m + "W_up_v"]))]
    m = "L3_ffn_"
    for l in range(DEPTH):
        qs, ks = a[m + "q_scale"][l], a[m + "k_scale"][l]
        w1, b1 = a[m + "W1"][l], a[m + "b1"][l]
        bias = np.zeros((2, 3 * P), np.float32)
        bias[0, :GLU], bias[1, :GLU] = b1[:GLU], b1[GLU:]
        w2 = np.zeros((3 * P, DIM), np.float32)
        w2[:GLU] = a[m + "W2"][l]
        out[f"layer{l}"] = [("wqkv", a[m + "Wqkv"][l]), ("wo", chunks(a[m + "Wo"][l])), ("w1", w1),
                            ("w2", chunks(w2)), ("b1", cols(bias)), ("b2", cols(a[m + "b2"][l])),
                            ("lng", cols(a[m + "ln_g"][l])), ("lnb", cols(a[m + "ln_b"][l])),
                            ("qs", rows(qs)), ("qsr", rotate_columns(rows(qs), LDIM // 2)),
                            ("ks", rows(ks)), ("ksr", rotate_columns(rows(ks), LDIM // 2))]
    return out


def tables():
    f = np.float32
    q = np.arange(P)[:, None]
    key = np.arange(2 * P)[None, :] - P
    out = [("ident", np.eye(P, dtype=f)), ("ones", np.ones((P, P), f)),
           ("center", (np.eye(P) - 1.0 / DIM).astype(f)), ("mean", np.full((P, P), 1.0 / DIM, f)),
           ("half", np.full((P, 64), -0.5, f))]
    out += [("magic", np.full((P, 1), MAGIC + 1, np.uint32).view(f))]
    window = np.where((key <= q) & (key > q - WIN0), 0, NEG).astype(f)
    out += [("window", window), ("windowmem", np.where((key < P - MEM0) & (q >= P - MEM0), NEG, window).astype(f)),
            ("causal", np.where(key <= q, 0, NEG).astype(f)),
            ("band", np.where((key <= q) & (key >= q - LWIN), 0, NEG).astype(f))]
    reg = np.zeros((P, TILES), f)
    reg[:REG, ::2] = 1
    turn = np.zeros((P, 1), f)
    for g in range(4):
        turn[32 * g + HDIM], turn[32 * g + HDIM + 1] = -1, 1
    block = np.zeros((P, HEADS, 32), f)
    pick = np.zeros((P, REG), f)
    for h in range(HEADS):
        block[h * REG:(h + 1) * REG, h, :HDIM] = 1
        for r in range(REG):
            pick[h * REG + r, r] = 0.5
    block = block.reshape(P, -1)
    out += [("reg", reg), ("turn", turn), ("block", block), ("pick", pick)]
    ch = np.arange(P)[:, None]
    out += [("blockdiag", (ch // HDIM == np.arange(DIM)[None, :] // HDIM).astype(f)),
            ("blockhead", (ch // HDIM == np.arange(HEADS)[None, :]).astype(f)),
            ("iota", np.broadcast_to(np.arange(16, dtype=f), (P, 16)))]
    inv = (f(1.0) / f(10000.0) ** (np.arange(0, HDIM, 2, dtype=f) / f(HDIM))).astype(f)
    fr = np.arange(SEQ, dtype=f)[:, None] * inv
    cos, sin = np.cos(fr).astype(f).T, np.sin(fr).astype(f).T
    ct, st = np.zeros((P, SEQ), f), np.zeros((P, SEQ), f)
    for g in range(4):
        ct[32 * g:32 * g + 4], ct[32 * g + 4:32 * g + 8] = cos, cos
        st[32 * g:32 * g + 4], st[32 * g + 4:32 * g + 8] = -sin, sin
    out += [("cosT", ct), ("sinT", st)]
    pos = np.arange(SEQ, dtype=f)
    decay = np.exp(f(-0.01 * 0.01) * np.abs(pos[:, None] - pos[None, :])).astype(f)
    out += [("decay", chunks(decay))]
    half = np.arange(0, LDIM, 2, dtype=f)
    inv = (f(1.0) / f(10000.0) ** (half / f(LDIM))).astype(f)
    t = np.arange(SEQ, dtype=f)
    fr = t[:, None] * inv[None, :]
    fr = np.concatenate([fr, fr], -1)
    base = ((half + f(0.4 * LDIM)) / f(1.4 * LDIM)).astype(f)
    sc = base[None, :] ** ((t - SEQ // 2) / f(LWIN // 2))[:, None]
    sc = np.concatenate([sc, sc], -1).astype(f)
    sign = np.concatenate([-np.ones(LDIM // 2, f), np.ones(LDIM // 2, f)])
    c, s = np.cos(fr).astype(f), np.sin(fr).astype(f)
    inv = f(1.0) / sc
    out += [("rqc", chunks(c * sc)), ("rqs", chunks(s * sc * sign)), ("rkc", chunks(c * inv)),
            ("rks", chunks(s * inv * sign))]
    return [(n, a.astype(f)) for n, a in out]



class Engine:

    def __init__(self, engine, sem):
        self.engine, self.sem, self.count, self.waited = engine, sem, 0, {}

    def wait(self, after):
        need = {}
        for sem, value in flat(after):
            need[sem.name] = (sem, max(value, need.get(sem.name, (sem, 0))[1]))
        for name, (sem, value) in need.items():
            if value > self.waited.get(name, 0):
                self.engine.wait_ge(sem, value)
                self.waited[name] = value

    def __call__(self, after, issue, *args, **kw):
        self.wait(after)
        return self.mark(issue(*args, **kw))

    def mark(self, instruction):
        instruction.then_inc(self.sem, 1)
        self.count += 1
        return [(self.sem, self.count)]


def flat(tokens):
    out = []
    for t in tokens:
        if isinstance(t, list):
            out += flat(t)
        elif t is not None:
            out.append(t)
    return out


class Slot:

    def __init__(self, ap, free=()):
        self.ap, self.free = ap, list(free)


class Ring:
    def __init__(self, slots):
        self.slots, self.at = slots, 0

    def take(self):
        for _ in self.slots:
            slot = self.slots[self.at % len(self.slots)]
            self.at += 1
            if slot.free is not None:
                break
        assert slot.free is not None, "taken before its release was written down"
        free, slot.free = slot.free, None
        return slot, free


def pipeline(units, beside=None, rate=0):
    running, units = [], iter(units)
    more = True
    while more or running:
        nxt = next(units, None) if more else None
        if nxt is None:
            more = False
        else:
            running.append(nxt)
        left, n = [], len(running)
        for i, u in enumerate(running):
            if next(u, "end") != "end":
                left.append(u)
            for _ in range((i + 1) * rate // n - i * rate // n):
                beside()
        running = left


class Machine:
    def __init__(self, nc, ctx, dram, places, sizes):
        self.nc, self.ctx, self.dram, self.places = nc, ctx, dram, places
        sem = lambda n: ctx.enter_context(nc.semaphore(n))
        self.sem = sem
        self.pe = Engine(nc.tensor, sem("pe_done"))
        self.act = Engine(nc.scalar, sem("act_done"))
        self.dve = Engine(nc.vector, sem("dve_done"))
        self.pool = Engine(nc.gpsimd, sem("pool_done"))
        self.sp = Engine(nc.sync, sem("sp_done"))
        sb = lambda n, s: ctx.enter_context(nc.sbuf_tensor(n, s, F32))[:]
        self.x = sb("x", [P, TILES, DIM])
        self.xn = sb("xn", [P, TILES, DIM])
        self.xnT = sb("xnT", [P, TOKENS])
        self.y = sb("y", [P, TILES, DIM])
        self.table = sb("table", [P, sizes["table"]])
        self.weights = [sb("weights0", [P, sizes["w0"]]), sb("weights1", [P, sizes["w1"]])]
        self.scratch = sb("scratch", [P, sizes["scratch"]])
        self.scratch_size = sizes["scratch"]
        self.stats = sb("stats", [P, 512])
        self.psum = ctx.enter_context(nc.psum_tensor("psum", [P, 8, 512], F32))[:]
        self.bank = [Slot(self.psum[:, i, :]) for i in range(8)]
        self.loaded = {}
        self.stage_end = []
        self.used = 0

    def c(self, name, n=None):
        at, width = self.places["table"][name]
        return self.table[:, at:at + (n or width)]

    def load(self, name, region, after=()):
        n = self.dram[name].shape[1]
        buf = self.table if region is None else self.weights[region]
        sem = self.sem("loaded_" + name)
        self.sp.wait(after)
        half = (n // 2) if n > 2048 else n
        k = 0
        for a, b in ((0, half), (half, n)):
            if b > a:
                self.nc.sync.dma_start(buf[:, a:b], self.dram[name][:, a:b]).then_inc(sem, 16)
                k += 1
        self.loaded[name] = ([(sem, 16 * k)], buf)

    def w(self, stage, name):
        at, n = self.places[stage][name]
        return self.loaded[stage][1][:, at:at + n]

    def everything(self):
        return [(e.sem, e.count) for e in (self.pe, self.act, self.dve, self.pool) if e.count]

    def begin(self, after_all):
        self.used, self.extra = 0, []
        for e in (self.pe, self.act, self.dve, self.pool):
            e.wait(after_all)
        for b in self.bank:
            b.free = []

    def alloc(self, *shape):
        n = int(np.prod(shape))
        if self.used + n <= self.scratch_size:
            ap = self.scratch[:, self.used:self.used + n]
            self.used += n
        else:
            place = next(e for e in self.extra if e[2] + n <= e[1])
            ap = place[0][:, place[2]:place[2] + n]
            place[2] += n
        if len(shape) == 2:
            ap = ap.rearrange("p (a b) -> p a b", a=shape[0])
        if len(shape) == 3:
            ap = ap.rearrange("p (a b c) -> p a b c", a=shape[0], b=shape[1])
        return ap

    def ring(self, n, *shape):
        return Ring([Slot(self.alloc(*shape)) for _ in range(n)])

    def mm(self, after, groups):
        self.pe.wait(after)
        last = None
        for out, pairs in groups:
            for i, (a, b) in enumerate(pairs):
                last = self.nc.tensor.matmul(out, a, b, start=(i == 0), stop=(i == len(pairs) - 1))
        return self.pe.mark(last)

    def transposes(self, after, pairs):
        self.pe.wait(after)
        last = None
        for out, src in pairs:
            k = src.shape[0]
            last = self.nc.tensor.transpose(out, src, self.c("ident")[0:k, 0:k])
        return self.pe.mark(last)

    def copy(self, eng, after, out, src):
        if eng is self.act:
            return eng(after, self.nc.scalar.copy, out, src)
        e = self.nc.vector if eng is self.dve else self.nc.gpsimd
        return eng(after, e.tensor_copy, out, src)

    def rsqrt(self, after, x, y, t):
        nc, dve = self.nc, self.dve
        n = x.shape[1]
        k = dve(after, nc.vector.tensor_scalar, y.bitcast(U32), x.bitcast(U32), 1, 0xFFFFFFFF,
                ALU.logical_shift_right, ALU.bitwise_xor)
        k = dve(k, nc.vector.tensor_tensor, y.bitcast(I32), y.bitcast(I32),
                self.c("magic").bitcast(I32).broadcast_to([P, n]), ALU.add)
        for _ in range(3):
            k = dve(k, nc.vector.tensor_tensor, t, x, y, ALU.mult)
            k = dve(k, nc.vector.scalar_tensor_tensor, t, t, -0.5, y, ALU.mult, ALU.mult)
            k = dve(k, nc.vector.scalar_tensor_tensor, y, t, 1.5, y, ALU.add, ALU.mult)
        return k

    def moments(self, after, tiles, n, at):
        nc, dve = self.nc, self.dve
        st = self.stats[:, at:at + 6 * n].rearrange("p (t s) -> p t s", s=6)
        r = self.stats[:, at + 6 * n:at + 12 * n].rearrange("p (k t) -> p k t", k=6)
        t = None
        for i, tile in enumerate(tiles):
            t = dve(after, nc.vector.bn_stats, st[:, i, :], tile)
        tt = nc.vector.tensor_tensor
        s = dve(t, tt, r[:, 0, :], st[:, :, 1], st[:, :, 4], ALU.add)
        d = dve([], tt, r[:, 1, :], st[:, :, 1], st[:, :, 4], ALU.subtract)
        v = dve([], tt, r[:, 2, :], st[:, :, 2], st[:, :, 5], ALU.add)
        mean = dve(s, nc.vector.tensor_scalar, r[:, 0, :], r[:, 0, :], 0.5, None, ALU.mult)
        d = dve(d, tt, r[:, 3, :], r[:, 1, :], r[:, 1, :], ALU.mult)
        v = dve(v, nc.vector.tensor_scalar, r[:, 2, :], r[:, 2, :], 1.0 / DIM, EPS, ALU.mult, ALU.add)
        v = dve([v, d], nc.vector.scalar_tensor_tensor, r[:, 4, :], r[:, 3, :], 0.25, r[:, 2, :], ALU.mult, ALU.add)
        if n == TILES:
            rstd = self.rsqrt(v, r[:, 4, :], r[:, 5, :], r[:, 3, :])
        else:
            rstd = self.pool(v, nc.gpsimd.tensor_tensor, r[:, 5, :], r[:, 4, :], self.c("half", n), ALU.pow)
        return r[:, 0, :], r[:, 5, :], [mean, rstd]

    def normalise(self, after, src, out, at=0):
        mean, rstd, ready = self.moments(after, [src[:, t, :] for t in range(TILES)], TILES, at)
        return [self.dve(ready, self.nc.vector.tensor_scalar, out[:, t, :], src[:, t, :], mean[:, t:t + 1],
                         rstd[:, t:t + 1], ALU.subtract, ALU.mult) for t in range(TILES)]

    def turn(self, after, src, dst, banks, scale=None):
        done = []
        for g in range(GROUPS):
            bank, free = banks.take()
            t = self.transposes([free, [after[4 * g + k] for k in range(4)]],
                                [(bank.ap[:, P * k:P * k + P], src[:, 4 * g + k, :]) for k in range(4)])
            out = dst[:, GROUP * g:GROUP * (g + 1)]
            if scale is None:
                t = self.copy(self.act if g % 2 else self.dve, t, out, bank.ap)
            else:
                t = self.dve(t, self.nc.vector.tensor_scalar, out, bank.ap, scale, None, ALU.mult)
            bank.free = t
            done.append(t)
        return done

    def attend(self, rings, heads, dv, scale, tile_of, finish):
        nc = self.nc
        c0 = min(col for col, _ in tile_of["segments"])
        blocks = sorted({k // P for col, n in tile_of["segments"] for k in (col, col + n - 1)})
        per = min(heads, 4 * P // max(dv, 32))
        order = tile_of["order"]
        shared = {}

        def pair(n, hs):
            cols = slice(hs[0], hs[1] + 1, hs[1] - hs[0])
            if n == 0:
                shared["small"], shared["free"] = rings["small"].take()
            small = shared["small"].ap
            bank, free = rings["S"].take()
            s = bank.ap.rearrange("p (h k) -> p h k", h=2)
            scored = [free, tile_of["ready"]]
            one = [[(s[:, i, col:col + n_], [(tile_of["q"](hs[i]), tile_of["k"](hs[i], (col, n_)))])
                    for col, n_ in tile_of["segments"]] for i in range(2)]
            if tile_of.get("apart"):
                scored = self.mm(self.mm(scored, one[0]), one[1])
            else:
                scored = self.mm(scored, one[0] + one[1])
            if n == len(order) - 1:
                tile_of["scored"](scored)
            yield
            probs, pfree = rings["P"].take()
            p = probs.ap
            m = small[:, 0, cols]
            if tile_of["mask"] is None:
                top = self.dve([scored, shared["free"]], nc.vector.tensor_reduce, m, s[:, :, c0:], AX, ALU.max)
                src = s
            elif tile_of.get("clip"):
                lim = tile_of["clip"]
                t = self.dve([scored, pfree, shared["free"]], nc.vector.tensor_scalar, p, s, lim, -lim, ALU.min, ALU.max)
                bank.free = t
                for i in range(2):
                    top = self.dve(t, nc.vector.tensor_tensor_reduce, p[:, i, :], p[:, i, :], tile_of["mask"], 1.0,
                                   -3.0e38, ALU.mult, ALU.max, small[:, 0, hs[i]:hs[i] + 1])
                src = p
            else:
                for i in range(2):
                    top = self.dve([scored, pfree, shared["free"]], nc.vector.tensor_tensor_reduce, p[:, i, c0:],
                                   s[:, i, c0:], tile_of["mask"][:, c0:], 1.0, -3.0e38, ALU.add, ALU.max,
                                   small[:, 0, hs[i]:hs[i] + 1])
                bank.free = top
                src = p
            bias = self.dve(top, nc.vector.tensor_scalar, small[:, 1, cols], m, -scale, None, ALU.mult)
            yield
            for i in range(2):
                h = hs[i]
                e = self.act([bias, pfree], nc.scalar.activation, p[:, i, c0:], src[:, i, c0:], ACT.Exp,
                             bias=small[:, 1, h:h + 1], scale=scale, accum_out=small[:, 2, h:h + 1])
            if tile_of["mask"] is None:
                bank.free = e
            yield
            dg, free = rings["D"].take()
            r = self.dve(e, nc.vector.reciprocal, small[:, 0, cols], small[:, 2, cols])
            for i in range(2):
                d = self.dve([r, free], nc.vector.tensor_scalar, dg.ap[:, i, :], self.c("ident"),
                              small[:, 0, hs[i]:hs[i] + 1], None, ALU.mult)
            if n == len(order) - 1:
                shared["small"].free = d
            yield
            bank, free = rings["T"].take()
            tp = bank.ap.rearrange("p (h b k) -> p h b k", h=2, b=2)
            turned = self.mm([free, d], [(tp[:, i, b, :], [(p[:, i, P * b:P * b + P], dg.ap[:, i, :])])
                                         for i in range(2) for b in blocks])
            probs.free = turned
            dg.free = turned
            yield
            pt, free = rings["PT"].take()
            ptv = pt.ap.rearrange("p (h b k) -> p h b k", h=2, b=2)
            b0, b1 = blocks[0], blocks[-1] + 1
            eng = self.act if n % 3 == 2 else self.dve
            t = self.copy(eng, [turned, free], ptv[:, :, b0:b1, :], tp[:, :, b0:b1, :])
            bank.free = t
            yield
            if n % (per // 2) == 0:
                shared["O"], shared["ofree"] = rings["O"].take()
            pad = max(dv, 32)
            out = lambda h: shared["O"].ap[h * pad % P:h * pad % P + pad, h % per * pad // P * P:h % per * pad // P * P + P]
            t = self.mm([t, shared["ofree"], tile_of["vready"]],
                        [(out(h), [(tile_of["v"](h, blk), ptv[:, i, blk, :]) for blk in blocks]) for i, h in enumerate(hs)])
            pt.free = t
            if n == len(order) - 1:
                tile_of["valued"](t)
            if (n + 1) % (per // 2) == 0:
                obank = shared["O"]
                width = per * pad // P * P
                yield
                attn, free = rings["A"].take()
                t = self.copy(self.act, [t, free], attn.ap[:, 0:width], obank.ap[:, 0:width])
                obank.free = t
                yield
                yield from finish(attn, t, n // (per // 2))

        return [pair(n, hs) for n, hs in enumerate(order)]

    def attention_rings(self, s=3, t=2, o=1):
        b = self.bank
        return {"S": Ring(b[0:s]), "T": Ring(b[s:s + t]), "O": Ring(b[s + t:s + t + o]),
                "P": self.ring(5, 2, 256), "PT": self.ring(3, 512), "D": self.ring(3, 2, P), "small": self.ring(8, 3, 16)}



def stage_titan(M, ready):
    nc, c, w = M.nc, M.c, lambda n: M.w("titan", n)
    wait_w = M.loaded["titan"][0]
    banks = Ring(M.bank)
    NT = TILES + 1
    ext = NT * P
    xT = M.alloc(ext)
    swaT = M.alloc(ext)
    turned = M.turn(ready, M.xn, xT, banks)
    mem = M.copy(M.pool, [wait_w], xT[:, TOKENS:], w("memT"))
    tile_ready = [turned[t // 4] for t in range(TILES)] + [mem]
    at = M.used
    q, k, v = M.alloc(ext), M.alloc(ext), M.alloc(NT, DIM)
    qk = {}
    spans = [(g * GROUP, GROUP) for g in range(GROUPS)] + [(TOKENS, P)]
    for i, (s, n) in enumerate(spans):
        for name, dst in (("wq", q), ("wk", k)):
            bank, free = banks.take()
            t = M.mm([free, wait_w, tile_ready[s // P]], [(bank.ap[:, 0:n], [(w(name), xT[:, s:s + n])])])
            t = M.copy(M.act if name == "wq" else M.dve, t, dst[:, s:s + n], bank.ap[:, 0:n])
            bank.free = t
            qk[name, i] = t
        bank, free = banks.take()
        t = M.mm(free, [(bank.ap[:, j:j + P], [(xT[:, s + j:s + j + P], w("wv"))]) for j in range(0, n, P)])
        t = M.copy(M.act, t, v[:, s // P:(s + n) // P, :], bank.ap[:, 0:n].rearrange("p (t d) -> p t d", d=DIM))
        bank.free = t
        qk["v", i] = t
    of = lambda t: [qk["wq", t // 4], qk["wk", t // 4]]
    rings = M.attention_rings(3, 2, 1)
    rings["A"] = M.ring(2, DIM)
    last = Ring(M.bank[6:8])
    hd = DIM // HEADS0
    swa_done = [None] * NT

    def units():
        for t in [TILES] + list(range(TILES)):
            prev = TILES if t % 2 == 0 else t - 1
            if t == TILES:
                segments, mask = [(P, P)], c("windowmem")
            elif t % 2:
                segments, mask = [(P - WIN0, WIN0 + P)], c("window")
            else:
                segments, mask = [(P - WIN0, WIN0), (P, P)], c("window")
            src = lambda col, t=t, prev=prev: t if col >= P else prev

            def finish(attn, done, g, t=t):
                bank, free = last.take()
                pr = M.mm([free, done], [(bank.ap[:, 0:P], [(w("wo"), attn.ap)])])
                attn.free = pr
                yield
                cp = M.copy(M.act, pr, swaT[:, t * P:t * P + P], bank.ap[:, 0:P])
                bank.free = cp
                swa_done[t] = cp

            tile = {"order": [(0, 1), (2, 3)], "apart": True, "valued": lambda token: None, "scored": lambda token: None, "ready": [of(t), of(prev)], "vready": [qk["v", t // 4], qk["v", prev // 4]],
                    "segments": segments, "mask": mask,
                    "q": lambda h, t=t: q[hd * h:hd * h + hd, t * P:t * P + P],
                    "k": lambda h, sg, src=src: k[hd * h:hd * h + hd,
                                                  src(sg[0]) * P + sg[0] % P:src(sg[0]) * P + sg[0] % P + sg[1]],
                    "v": lambda h, blk, src=src: v[:, src(blk * P), hd * h:hd * h + hd]}
            yield from M.attend(rings, HEADS0, hd, 1.0 / float(np.sqrt(hd)), tile, finish)

    for r in rings["P"].slots:
        r.free = M.pool([], nc.gpsimd.memset, r.ap, 0.0)
    pipeline(units())
    attention_end = M.everything()
    for e in (M.pe, M.act, M.dve, M.pool):
        e.wait(attention_end)
    M.used = at
    for b in M.bank:
        b.free = []
    ones = c("ones")
    g1, g2, gb1, gb2 = (M.bank[i].ap for i in range(4))
    banks = Ring(M.bank[4:8])
    sig, h, hT, dT, dtok, dh = (M.ring(2, HID0), M.ring(2, HID0), M.ring(2, HID0), M.ring(2, P), M.ring(2, P),
                                M.ring(2, HID0))
    grads = []

    def gradient(t):
        tok = w("mem") if t == TILES else M.xn[:, t, :]
        xt, first, final = xT[:, t * P:t * P + P], t == 0, t == TILES
        zb, free = banks.take()
        z = M.mm([free, tile_ready[t]], [(zb.ap, [(xt, w("w1")), (ones[0:1, :], w("b1")[0:1, :])])])
        yield
        s, free = sig.take()
        st = M.act([z, free], nc.scalar.activation, s.ap, zb.ap, ACT.Sigmoid)
        hs, free = h.take()
        ht = M.dve([st, free], nc.vector.tensor_tensor, hs.ap, zb.ap, s.ap, ALU.mult)
        zb.free = ht
        yield
        tb, free = banks.take()
        tr = M.transposes([free, ht], [(tb.ap[:, j:j + P], hs.ap[:, j:j + P]) for j in range(0, HID0, P)])
        yield
        hTs, free = hT.take()
        cp = M.copy(M.act, [tr, free], hTs.ap, tb.ap)
        yield
        pr = M.mm(cp, [(tb.ap[:, 0:P], [(w("w2T")[:, j * P:j * P + P], hTs.ap[:, j * P:j * P + P]) for j in range(4)])])
        hTs.free = pr
        yield
        d, free = dT.take()
        dt = M.dve([pr, free], nc.vector.scalar_tensor_tensor, d.ap, tb.ap[:, 0:P], w("b2col"),
                   swaT[:, t * P:t * P + P], ALU.add, ALU.subtract)
        if final:
            dt = M.dve(dt, nc.vector.tensor_scalar, d.ap[:, P - MEM0:], d.ap[:, P - MEM0:], float(BATCH), None, ALU.mult)
            dt = M.dve(dt, nc.vector.memset, d.ap[:, 0:P - MEM0], 0.0)
        tb.free = dt
        yield
        db, free = banks.take()
        tr = M.transposes([free, dt], [(db.ap[:, 0:P], d.ap)])
        hb, free = banks.take()
        dz = M.mm(free, [(hb.ap, [(d.ap, w("w2"))])])
        d.free = dz
        yield
        dk, free = dtok.take()
        dc = M.copy(M.act, [tr, free], dk.ap, db.ap[:, 0:P])
        db.free = dc
        e, free = dh.take()
        a = M.dve([free, st, ht], nc.vector.scalar_tensor_tensor, e.ap, s.ap, 1.0, hs.ap, ALU.subtract, ALU.mult)
        a = M.dve(a, nc.vector.tensor_tensor, e.ap, s.ap, e.ap, ALU.subtract)
        s.free = a
        a = M.dve([a, dz], nc.vector.tensor_tensor, e.ap, hb.ap, e.ap, ALU.mult)
        hb.free = a
        yield
        pe = M.pe
        pe.wait([a, dc])
        mm = nc.tensor.matmul
        kw = dict(start=first, stop=final, skip_group_check=True)
        mm(g1, tok, e.ap, **kw)
        for j in range(4):
            mm(g2[:, j * P:j * P + P], hs.ap[:, j * P:j * P + P], dk.ap, start=first and j == 0, stop=final,
               skip_group_check=True)
        mm(gb1[0:1, :], ones[:, 0:1], e.ap, **kw)
        end = pe.mark(mm(gb2[:, 0:1], dk.ap, ones[:, 0:1], **kw))
        for x in (e, hs, dk):
            x.free = end
        grads.append(end)

    for t in range(NT):
        for _ in gradient(t):
            pass
    nw1, nw2, nb1, nb2, keep = M.alloc(HID0), M.alloc(HID0), M.alloc(HID0), M.alloc(1), M.alloc(1)
    k1 = M.dve([], nc.vector.tensor_scalar, keep, w("alpha"), -1.0, 1.0, ALU.mult, ALU.add)

    def step(out, p, g, parts):
        t = M.dve([grads[-1]], nc.vector.tensor_scalar, out, g, w("theta")[0:parts], None, ALU.mult)
        return M.dve([t, k1], nc.vector.scalar_tensor_tensor, out, p, keep[0:parts], out, ALU.mult, ALU.subtract)

    updated = [step(nw1, w("w1"), g1, P), step(nw2, w("w2T"), g2, P), step(nb1[0:1, :], w("b1")[0:1, :], gb1[0:1, :], 1),
               step(nb2, w("b2col"), gb2[:, 0:1], P)]
    for b in M.bank:
        b.free = updated
    banks = Ring(M.bank)
    hid, outm, gate1, gate2 = M.ring(2, 4, GROUP), M.ring(2, GROUP), M.ring(2, GROUP), M.ring(2, GROUP)
    done = []
    for g in range(GROUPS):
        sl = slice(g * GROUP, (g + 1) * GROUP)
        hs, hfree = hid.take()
        ts = []
        for j in range(4):
            b, free = banks.take()
            t = M.mm([free, updated], [(b.ap, [(nw1[:, j * P:j * P + P], xT[:, sl]),
                                               (nb1[0:1, j * P:j * P + P], ones512(M)[0:1, :])])])
            t2 = M.act([t, hfree], nc.scalar.activation, hs.ap[:, j, :], b.ap, ACT.Sigmoid)
            t2 = M.dve(t2, nc.vector.tensor_tensor, hs.ap[:, j, :], b.ap, hs.ap[:, j, :], ALU.mult)
            b.free = t2
            ts.append(t2)
        b, free = banks.take()
        t = M.mm([free, ts], [(b.ap, [(nw2[:, j * P:j * P + P], hs.ap[:, j, :]) for j in range(4)])])
        hs.free = t
        om, free = outm.take()
        t = M.dve([t, free], nc.vector.tensor_scalar, om.ap, b.ap, nb2, None, ALU.add)
        b.free = t
        b2, free = banks.take()
        t2 = M.mm([free, t], [(b2.ap, [(w("lin2"), om.ap)])])
        b1, free = banks.take()
        t1 = M.mm(free, [(b1.ap, [(w("lin1"), swaT[:, sl])])])
        a, free = gate1.take()
        t1 = M.act([t1, free], nc.scalar.activation, a.ap, b1.ap, ACT.Sigmoid)
        b1.free = t1
        z, free = gate2.take()
        t2 = M.act([t2, free], nc.scalar.activation, z.ap, b2.ap, ACT.Sigmoid)
        b2.free = t2
        t1 = M.dve(t1, nc.vector.tensor_tensor, a.ap, a.ap, swaT[:, sl], ALU.mult)
        t2 = M.dve(t2, nc.vector.tensor_tensor, z.ap, z.ap, om.ap, ALU.mult)
        om.free = t2
        t = M.dve([t1, t2], nc.vector.tensor_tensor, a.ap, a.ap, z.ap, ALU.add)
        z.free = t
        b, free = banks.take()
        tr = M.transposes([free, t], [(b.ap[:, j:j + P], a.ap[:, j:j + P]) for j in range(0, GROUP, P)])
        a.free = tr
        t = M.copy(M.act, tr, M.y[:, 4 * g:4 * g + 4, :], b.ap.rearrange("p (t d) -> p t d", d=DIM))
        b.free = t
        done += [t] * 4
    return done


def ones512(M):
    return M.c("ones")[:, 0:1].broadcast_to([P, GROUP])


def attention_heads8(M, stage, rings, batch_state, kv_pick, mask_of, clip, scale, finish_tile, b):
    st = batch_state[b]
    qT, kT, v = st["q"], st["k"], st["v"]
    out = []
    for half in range(2):
        t = 2 * b + half
        mask = mask_of(half)
        if mask is not None and not clip:
            segments = [(P, P)] if half == 0 else [(0, 2 * P)]
            block = lambda col, half=half: half if col >= P else 0
        else:
            segments = [(0, 2 * P)]
            block = lambda col: col // P
        def scored(token, half=half, st=st):
            if half == 1:
                st["slots"][0].free = token

        def valued(token, half=half, st=st):
            if half == 1:
                st["slots"][1].free = token

        tile = {"order": [(h, h + 4) for h in (0, 1, 2, 3, 8, 9, 10, 11)], "scored": scored, "valued": valued, "ready": st["ready"], "vready": st["vready"], "segments": segments, "mask": mask, "clip": clip,
                "q": lambda h, half=half: qT[32 * (h % 4):32 * (h % 4) + 32, h // 4, half * P:half * P + P],
                "k": lambda h, sg, block=block: kT[32 * (h % 4):32 * (h % 4) + 32, h // 4,
                                                   block(sg[0]) * P:block(sg[0]) * P + sg[1]],
                "v": lambda h, blk, block=block: v[:, block(blk * P), 32 * kv_pick(h):32 * kv_pick(h) + 32]}
        out += M.attend(rings, HEADS, HDIM, scale, tile, lambda attn, done, g, t=t: finish_tile(attn, done, t))
    return out


def run_batches(prepare, pairs):
    for _ in prepare(0):
        pass

    following = [iter(())]

    def units():
        for b in range(BATCH):
            following[0] = prepare(b + 1) if b + 1 < BATCH else iter(())
            for p in pairs(b):
                yield p
            for _ in following[0]:
                pass

    pipeline(units(), lambda: next(following[0], None), 2)


def project_out(M, banks, wo, wait_w, done_y, bias=None):
    def finish(attn, done, t):
        bank, free = banks.take()
        pairs = [(attn.ap[:, k * P:k * P + P], wo[:, k * P:k * P + P]) for k in range(CHUNKS)]
        if bias is not None:
            pairs.append((M.c("ones")[0:1, :], bias[0:1, :]))
        pr = M.mm([free, done, wait_w], [(bank.ap[:, 0:P], pairs)])
        attn.free = pr
        yield
        cp = M.copy(M.act, pr, M.y[:, t, :], bank.ap[:, 0:P])
        bank.free = cp
        done_y[t] = cp
    return finish


def zero_ring(M, n, *shape):
    ring = M.ring(n, *shape)
    for s in ring.slots:
        s.free = M.pool([], M.nc.gpsimd.memset, s.ap, 0.0)
    return ring


def stage_split(M, ready):
    nc, c, w = M.nc, M.c, lambda n: M.w("split", n)
    wait_w = M.loaded["split"][0]
    tt, ts, stt = nc.vector.tensor_tensor, nc.vector.tensor_scalar, nc.vector.scalar_tensor_tensor
    banks = Ring(M.bank)
    turned = M.turn(ready, M.xn, M.xnT, banks)
    heads = lambda ap: ap.rearrange("p (h d) -> p h d", d=HDIM)
    gn, gsq, gl = M.alloc(DIM), M.alloc(DIM), M.alloc(HEADS)
    t = M.dve(wait_w, tt, gsq, w("g"), w("g"), ALU.mult)
    t = M.dve(t, nc.vector.tensor_reduce, gl, heads(gsq), AX, ALU.add)
    t = M.pool(t, nc.gpsimd.tensor_tensor, gl, gl, c("half", HEADS), ALU.pow)
    guide = M.dve(t, tt, heads(gn), heads(w("g")), gl.unsqueeze(2).broadcast_to([P, HEADS, HDIM]), ALU.mult)
    dots, lens = M.alloc(TILES, HEADS), M.alloc(TILES, HEADS)
    tmp, tmp2 = M.ring(2, GROUP), M.ring(2, GROUP)
    ts_ = []
    four = lambda ap: ap.rearrange("p (t h d) -> p t h d", t=4, d=HDIM)
    for g in range(GROUPS):
        bank, free = banks.take()
        t = M.mm([free, turned[g], wait_w], [(bank.ap[:, P * k:P * k + P],
                                              [(M.xnT[:, GROUP * g + P * k:GROUP * g + P * k + P], w("wq"))]) for k in range(4)])
        a, free = tmp.take()
        t1 = M.dve([t, free, guide], tt, a.ap.rearrange("p (t d) -> p t d", t=4),
                   bank.ap.rearrange("p (t d) -> p t d", t=4), gn.unsqueeze(1).broadcast_to([P, 4, DIM]), ALU.mult)
        s, free = tmp2.take()
        t2 = M.act([t1, free], nc.scalar.activation, s.ap, bank.ap, ACT.Square)
        bank.free = [t1, t2]
        a.free = M.dve(t1, nc.vector.tensor_reduce, dots[:, 4 * g:4 * g + 4, :], four(a.ap), AX, ALU.add)
        s.free = M.dve(t2, nc.vector.tensor_reduce, lens[:, 4 * g:4 * g + 4, :], four(s.ap), AX, ALU.add)
        ts_ += [a.free, s.free]
    flat2 = lambda ap: ap.rearrange("p t h -> p (t h)")
    inverse, room = M.alloc(TILES, HEADS), M.alloc(TILES, HEADS)
    t = M.rsqrt(ts_, flat2(lens), flat2(inverse), flat2(room))
    t = M.dve(t, tt, dots, dots, inverse, ALU.mult)
    sim, lo, ext, ext2 = M.alloc(TILES), M.alloc(TILES), M.alloc(2), M.alloc(2)
    t = M.dve(t, nc.vector.tensor_reduce, sim, dots, AX, ALU.add)
    sim_t = M.dve(t, ts, sim, sim, 1.0 / HEADS, None, ALU.mult)
    t = M.dve(sim_t, stt, lo, c("reg"), NEG, sim, ALU.mult, ALU.add)
    t = M.dve(t, nc.vector.tensor_reduce, ext[:, 0:1], lo, AX, ALU.max)
    t = M.dve(t, stt, lo, c("reg"), NEG, sim, ALU.mult, ALU.subtract)
    t = M.dve(t, nc.vector.tensor_reduce, ext[:, 1:2], lo, AX, ALU.max)
    t = M.pool(t, nc.gpsimd.partition_all_reduce, ext2, ext, P, bass.bass_isa.ReduceOp.max)
    rng, up, pos, neg = M.alloc(1), M.alloc(TILES), M.alloc(TILES), M.alloc(TILES)
    t = M.dve(t, ts, rng, ext2[:, 0:1], ext2[:, 1:2], 0.9, ALU.add, ALU.mult)
    t = M.dve(t, ts, up, sim, ext2[:, 1:2], rng, ALU.add, ALU.is_gt)
    notreg = M.alloc(TILES)
    a = M.dve([], ts, notreg, c("reg"), -1.0, 1.0, ALU.mult, ALU.add)
    kpos, kneg = M.alloc(TILES), M.alloc(TILES)
    b0 = M.dve([t, a], tt, kpos, up, notreg, ALU.mult)
    b1 = M.dve(b0, tt, kneg, notreg, kpos, ALU.subtract)
    b2 = M.dve(b0, tt, pos, kpos, c("reg"), ALU.add)
    b3 = M.dve(b2, ts, neg, pos, -1.0, 1.0, ALU.mult, ALU.add)
    extra = M.alloc(2, TILES, 2)
    fills = [M.dve(b3, ts, extra[:, 0, :, 0], pos, 1.0, None, ALU.mult), M.dve(b3, ts, extra[:, 0, :, 1], neg, 1.0, None, ALU.mult),
             M.dve(b3, ts, extra[:, 1, :, 0], kneg, NEG, None, ALU.mult), M.dve(b3, ts, extra[:, 1, :, 1], kpos, NEG, None, ALU.mult)]
    spread = M.ring(2, 2, P)
    for s in spread.slots:
        s.free = M.pool([], nc.gpsimd.memset, s.ap, 0.0)
    qx = M.ring(2, 4, HEADS * REG)
    for s in qx.slots:
        s.free = M.pool([], nc.gpsimd.memset, s.ap, 0.0)
    rings = M.attention_rings(3, 2, 1)
    rings["A"] = M.ring(2, 4 * P)
    gen = Ring(M.bank[6:8])
    start = M.everything()
    for b in M.bank:
        b.free = start
    M.extra = [[M.xn.rearrange("p t d -> p (t d)"), TILES * DIM, 0]]
    kq = M.ring(2, 2, 4, SEQ)
    vs, exs = zero_ring(M, 3, 2, 4 * P), M.ring(2, 2, SEQ)
    regs = M.ring(3, 4 * REG)
    small = M.ring(2, 4)
    pr_, prT, orr = M.ring(2, SEQ), M.ring(2, 2 * HEADS * REG), M.ring(2, 4 * P)
    spread_v = lambda v: v.rearrange("p b (h d) -> p b h d", h=HEADS)[:, :, :, 0:HDIM]
    state, done_y = {}, [None] * TILES
    NR = HEADS * REG

    def prepare(b):
        sl = slice(b * SEQ, (b + 1) * SEQ)
        g = b // 2
        ex, xfree = exs.take()
        bank, free = gen.take()
        trs = []
        for half in range(2):
            sp, free2 = spread.take()
            v = sp.ap.rearrange("p s (g r) -> p s g r", g=4)[:, :, :, HDIM:HDIM + 2]
            src = extra[:, :, 2 * b + half, :].unsqueeze(2).broadcast_to([P, 2, 4, 2])
            t1 = M.pool([fills, free2], nc.gpsimd.tensor_copy, v[:, 0], src[:, 0])
            t1 = M.pool([], nc.gpsimd.tensor_copy, v[:, 1], src[:, 1])
            t1 = M.transposes([free, t1], [(bank.ap[:, s * SEQ + half * P:s * SEQ + half * P + P], sp.ap[:, s, :]) for s in range(2)])
            sp.free = t1
        yield
        ext_t = M.copy(M.act, [t1, xfree], ex.ap, bank.ap.rearrange("p (s n) -> p s n", s=2))
        bank.free = ext_t
        yield
        slot, kfree = kq.take()
        outs = []
        for which, name in enumerate(("wqs", "wks")):
            for pairc in range(2):
                bank, free = gen.take()
                t = M.mm([free, turned[g], wait_w], [(bank.ap[:, i * SEQ:(i + 1) * SEQ],
                         [(w(name)[:, (2 * pairc + i) * P:(2 * pairc + i + 1) * P], M.xnT[:, sl])]) for i in range(2)])
                yield
                t = M.dve([t, kfree, ext_t], tt, slot.ap[:, which, 2 * pairc:2 * pairc + 2, :],
                          bank.ap.rearrange("p (c n) -> p c n", c=2),
                          ex.ap[:, which, :].unsqueeze(1).broadcast_to([P, 2, SEQ]), ALU.add)
                bank.free = t
                outs.append(t)
        ex.free = outs
        bank, free = gen.take()
        v, vfree = vs.take()
        t = M.mm([free], [(bank.ap[:, i * P:i * P + P], [(M.xnT[:, b * SEQ + i * P:b * SEQ + (i + 1) * P], w("wv"))]) for i in range(2)])
        yield
        vt = None
        for i in range(2):
            vt = M.copy(M.act, [t, vfree], spread_v(v.ap)[:, i], bank.ap[:, i * P:i * P + P].rearrange("p (h d) -> p h d", h=HEADS))
        bank.free = vt
        q = slot.ap[:, 0]
        k = slot.ap[:, 1]
        x, xf = qx.take()
        for gg in range(4):
            dst = x.ap[32 * gg:32 * gg + 32].rearrange("p c (h r) -> p c h r", r=REG)
            for cc in range(4):
                t = M.dve([xf, outs], ts, dst[:, cc, 4 * cc + gg, :], q[32 * gg:32 * gg + 32, cc, 0:REG],
                          c("turn")[32 * gg:32 * gg + 32], None, ALU.add)
        yield
        bank, free = gen.take()
        t = M.mm([free, t], [(bank.ap[0:NR, 0:SEQ], [(x.ap[:, cc, :], k[:, cc, :]) for cc in range(4)])])
        x.free = t
        yield
        sm, sf = small.take()
        s = sm.ap[0:NR]
        t = M.dve([t, sf], nc.vector.tensor_reduce, s[:, 0:1], bank.ap[0:NR, 0:SEQ], AX, ALU.max)
        t = M.dve(t, ts, s[:, 1:2], s[:, 0:1], -(HDIM ** -0.5), None, ALU.mult)
        p_, pf = pr_.take()
        yield
        e = M.act([t, pf], nc.scalar.activation, p_.ap[0:NR], bank.ap[0:NR, 0:SEQ], ACT.Exp, bias=s[:, 1:2],
                  scale=HDIM ** -0.5, accum_out=s[:, 2:3])
        bank.free = e
        yield
        bank, free = gen.take()
        t = M.transposes([e, free], [(bank.ap[:, i * NR:(i + 1) * NR], p_.ap[0:NR, i * P:i * P + P]) for i in range(2)])
        p_.free = t
        yield
        pT, pf = prT.take()
        t = M.copy(M.act, [t, pf], pT.ap, bank.ap[:, 0:2 * NR])
        yield
        bank.free = t
        bank, free = gen.take()
        t = M.mm([t, vt, free], [(bank.ap[0:NR], [(pT.ap[:, i * NR:(i + 1) * NR], v.ap[:, i, :]) for i in range(2)])])
        pT.free = t
        yield
        r = M.dve(e, nc.vector.reciprocal, s[:, 3:4], s[:, 2:3])
        o, of_ = orr.take()
        t = M.dve([t, r, of_], stt, o.ap[0:NR], bank.ap[0:NR], s[:, 3:4], c("block")[0:NR], ALU.mult, ALU.mult)
        sm.free = t
        yield
        t = M.mm(t, [(bank.ap[:, k_ * REG:(k_ + 1) * REG], [(o.ap[0:NR, k_ * P:k_ * P + P], c("pick")[0:NR, :])])
                     for k_ in range(CHUNKS)])
        o.free = t
        yield
        rg, rf = regs.take()
        t = M.copy(M.act, [t, rf], rg.ap, bank.ap[:, 0:4 * REG])
        bank.free = t
        state[b] = {"q": q, "k": k, "v": v.ap, "ready": outs, "vready": vt, "reg": rg, "regt": t, "slots": (slot, v)}

    out = project_out(M, gen, w("wo"), wait_w, done_y, bias=w("bo"))

    def finish(attn, done, t):
        if t % 2 == 0:
            st = state[t // 2]
            both = attn.ap.rearrange("p (c n) -> p c n", c=CHUNKS)[:, :, 0:REG]
            done = M.dve([done, st["regt"]], stt, both, both, 0.5, st["reg"].ap.rearrange("p (c n) -> p c n", c=CHUNKS),
                         ALU.mult, ALU.add)
            st["reg"].free = done
        yield from out(attn, done, t)

    def pairs(b):
        yield from attention_heads8(M, "split", rings, state, lambda h: h, lambda half: None, None, HDIM ** -0.5, finish, b)

    run_batches(prepare, pairs)
    return done_y


def stage_linear(M, ready):
    nc, c, w = M.nc, M.c, lambda n: M.w("linear", n)
    wait_w = M.loaded["linear"][0]
    tt, ts, stt = nc.vector.tensor_tensor, nc.vector.tensor_scalar, nc.vector.scalar_tensor_tensor
    banks = Ring(M.bank)
    turned = M.turn(ready, M.xn, M.xnT, banks)
    ones = c("ones")
    gate = M.alloc(HEADS)
    gt = M.act(wait_w, nc.scalar.activation, gate, w("stdp"), ACT.Sigmoid)
    qT = M.alloc(TOKENS)
    kk, vv = M.alloc(TILES, DIM), M.alloc(TILES, DIM)
    ex = M.ring(3, GROUP)
    kv = M.ring(2, DIM + HEADS)
    an, aT, rd = M.ring(2, DIM), M.ring(2, DIM), M.ring(2, HEADS)

    def phi(after, bank, out, bias=None):
        e, free = ex.take()
        z = bank.ap
        if bias is None:
            t = M.dve([after, free], ts, e.ap, z, 0.0, None, ALU.min)
        else:
            t = M.dve([after, free], ts, e.ap, z, bias, 0.0, ALU.add, ALU.min)
        t = M.act(t, nc.scalar.activation, e.ap, e.ap, ACT.Exp)
        if bias is None:
            t = M.dve(t, stt, out, z, 0.0, e.ap, ALU.max, ALU.add)
        else:
            t1 = M.dve([after], ts, out, z, bias, 0.0, ALU.add, ALU.max)
            t = M.dve([t, t1], tt, out, out, e.ap, ALU.add)
        bank.free = t
        e.free = t
        return t

    qd, kd, vd = {}, {}, {}
    for g in range(GROUPS):
        sl = slice(g * GROUP, (g + 1) * GROUP)
        b, free = banks.take()
        t = M.mm([free, turned[g], wait_w], [(b.ap, [(w("Wq"), M.xnT[:, sl])])])
        qd[g] = phi(t, b, qT[:, sl], w("bq"))
        for name, bias, dst in (("Wk", "bk", kk), ("Wv", "bv", vv)):
            b, free = banks.take()
            t = M.mm([free], [(b.ap[:, P * i:P * i + P], [(M.xnT[:, g * GROUP + i * P:g * GROUP + (i + 1) * P], w(name)),
                                                          (ones[0:1, :], w(bias)[0:1, :])]) for i in range(4)])
            d = dst[:, 4 * g:4 * g + 4, :].rearrange("p t d -> p (t d)")
            if name == "Wk":
                kd[g] = phi(t, b, d)
            else:
                vd[g] = M.copy(M.act, t, d, b.ap)
                b.free = vd[g]
    done = []
    for bt in range(BATCH):
        g = bt // 2
        b, free = banks.take()
        t = M.mm([free, kd[g], vd[g]], [(b.ap[:, 0:P], [(kk[:, 2 * bt + i, :], vv[:, 2 * bt + i, :]) for i in range(2)]),
                                        (b.ap[:, P:P + 1], [(kk[:, 2 * bt + i, :], ones[:, 0:1]) for i in range(2)])])
        s, free = kv.take()
        t1 = M.dve([t, free], tt, s.ap[:, 0:P], b.ap[:, 0:P], c("blockdiag"), ALU.mult)
        t2 = M.dve([], ts, s.ap[:, P:], c("blockhead"), b.ap[:, P:P + 1], None, ALU.mult)
        b.free = [t1, t2]
        for i in range(2):
            tile = 2 * bt + i
            b, free = banks.take()
            t = M.mm([free, t1, t2, qd[g]], [(b.ap[:, 0:P + HEADS], [(qT[:, tile * P:tile * P + P], s.ap)])])
            s.free = t
            r, free = rd.take()
            t3 = M.dve([t, free], ts, r.ap, b.ap[:, P:P + HEADS], 1e-6, None, ALU.add)
            t3 = M.dve(t3, nc.vector.reciprocal, r.ap, r.ap)
            t3 = M.dve([t3, gt], tt, r.ap, r.ap, gate, ALU.mult)
            a, free = an.take()
            t4 = M.dve([t3, free], tt, a.ap.rearrange("p (h d) -> p h d", d=HDIM),
                       b.ap[:, 0:P].rearrange("p (h d) -> p h d", d=HDIM),
                       r.ap.unsqueeze(2).broadcast_to([P, HEADS, HDIM]), ALU.mult)
            r.free = t4
            t5 = M.transposes(t4, [(b.ap[:, 256:384], a.ap)])
            a.free = t5
            x, free = aT.take()
            t5 = M.copy(M.act, [t5, free], x.ap, b.ap[:, 256:384])
            t5 = M.mm(t5, [(b.ap[:, 384:512], [(x.ap, w("Wo")), (ones[0:1, :], w("bo")[0:1, :])])])
            x.free = t5
            t5 = M.copy(M.act, t5, M.y[:, tile, :], b.ap[:, 384:512])
            b.free = t5
            done.append(t5)
    return done


def top_two(M, after, logits, E):
    nc = M.nc
    tt, ts = nc.vector.tensor_tensor, nc.vector.tensor_scalar
    B3 = lambda ap: ap.broadcast_to([P, TILES, E])
    red, coef = M.alloc(TILES), M.alloc(TILES, E)
    t = M.dve(after, nc.vector.tensor_reduce, red, logits, AX, ALU.max)
    t = M.dve(t, tt, logits, logits, B3(red.unsqueeze(2)), ALU.subtract)
    t = M.act(t, nc.scalar.activation, logits, logits, ACT.Exp)
    t = M.dve(t, nc.vector.tensor_reduce, red, logits, AX, ALU.add)
    t = M.dve(t, nc.vector.reciprocal, red, red)
    t = M.dve(t, tt, logits, logits, B3(red.unsqueeze(2)), ALU.mult)
    best, index = M.alloc(TILES, 8), M.alloc(TILES, 8)
    fi = M.alloc(TILES, 8)
    for i in range(TILES):
        u = M.dve(t, nc.vector.max, best[:, i, :], logits[:, i, :])
        v = M.dve(u, nc.vector.max_index, index[:, i, :].bitcast(U32), best[:, i, :], logits[:, i, :])
    v = M.dve(v, nc.vector.tensor_copy, fi, index.bitcast(U32))
    t = M.dve(v, tt, red, best[:, :, 0], best[:, :, 1], ALU.add)
    t = M.dve(t, nc.vector.reciprocal, red, red)
    t = M.dve(t, tt, best[:, :, 0:2], best[:, :, 0:2], red.unsqueeze(2).broadcast_to([P, TILES, 2]), ALU.mult)
    iota = M.c("iota", E).unsqueeze(1)
    hot = M.alloc(TILES, E)
    t0 = M.dve(t, tt, coef, B3(iota), B3(fi[:, :, 0:1]), ALU.is_equal)
    t0 = M.dve(t0, tt, coef, coef, B3(best[:, :, 0:1]), ALU.mult)
    t1 = M.dve(t0, tt, hot, B3(iota), B3(fi[:, :, 1:2]), ALU.is_equal)
    t1 = M.dve(t1, tt, hot, hot, B3(best[:, :, 1:2]), ALU.mult)
    return coef, M.dve(t1, tt, coef, coef, hot, ALU.add)


def experts(M, stage, E, xT, x_ready, coef, coef_ready, norm, first):
    nc, w = M.nc, lambda n: M.w(stage, n)
    wait_w = M.loaded[stage][0]
    tt, ts, stt = nc.vector.tensor_tensor, nc.vector.tensor_scalar, nc.vector.scalar_tensor_tensor
    up, down = Ring(M.bank[0:6]), Ring(M.bank[6:8])
    act, hid = M.ring(4, GROUP), M.ring(3, 2, GROUP)
    mid = M.ring(3, 4, DIM)
    st_at = [0]
    last = [first[t] for t in range(TILES)]

    def unit(e, g):
        sl = slice(g * GROUP, (g + 1) * GROUP)
        gates, ups = [], []
        for f in range(2):
            b, free = up.take()
            t = M.mm([free, wait_w, x_ready], [(b.ap, [(w(f"gate{e}")[:, f * P:f * P + P], xT[:, sl])])])
            gates.append((b, t))
            b, free = up.take()
            t = M.mm([free], [(b.ap, [(w(f"up{e}")[:, f * P:f * P + P], xT[:, sl])])])
            ups.append((b, t))
        yield
        h, hfree = hid.take()
        ts_ = []
        for f in range(2):
            a, free = act.take()
            t = M.act([gates[f][1], free], nc.scalar.activation, a.ap, gates[f][0].ap, ACT.Silu)
            gates[f][0].free = t
            t = M.dve([t, ups[f][1], hfree], tt, h.ap[:, f, :], ups[f][0].ap, a.ap, ALU.mult)
            ups[f][0].free = t
            a.free = t
            ts_.append(t)
        yield
        b, free = down.take()
        yv = b.ap.rearrange("p (t d) -> p t d", t=4)
        t = M.mm([free, ts_], [(yv[:, k, :], [(h.ap[:, f, k * P:k * P + P], w(f"down{e}")[:, f * P:f * P + P])
                                              for f in range(2)]) for k in range(4)])
        h.free = t
        yield
        y = M.y[:, 4 * g:4 * g + 4, :]
        cf = coef[:, 4 * g:4 * g + 4, e]
        if not norm:
            for k in range(4):
                t2 = M.dve([t, coef_ready, last[4 * g]], stt, y[:, k, :], yv[:, k, :], coef[:, 4 * g + k, e:e + 1],
                           y[:, k, :], ALU.mult, ALU.add)
            b.free = t2
            last[4 * g] = t2
            return
        at = 48 * (st_at[0] % 4)
        st_at[0] += 1
        mean, rstd, mt = M.moments([t, stats_free[(st_at[0] - 1) % 4]], [yv[:, k, :] for k in range(4)], 4, at)
        sc = M.stats[:, 200 + at // 12:204 + at // 12]
        t2 = M.dve([mt, coef_ready], tt, sc, rstd, cf, ALU.mult)
        m, free = mid.take()
        for k in range(4):
            t3 = M.dve([t2, free], ts, m.ap[:, k, :], yv[:, k, :], mean[:, k:k + 1], sc[:, k:k + 1], ALU.subtract, ALU.mult)
        b.free = t3
        stats_free[(st_at[0] - 1) % 4] = t3
        yield
        gain = w("lng")[:, e * DIM:(e + 1) * DIM].unsqueeze(1).broadcast_to([P, 4, DIM])
        t4 = M.pool([t3], nc.gpsimd.tensor_tensor, m.ap, m.ap, gain, ALU.mult)
        t4 = M.pool([t4, last[4 * g]], nc.gpsimd.tensor_tensor, y, y, m.ap, ALU.add)
        m.free = t4
        last[4 * g] = t4

    stats_free = [None] * 4
    pipeline(unit(e, g) for e in range(E) for g in range(GROUPS))
    return [last[4 * (t // 4)] for t in range(TILES)]


def router(M, xT, x_ready, wr, E, banks, bias=None):
    nc = M.nc
    logits = M.alloc(TILES, E)
    b, free = banks.take()
    t = M.mm([free, x_ready], [(b.ap[:, E * i:E * i + E], [(xT[:, P * i:P * i + P], wr)] + (
        [(M.c("ones")[0:1, :], bias[0:1, :])] if bias is not None else [])) for i in range(TILES)])
    t = M.copy(M.dve, t, logits, b.ap[:, 0:E * TILES].rearrange("p (t e) -> p t e", e=E))
    b.free = t
    return top_two(M, t, logits, E)


def stage_moe1(M, ready):
    nc, w = M.nc, lambda n: M.w("moe1", n)
    banks = Ring(M.bank)
    turned = M.turn(ready, M.xn, M.xnT, banks)
    coef, ct = router(M, M.xnT, [turned, M.loaded["moe1"][0]], w("router"), EXP1, banks, w("rb"))
    cT = M.ring(2, 4, P)
    first = []
    for g in range(GROUPS):
        b, free = banks.take()
        t = M.transposes([free, ct], [(b.ap[0:EXP1, P * k:P * k + P], coef[:, 4 * g + k, :]) for k in range(4)])
        s, sf = cT.take()
        t = M.copy(M.act, [t, sf], s.ap[0:EXP1], b.ap[0:EXP1, :].rearrange("p (k n) -> p k n", k=4))
        b.free = t
        b, free = banks.take()
        t = M.mm([free, t], [(b.ap[:, P * k:P * k + P], [(s.ap[0:EXP1, k, :], w("lnb")[0:EXP1, :])]) for k in range(4)])
        s.free = t
        t = M.copy(M.act, t, M.y[:, 4 * g:4 * g + 4, :], b.ap.rearrange("p (k n) -> p k n", k=4))
        b.free = t
        first += [t] * 4
    return experts(M, "moe1", EXP1, M.xnT, turned, coef, ct, True, first)


def stage_mamba(M, ready):
    nc, c, w = M.nc, M.c, lambda n: M.w("mamba", n)
    wait_w = M.loaded["mamba"][0]
    tt, ts, stt = nc.vector.tensor_tensor, nc.vector.tensor_scalar, nc.vector.scalar_tensor_tensor
    banks = Ring(M.bank)
    turned = M.turn(ready, M.xn, M.xnT, banks)
    xn_free = turned
    u, dl = M.alloc(2, TOKENS), M.alloc(2, TOKENS)
    bc = M.alloc(TOKENS)
    raw = M.ring(1, TOKENS)
    du = M.alloc(2, TOKENS)
    ut = {}
    act1 = M.xn.rearrange("p t d -> p (t d)")
    for h in range(2):
        r, rfree = raw.take()
        seq = lambda ap: ap.rearrange("p (b s) -> p b s", b=BATCH)
        for g in range(GROUPS):
            b, free = banks.take()
            t = M.mm([free, turned[g], wait_w], [(b.ap, [(w("in")[:, h * P:h * P + P], M.xnT[:, g * GROUP:(g + 1) * GROUP])])])
            t = M.copy(M.act, [t, rfree], r.ap[:, g * GROUP:(g + 1) * GROUP], b.ap)
            b.free = t
        tap = lambda k: w("conv")[:, 3 * h + k:3 * h + k + 1]
        o, s = seq(u[:, h, :]), seq(r.ap)
        t = M.dve([t], ts, u[:, h, :], r.ap, tap(1), w("convb")[:, h:h + 1], ALU.mult, ALU.add)
        t = M.dve(t, stt, o[:, :, 1:], s[:, :, :-1], tap(0), o[:, :, 1:], ALU.mult, ALU.add)
        t = M.dve(t, stt, o[:, :, :-1], s[:, :, 1:], tap(2), o[:, :, :-1], ALU.mult, ALU.add)
        r.free = t
        sg = M.act([t, xn_free] + ([ut[0]] if h else []), nc.scalar.activation, act1, u[:, h, :], ACT.Sigmoid)
        ut[h] = M.dve(sg, tt, u[:, h, :], u[:, h, :], act1, ALU.mult)
    NX = INNER + 2 * STATE
    xd = du
    for g in range(GROUPS):
        sl = slice(g * GROUP, (g + 1) * GROUP)
        for m0, mn, dst in ((0, P, xd[:, 0, sl]), (P, P, xd[:, 1, sl]), (2 * P, 2 * STATE, bc[0:2 * STATE, sl])):
            b, free = banks.take()
            t = M.mm([free, ut[0], ut[1]], [(b.ap[0:mn, :], [(w("xp")[:, h * NX + m0:h * NX + m0 + mn], u[:, h, sl]) for h in range(2)])])
            t = M.copy(M.act, t, dst, b.ap[0:mn, :])
            b.free = t
    xdt = t
    ready_d = []
    ex, lnb = act1, raw.slots[0].ap
    for h in range(2):
        for g in range(GROUPS):
            sl = slice(g * GROUP, (g + 1) * GROUP)
            b, free = banks.take()
            t = M.mm([free, xdt], [(b.ap, [(w("dt")[:, k * INNER + h * P:k * INNER + h * P + P], xd[:, k, sl]) for k in range(2)])])
            t = M.dve(t, ts, dl[:, h, sl], b.ap, w("dtb")[:, h:h + 1], None, ALU.add)
            b.free = t
        dt_used = t
        d = dl[:, h, :]
        t = M.dve([t, ready_d], ts, ex, d, -1.0, None, ALU.mult)
        t = M.dve(t, tt, ex, ex, d, ALU.min)
        e = M.act(t, nc.scalar.activation, ex, ex, ACT.Exp)
        t = M.dve(e, ts, lnb, ex, 1.0, None, ALU.add)
        yv = M.y.rearrange("p t d -> p (t d)")
        l = M.act(t, nc.scalar.activation, yv, lnb, ACT.Ln)
        t = M.dve(l, ts, lnb, lnb, -1.0, None, ALU.add)
        z = M.alloc(TOKENS) if h == 0 else z
        q = M.dve(t, ts, z, lnb, 0.0, None, ALU.is_equal)
        t = M.dve(q, tt, lnb, lnb, z, ALU.add)
        t2 = M.dve(q, tt, yv, yv, z, ALU.add)
        t = M.dve(t, nc.vector.reciprocal, lnb, lnb)
        t = M.dve([t, t2], tt, lnb, lnb, yv, ALU.mult)
        t = M.dve(t, tt, lnb, lnb, ex, ALU.mult)
        t = M.dve(t, stt, d, d, 0.0, lnb, ALU.max, ALU.add)
        ready_d.append(t)
    M.used -= TOKENS
    for h in range(2):
        t = M.dve([ready_d, dt_used], tt, du[:, h, :], dl[:, h, :], u[:, h, :], ALU.mult)
    du_t = t
    am = M.alloc(2 * STATE)
    t = M.dve([], ts, am, w("alog"), 88.7, None, ALU.min)
    t = M.act(t, nc.scalar.activation, am, am, ACT.Exp)
    a_t = M.dve(t, ts, am, am, -1.0, None, ALU.mult)
    start = M.everything()
    for b_ in M.bank:
        b_.free = start
    N = TOKENS // 2
    M.used -= 2 * STATE
    assert True
    keep = am
    M.used += 2 * STATE
    fr = [M.xn.rearrange("p t d -> p (t d)"), raw.slots[0].ap]
    big = [fr[0][:, 0:N], fr[0][:, N:], fr[1][:, 0:N], fr[1][:, N:]]
    yv = M.y.rearrange("p t d -> p (t d)")
    big += [yv[:, 0:N], yv[:, N:]]
    decay, inp = Ring([Slot(x, start) for x in big[0:2]]), Ring([Slot(x, start) for x in big[2:4]])
    hs = Ring([Slot(x, start) for x in big[4:6]])
    hc = M.ring(2, N)
    bcast = Ring([M.bank[0:2], M.bank[2:4], M.bank[4:6]]) if False else None
    bk = Ring([Slot(M.psum[:, 2 * i:2 * i + 2, :].rearrange("p a b -> p (a b)"), start) for i in range(3)])
    ybank = M.psum[:, 6:8, :].rearrange("p a b -> p (a b)")
    yfree = start
    gated = {}

    def unit(h, part, s, ctx_):
        sl = slice(part * N, (part + 1) * N)
        sel = lambda k: c("ident")[0:2 * STATE, k:k + 1].broadcast_to([2 * STATE, P])
        b, free = bk.take()
        bt = M.mm([free], [(b.ap[:, j:j + GROUP], [(sel(s), bc[0:2 * STATE, part * N + j:part * N + j + GROUP])])
                           for j in range(0, N, GROUP)])
        dc, free = decay.take()
        d = M.pool([free, a_t, du_t], nc.gpsimd.tensor_scalar, dc.ap, dl[:, h, sl], am[:, h * STATE + s:h * STATE + s + 1],
                   -1e4, ALU.mult, ALU.max)
        d = M.act(d, nc.scalar.activation, dc.ap, dc.ap, ACT.Exp)
        d = M.pool(d, nc.gpsimd.memset, dc.ap.rearrange("p (b n) -> p b n", n=SEQ)[:, :, 0:1], 0.0)
        yield
        i, free = inp.take()
        t = M.dve([bt, free, du_t], tt, i.ap, du[:, h, sl], b.ap, ALU.mult)
        b.free = t
        b, free = bk.take()
        ct = M.mm([free], [(b.ap[:, j:j + GROUP], [(sel(STATE + s), bc[0:2 * STATE, part * N + j:part * N + j + GROUP])])
                           for j in range(0, N, GROUP)])
        hh, free = hs.take()
        t = M.dve([t, d, free], nc.vector.tensor_tensor_scan, hh.ap, dc.ap, i.ap, 0.0, ALU.mult, ALU.add)
        dc.free = t
        i.free = t
        yield
        o, free = hc.take()
        t = M.dve([t, ct, free], tt, o.ap, hh.ap, b.ap, ALU.mult)
        hh.free = t
        b.free = t
        yield
        M.pe.wait([t, ctx_["yfree"]] if s == 0 else t)
        for j in range(0, N, GROUP):
            m = nc.tensor.matmul(ybank[:, j:j + GROUP], c("ident"), o.ap[:, j:j + GROUP], start=(s == 0), stop=(s == STATE - 1),
                                 skip_group_check=True)
        t = M.pe.mark(m)
        o.free = t
        if s == STATE - 1:
            yield
            t = M.dve([t], stt, u[:, h, sl], u[:, h, sl], w("dp")[:, h:h + 1], ybank, ALU.mult, ALU.add)
            ctx_["next"]["yfree"] = t
            gated[h, part] = t

    ctxs = [{"yfree": start}]
    us = []
    for h in range(2):
        for part in range(2):
            ctxs.append({})
            ctxs[-2]["next"] = ctxs[-1]
            us += [unit(h, part, s, ctxs[-2]) for s in range(STATE)]
    pipeline(us)
    end = M.everything()
    for b_ in M.bank:
        b_.free = end
    banks = Ring(M.bank)
    ya, yb = Ring([Slot(big[0][:, 0:GROUP], end), Slot(big[0][:, GROUP:], end)]), Ring([Slot(big[2][:, 0:GROUP], end)])
    done = []
    gt = {}
    for g in range(GROUPS):
        sl = slice(g * GROUP, (g + 1) * GROUP)
        for h in range(2):
            b, free = banks.take()
            t = M.mm([free], [(b.ap, [(w("in")[:, INNER + h * P:INNER + h * P + P], M.xnT[:, sl])])])
            s, free = ya.take()
            t1 = M.act([t, free], nc.scalar.activation, s.ap, b.ap, ACT.Silu)
            b.free = t1
            t = M.dve([t1, gated[h, g // 2]], tt, u[:, h, sl], u[:, h, sl], s.ap, ALU.mult)
            s.free = t
            gt[h] = t
        b, free = banks.take()
        t = M.mm([free, gt[0], gt[1]], [(b.ap[:, P * k:P * k + P], [(u[:, h, g * GROUP + k * P:g * GROUP + k * P + P], w("out")[:, h * P:h * P + P])
                                                      for h in range(2)]) for k in range(4)])
        t = M.copy(M.act, [t, end], M.y[:, 4 * g:4 * g + 4, :], b.ap.rearrange("p (k n) -> p k n", k=4))
        b.free = t
        done += [t] * 4
    return done


def stage_gqa(M, ready):
    nc, c, w = M.nc, M.c, lambda n: M.w("gqa", n)
    wait_w = M.loaded["gqa"][0]
    tt, ts, stt = nc.vector.tensor_tensor, nc.vector.tensor_scalar, nc.vector.scalar_tensor_tensor
    banks = Ring(M.bank)

    def rms(after, src, out, sq):
        ss = M.stats[:, 400:400 + TILES]
        t = M.act([after, wait_w], nc.scalar.activation, sq, src, ACT.Square)
        M.dve.wait(wait_w)
        t = M.dve(t, nc.vector.tensor_reduce, ss, sq, AX, ALU.add)
        t = M.dve(t, ts, ss, ss, 1.0 / DIM, EPS, ALU.mult, ALU.add)
        inv = M.stats[:, 432:432 + TILES]
        t = M.rsqrt(t, ss, inv, M.stats[:, 464:464 + TILES])
        return [M.dve(t, ts, out[:, i, :], src[:, i, :], inv[:, i:i + 1], None, ALU.mult) for i in range(TILES)]

    h1 = M.y
    at = M.used
    sq = M.alloc(TILES, DIM)
    n1 = rms(ready, M.xn, h1, sq)
    turned = M.turn(n1, h1, M.xnT, banks, scale=w("ln1"))
    M.used = at
    start = M.everything()
    for b in M.bank:
        b.free = start
    rings = M.attention_rings(3, 2, 1)
    rings["A"] = M.ring(2, 4 * P)
    gen = Ring(M.bank[6:8])
    for r in [*rings["P"].slots, *rings["PT"].slots]:
        r.free = start
    kq, vs = M.ring(2, 2, 4, SEQ), M.ring(3, 2, P)
    rot, cs = M.ring(2, 2, SEQ), M.ring(2, 2, SEQ)
    for ring_ in (kq, rot, cs, rings["A"], rings["small"], rings["D"]):
        for s in ring_.slots:
            s.free = start
    for s in vs.slots:
        s.free = M.pool(start, nc.gpsimd.memset, s.ap, 0.0)
    state, done_y = {}, [None] * TILES

    def prepare(b):
        sl = slice(b * SEQ, (b + 1) * SEQ)
        slot, kfree = kq.take()
        outs = []
        for which, (name, rname) in enumerate((("wqs", "wqr"), ("wks", "wkr"))):
            for pc in range(2):
                parts = []
                for nm, tab, ring_ in ((name, "cosT", cs), (rname, "sinT", rot)):
                    bank, free = gen.take()
                    t = M.mm([free, turned[b // 2], wait_w], [(bank.ap[:, i * SEQ:(i + 1) * SEQ],
                             [(w(nm)[:, (2 * pc + i) * P:(2 * pc + i + 1) * P], M.xnT[:, sl])]) for i in range(2)])
                    yield
                    s, free = ring_.take()
                    t = M.dve([t, free], tt, s.ap, bank.ap.rearrange("p (c n) -> p c n", c=2),
                              c(tab).unsqueeze(1).broadcast_to([P, 2, SEQ]), ALU.mult)
                    bank.free = t
                    parts.append((s, t))
                t = M.pool([parts[0][1], parts[1][1], kfree], nc.gpsimd.tensor_tensor, slot.ap[:, which, 2 * pc:2 * pc + 2, :],
                           parts[0][0].ap, parts[1][0].ap, ALU.add)
                parts[0][0].free = t
                parts[1][0].free = t
                outs.append(t)
        bank, free = gen.take()
        v, vfree = vs.take()
        t = M.mm([free], [(bank.ap[:, i * 32:i * 32 + 32], [(M.xnT[:, b * SEQ + i * P:b * SEQ + (i + 1) * P], w("wv"))]) for i in range(2)])
        yield
        for i in range(2):
            vt = M.copy(M.act, [t, vfree], v.ap[:, i, :].rearrange("p (h d) -> p h d", h=4)[:, :, 0:HDIM],
                        bank.ap[:, i * 32:i * 32 + 32].rearrange("p (h d) -> p h d", h=4))
        bank.free = vt
        state[b] = {"q": slot.ap[:, 0], "k": slot.ap[:, 1], "v": v.ap, "ready": outs, "vready": vt, "slots": (slot, v)}

    out = project_out(M, gen, w("wo"), wait_w, done_y)

    def finish(attn, done, t):
        yield from out(attn, done, t)

    run_batches(prepare, lambda b: attention_heads8(M, "gqa", rings, state, lambda h: h // 4, lambda half: c("causal"), None,
                                                    HDIM ** -0.5, finish, b))
    end = M.everything()
    for e in (M.pe, M.act, M.dve, M.pool):
        e.wait(end)
    for b in M.bank:
        b.free = []
    banks = Ring(M.bank)
    M.used = at
    h2, sq = M.alloc(TILES, DIM), M.alloc(TILES, DIM)
    t = M.dve(done_y, tt, M.xn, M.xn, M.y, ALU.add)
    t = M.dve(t, ts, M.xn, M.xn, 100.0, -100.0, ALU.min, ALU.max)
    n2 = rms(t, M.xn, h2, sq)
    turned = M.turn(n2, h2, M.xnT, banks, scale=w("ln2"))
    M.used = at
    coef, ct = router(M, M.xnT, [turned, n2, wait_w], w("wr"), EXP2, banks)
    y0 = M.dve([], nc.vector.tensor_copy, M.y, M.xn)
    done = experts(M, "gqa", EXP2, M.xnT, turned, coef, ct, False, [y0] * TILES)
    clipped = [M.dve(done[4 * g], ts, M.y[:, 4 * g:4 * g + 4, :], M.y[:, 4 * g:4 * g + 4, :], 100.0, -100.0, ALU.min, ALU.max)
               for g in range(GROUPS)]
    return [clipped[t // 4] for t in range(TILES)]


def stage_mla(M, ready):
    nc, c, w = M.nc, M.c, lambda n: M.w("mla", n)
    wait_w = M.loaded["mla"][0]
    banks = Ring(M.bank)
    turned = M.turn(ready, M.xn, M.xnT, banks)
    start = M.everything()
    for b in M.bank:
        b.free = start
    rings = M.attention_rings(3, 2, 1)
    rings["A"] = M.ring(2, 4 * P)
    gen = Ring(M.bank[6:8])
    kq, kv, lat = M.ring(2, 2, 4, SEQ), M.ring(2, SEQ), M.ring(2, SEQ)
    vs = zero_ring(M, 3, 2, 4 * P)
    spread_v = lambda v: v.rearrange("p b (h d) -> p b h d", h=HEADS)[:, :, :, 0:HDIM]
    state, done_y = {}, [None] * TILES

    def prepare(b):
        sl = slice(b * SEQ, (b + 1) * SEQ)
        slot, kfree = kq.take()
        outs = []
        bank, free = gen.take()
        t = M.mm([free, turned[b // 2], wait_w], [(bank.ap[:, 0:SEQ], [(w("Wk"), M.xnT[:, sl]), (w("Wv"), M.xnT[:, sl])])])
        yield
        s, free = kv.take()
        t = M.copy(M.act, [t, free], s.ap, bank.ap[:, 0:SEQ])
        yield
        t = M.mm(t, [(bank.ap[0:LATENT, SEQ:2 * SEQ], [(w("down"), s.ap)])])
        s.free = t
        yield
        l, free = lat.take()
        lt = M.copy(M.act, [t, free], l.ap[0:LATENT], bank.ap[0:LATENT, SEQ:2 * SEQ])
        bank.free = lt
        yield
        for which in range(2):
            for pc in range(2):
                bank, free = gen.take()
                wt = w("wqs") if which == 0 else w("upk")[0:LATENT]
                src = M.xnT[:, sl] if which == 0 else l.ap[0:LATENT]
                t = M.mm([free, lt], [(bank.ap[:, i * SEQ:(i + 1) * SEQ], [(wt[:, (2 * pc + i) * P:(2 * pc + i + 1) * P], src)])
                                      for i in range(2)])
                yield
                t = M.copy(M.act, [t, kfree], slot.ap[:, which, 2 * pc:2 * pc + 2, :], bank.ap.rearrange("p (c n) -> p c n", c=2))
                bank.free = t
                outs.append(t)
        bank, free = gen.take()
        v, vfree = vs.take()
        t = M.mm([free], [(bank.ap[:, i * P:i * P + P], [(l.ap[0:LATENT, i * P:i * P + P], w("upv")[0:LATENT])]) for i in range(2)])
        l.free = t
        yield
        for i in range(2):
            vt = M.copy(M.act, [t, vfree], spread_v(v.ap)[:, i], bank.ap[:, i * P:i * P + P].rearrange("p (h d) -> p h d", h=HEADS))
        bank.free = vt
        state[b] = {"q": slot.ap[:, 0], "k": slot.ap[:, 1], "v": v.ap, "ready": outs, "vready": vt, "slots": (slot, v)}

    out = project_out(M, gen, w("Wo"), wait_w, done_y)

    def finish(attn, done, t):
        yield from out(attn, done, t)

    scale = float(np.float32(1.0) / (np.sqrt(np.float32(DIM)) + np.float32(1e-8)))
    run_batches(prepare, lambda b: attention_heads8(M, "mla", rings, state, lambda h: h,
                                                    lambda half: c("decay")[:, half * SEQ:(half + 1) * SEQ], CLAMP / scale,
                                                    scale, finish, b))
    return done_y


def stage_local(M, ready, stage_end):
    nc, c = M.nc, M.c
    tt, ts, stt = nc.vector.tensor_tensor, nc.vector.tensor_scalar, nc.vector.scalar_tensor_tensor
    xT = M.xnT
    turned = M.turn(ready, M.xn, xT, Ring(M.bank))
    start = M.everything()
    for e in (M.pe, M.act, M.dve, M.pool):
        e.wait(start)
    for b in M.bank:
        b.free = []
    layer_width = M.dram["layer0"].shape[1]
    M.extra = [[M.xn.rearrange("p t d -> p (t d)"), TILES * DIM, 0], [M.y.rearrange("p t d -> p (t d)"), TILES * DIM, 0],
               [M.weights[0][:, layer_width:], M.weights[0].shape[1] - layer_width, 0]]
    rings = {"S": Ring(M.bank[0:2]), "T": Ring(M.bank[2:4]), "O": Ring(M.bank[4:5]),
             "P": M.ring(5, 2, 256), "PT": M.ring(3, 512), "D": M.ring(3, 2, P), "small": M.ring(4, 3, 16), "A": M.ring(2, 512)}
    gen = Ring(M.bank[5:8])
    for s in rings["P"].slots:
        s.free = M.pool([], nc.gpsimd.memset, s.ap, 0.0)
    shifted = M.ring(3, SEQ)
    for s in shifted.slots:
        s.free = M.pool([], nc.gpsimd.memset, s.ap, 0.0)
    rope = M.ring(2, 4, 2, LDIM)
    A, B, SQ, NRM = M.ring(5, 512), M.ring(2, 512), M.ring(2, 512), M.ring(2, 3, 32)
    QT, KT, V = M.ring(4, 8, P), M.ring(3, 8, SEQ), M.ring(5, LIN)
    XC, SQ2, XN, AG, GL = M.ring(1, SEQ), M.ring(1, SEQ), M.ring(2, SEQ), M.ring(2, 3, SEQ), M.ring(3, SEQ)
    RAW = M.ring(2, 512)
    VAR, DG = M.ring(2, 3, 2), M.ring(1, 2, P)
    res = [turned[b // 2] for b in range(BATCH)]
    tabs, tile_state = {}, {}
    HB = 8
    WAIT_STEPS, RATE = 4, 3

    def shift(b, after):
        s, free = shifted.take()
        x = xT[:, b * SEQ:(b + 1) * SEQ]
        t1 = M.dve([after, free], nc.vector.tensor_copy, s.ap[0:64], x[0:64])
        t2 = M.dve([], nc.vector.tensor_copy, s.ap[64:P, 1:], x[64:P, :-1])
        return s, [t1, t2]

    def layer_tables(l):
        if l in tabs:
            return
        w = lambda n: M.w(f"layer{l}", n)
        s, free = rope.take()
        t = [free, M.loaded[f"layer{l}"][0]]
        two = lambda ap: ap.rearrange("p (a d) -> p a d", a=2)
        out = [M.pool(t, nc.gpsimd.tensor_tensor, s.ap[:, i], two(c(tab)), w(sc).unsqueeze(1).broadcast_to([P, 2, LDIM]), ALU.mult)
               for i, (tab, sc) in enumerate((("rqc", "qs"), ("rqs", "qsr"), ("rkc", "ks"), ("rks", "ksr")))]
        tabs[l] = (s, out)

    def prepare(n):
        l, b = divmod(n, BATCH)
        layer_tables(l)
        if b == 0 and l > 0:
            pass
        w = lambda nm: M.w(f"layer{l}", nm)
        wt = M.loaded[f"layer{l}"][0]
        tab, tab_t = tabs[l]
        xs, xst = shift(b, res[b])
        last = []
        for i in range(2):
            st = {}
            nr, nfree = NRM.take()
            lens, inv, room = nr.ap[:, 0, :], nr.ap[:, 1, :], nr.ap[:, 2, :]
            heads = lambda ap: ap.rearrange("p (h d) -> p h d", d=LDIM)
            bc = lambda ap, k: ap.unsqueeze(1).broadcast_to([P, HB, k])
            hd = LDIM // 2
            parts = []
            for part in range(4):
                which = part // 2
                bank, free = gen.take()
                at = part * 512
                t = M.mm([free, xst, wt], [(bank.ap, [(xs.ap[:, i * P:i * P + P], w("wqkv")[:, at:at + 512])])])
                last.append(t)
                yield
                raw, free = RAW.take()
                t = M.copy(M.act, [t, free], raw.ap, bank.ap)
                bank.free = t
                sq, free = SQ.take()
                t0 = M.act([t, free], nc.scalar.activation, sq.ap, raw.ap, ACT.Square)
                yield
                src = heads(raw.ap)
                ct, st_ = tab.ap[:, 2 * which, i, :], tab.ap[:, 2 * which + 1, i, :]
                a, free = A.take()
                t1 = M.dve([t, free, tab_t], tt, heads(a.ap), src, bc(ct, LDIM), ALU.mult)
                r, free = B.take()
                t2 = M.dve([free], tt, heads(r.ap)[:, :, 0:hd], src[:, :, hd:], bc(st_[:, 0:hd], hd), ALU.mult)
                t3 = M.dve([], tt, heads(r.ap)[:, :, hd:], src[:, :, 0:hd], bc(st_[:, hd:], hd), ALU.mult)
                raw.free = [t0, t3]
                t1 = M.pool([t1, t2, t3], nc.gpsimd.tensor_tensor, a.ap, a.ap, r.ap, ALU.add)
                r.free = t1
                t4 = M.dve([t0, nfree], nc.vector.tensor_reduce, lens[:, 8 * part:8 * part + 8], heads(sq.ap), AX, ALU.add)
                sq.free = t4
                parts.append((a, t1, t4))
            t4 = M.dve([p[2] for p in parts], ts, lens, lens, 1e-24, None, ALU.max)
            t4 = M.rsqrt(t4, lens, inv, room)
            for part, (a, t1, _) in enumerate(parts):
                t1 = M.pool([t4, t1], nc.gpsimd.tensor_tensor, heads(a.ap), heads(a.ap),
                            inv[:, 8 * part:8 * part + 8].unsqueeze(2).broadcast_to([P, HB, LDIM]), ALU.mult)
                parts[part] = (a, t1)
            nr.free = t1
            yield
            v, vfree = V.take()
            outs = []
            for hf in range(2):
                bank, free = gen.take()
                at = 2 * LIN + hf * 512
                t = M.mm([free], [(bank.ap, [(xs.ap[:, i * P:i * P + P], w("wqkv")[:, at:at + 512])])])
                last.append(t)
                yield
                t = M.copy(M.act, [t, vfree], v.ap[:, hf * 512:hf * 512 + 512], bank.ap)
                bank.free = t
                outs.append(t)
            st["v"] = (v, outs)
            tile_state[n, i] = st
            for _ in range(WAIT_STEPS):
                yield
            for part, (a, t1) in enumerate(parts):
                if part == 0:
                    dst, dfree = QT.take()
                if part == 2 and i == 0:
                    keys, kfree = KT.take()
                if part == 2:
                    dst, dfree = keys, kfree
                if part % 2 == 0:
                    outs = []
                bank, free = gen.take()
                t = M.transposes([t1, free], [(bank.ap[:, j:j + P], a.ap[:, j:j + P]) for j in range(0, 512, P)])
                a.free = t
                yield
                hf = part % 2
                place = dst.ap[:, 4 * hf:4 * hf + 4, :] if part < 2 else dst.ap[:, 4 * hf:4 * hf + 4, i * P:(i + 1) * P]
                t = M.copy(M.act, [t, dfree], place, bank.ap.rearrange("p (k n) -> p k n", k=4))
                bank.free = t
                outs.append(t)
                st[part // 2] = (dst, outs)
        xs.free = last
        tab.free = last

    adds = {}

    def pairs(n):
        l, b = divmod(n, BATCH)
        w = lambda nm: M.w(f"layer{l}", nm)
        for i in range(2):
            st = tile_state[n, i]
            prev = tile_state[n, 0] if i else None
            segments = [(P - LWIN, LWIN + P)] if i else [(P, P)]
            of = lambda col, st=st, prev=prev: st if col >= P else prev

            def finish(attn, done, g, i=i, st=st, n=n, b=b, w=w):
                bank, free = gen.take()
                t = M.mm([free, done], [(bank.ap[:, 0:P], [(w("wo")[:, (4 * g + k) * DIM:(4 * g + k + 1) * DIM],
                                                            attn.ap[:, k * P:k * P + P]) for k in range(4)])])
                attn.free = t
                yield
                x = xT[:, b * SEQ + i * P:b * SEQ + (i + 1) * P]
                t = M.dve([t, adds.get((n, i))], tt, x, bank.ap[:, 0:P], x, ALU.add)
                bank.free = t
                adds[n, i] = t

            def scored(token, i=i, n=n, st=st):
                st[0][0].free = token
                if i == 1:
                    st[1][0].free = token

            def valued(token, i=i, n=n, st=st):
                if i == 1:
                    for x in (tile_state[n, 0], st):
                        x["v"][0].free = token

            tile = {"order": [(h, h + 2) for h in range(LHEADS) if h % 4 < 2], "scored": scored, "valued": valued, "ready": [st[0][1], st[1][1]] + ([prev[1][1]] if prev else []),
                    "vready": [st["v"][1]] + ([prev["v"][1]] if prev else []), "segments": segments, "mask": c("band"),
                    "q": lambda h, st=st: st[0][0].ap[64 * (h % 2):64 * (h % 2) + 64, h // 2, :],
                    "k": lambda h, sg, st=st, i=i: st[1][0].ap[64 * (h % 2):64 * (h % 2) + 64, h // 2,
                                                               sg[0] - P + i * P:sg[0] - P + i * P + sg[1]],
                    "v": lambda h, blk, of=of: of(blk * P)["v"][0].ap[:, LDIM * h:LDIM * h + LDIM]}
            yield from M.attend(rings, LHEADS, LDIM, 8.0, tile, finish)

    def feed(n):
        l, b = divmod(n, BATCH)
        w = lambda nm: M.w(f"layer{l}", nm)
        xs, t = shift(b, [adds[n, 0], adds[n, 1]])
        bank, free = gen.take()
        t = M.mm([free, t], [(bank.ap[:, 0:SEQ], [(c("center"), xs.ap)])])
        xs.free = t
        yield
        xc, free = XC.take()
        t1 = M.copy(M.act, [t, free], xc.ap, bank.ap[:, 0:SEQ])
        sq, free = SQ2.take()
        t2 = M.act([free], nc.scalar.activation, sq.ap, bank.ap[:, 0:SEQ], ACT.Square)
        yield
        t = M.mm([t1, t2], [(bank.ap[:, SEQ + i:SEQ + i + 1], [(sq.ap[:, i * P:i * P + P], c("mean")[:, 0:1])]) for i in range(2)])
        sq.free = t
        yield
        v, free = VAR.take()
        t = M.dve([t, free], ts, v.ap[:, 0, :], bank.ap[:, SEQ:SEQ + 2], EPS, None, ALU.add)
        t = M.rsqrt(t, v.ap[:, 0, :], v.ap[:, 1, :], v.ap[:, 2, :])
        dg, free = DG.take()
        for i in range(2):
            t = M.dve([t, free], ts, dg.ap[:, i, :], c("ident"), v.ap[:, 1, i:i + 1], None, ALU.mult)
        v.free = t
        yield
        t = M.mm(t, [(bank.ap[:, SEQ + i * P:SEQ + (i + 1) * P], [(c("ones"), dg.ap[:, i, :])]) for i in range(2)])
        dg.free = t
        yield
        xn, free = XN.take()
        t = M.dve([t, free, t1], tt, xn.ap, xc.ap, bank.ap[:, SEQ:], ALU.mult)
        xc.free = t
        bank.free = t
        t = M.dve(t, ts, xn.ap, xn.ap, w("lng"), w("lnb"), ALU.mult, ALU.add)
        ag, afree = AG.take()
        ready = []
        yield
        gated = []
        for j, (at, m) in enumerate(GLU_PARTS):
            bank, free = gen.take()
            t1 = M.mm([t, free], [(bank.ap[0:m, 0:SEQ], [(w("w1")[:, at:at + m], xn.ap)]),
                                  (bank.ap[0:m, SEQ:], [(w("w1")[:, GLU + at:GLU + at + m], xn.ap)])])
            gl, free = GL.take()
            t2 = M.act([t1, free], nc.scalar.activation, gl.ap[0:m], bank.ap[0:m, SEQ:], ACT.Gelu, bias=w("b1")[0:m, 3 + j:4 + j])
            gated.append((bank, gl, t2))
        yield
        for j, (at, m) in enumerate(GLU_PARTS):
            bank, gl, t2 = gated[j]
            t2 = M.dve([t2, afree], stt, ag.ap[0:m, j, :], bank.ap[0:m, 0:SEQ], w("b1")[0:m, j:j + 1], gl.ap[0:m], ALU.add, ALU.mult)
            bank.free = t2
            gl.free = t2
            ready.append(t2)
        xn.free = t1
        yield
        bank, free = gen.take()
        t = M.mm([free, ready], [(bank.ap[:, 0:SEQ], [(w("w2")[0:m, j * DIM:(j + 1) * DIM], ag.ap[0:m, j, :])
                                                      for j, (at, m) in enumerate(GLU_PARTS)])])
        ag.free = t
        yield
        x = xT[:, b * SEQ:(b + 1) * SEQ]
        t = M.dve(t, stt, x, bank.ap[:, 0:SEQ], w("b2"), x, ALU.add, ALU.add)
        bank.free = t
        res[b] = t
        layer_end[l] = t

    layer_end = {}
    steps = DEPTH * BATCH
    for _ in prepare(0):
        pass

    following = [iter(())]

    def units():
        for n in range(steps):
            nxt = following[0] = prepare(n + 1) if n + 1 < steps else iter(())
            for k, p in enumerate(pairs(n)):
                yield p
                if k == 14 and n:
                    yield feed(n - 1)
                    l, b = divmod(n - 1, BATCH)
                if k == 15 and n and n % BATCH == 4 and n // BATCH + 1 < DEPTH and n >= BATCH:
                    M.load(f"layer{n // BATCH + 1}", (n // BATCH + 1) % 2, layer_end[n // BATCH - 1])
            for _ in nxt:
                pass
        for _ in range(16):
            yield iter(())
        yield feed(steps - 1)

    pipeline(units(), lambda: next(following[0], None), RATE)
    end = M.everything()
    for b in M.bank:
        b.free = end
    banks = Ring(M.bank)
    done = []
    for g in range(GROUPS):
        b, free = banks.take()
        t = M.transposes([free], [(b.ap[:, P * k:P * k + P], xT[:, GROUP * g + P * k:GROUP * g + P * k + P]) for k in range(4)])
        t = M.copy(M.act, t, M.y[:, 4 * g:4 * g + 4, :], b.ap.rearrange("p (k n) -> p k n", k=4))
        b.free = t
        done += [t] * 4
    M.extra = []
    return done


STAGES = [("titan", 1, stage_titan), ("split", 0, stage_split), ("linear", 1, stage_linear), ("moe1", 0, stage_moe1),
          ("mamba", 1, stage_mamba), ("gqa", 0, stage_gqa), ("mla", 1, stage_mla), ("layer0", 0, stage_local)]
FIRST, LAST = 0, 8


def build(nc, dram, places, x_in, x_out):
    with ExitStack() as ctx:
        width = lambda n: dram[n].shape[1]
        sizes = {"table": width("table"), "w0": max(width(n) for n in ("split", "moe1", "gqa", "layer0")),
                 "w1": max(width(n) for n in ("titan", "linear", "mamba", "mla", "layer1"))}
        fixed = 4 * TILES * DIM + 512 + sizes["table"] + sizes["w0"] + sizes["w1"]
        sizes["scratch"] = min(22400, 212000 // 4 - fixed)
        M = Machine(nc, ctx, dram, places, sizes)
        tokens = "(t p) d -> p t d"
        src, dst = (a.rearrange("b s d -> (b s) d").rearrange(tokens, p=P) for a in (x_in, x_out))
        x_sem, out_sem = M.sem("x_loaded"), M.sem("out_stored")
        nc.sync.dma_start(M.x, src).then_inc(x_sem, 16)
        stages = STAGES[FIRST:LAST]
        M.load("table", None)
        for name, region, _ in stages[:2]:
            M.load(name, region)
        if len(stages) == 1 and stages[0][0] == "layer0":
            M.load("layer1", 1)
        M.extra = []
        x_ready, ends = [(x_sem, 16)], [[]]
        for e in (M.pe, M.act, M.dve, M.pool):
            e.wait(M.loaded["table"][0])
        for i, (name, _, stage) in enumerate(stages):
            if i >= 1 and i + 1 < len(stages):
                M.load(stages[i + 1][0], stages[i + 1][1], M.everything())
            if i >= 1 and i == len(stages) - 1 and name == "layer0":
                M.load("layer1", 1, M.everything())
            M.begin(M.everything())
            ready = M.normalise(x_ready, M.x, M.xn)
            done = stage(M, ready, None) if stage is stage_local else stage(M, ready)
            t = M.normalise([done, M.everything()], M.y, M.y)
            x_ready = [M.pool([t, x_ready], nc.gpsimd.tensor_tensor, M.x[:, 4 * g:4 * g + 4, :], M.x[:, 4 * g:4 * g + 4, :],
                              M.y[:, 4 * g:4 * g + 4, :], ALU.add) for g in range(GROUPS)]
        M.sp.wait(x_ready)
        nc.sync.dma_start(dst, M.x).then_inc(out_sem, 16)
        nc.sync.wait_ge(out_sem, 16)


def kernel(**inputs):
    from concourse import bacc
    from concourse.bass_utils import run_bass_kernel_spmd

    nc = bacc.Bacc("TRN2", target_bir_lowering=False, num_devices=1)
    arrays, dram, places = {}, {}, {}
    packs = {"table": tables(), **layout(inputs)}
    for name, parts in packs.items():
        arrays[name + "_dram"], places[name] = pack(parts)
        dram[name] = nc.dram_tensor(name + "_dram", arrays[name + "_dram"].shape, F32, kind="ExternalInput").ap()
    arrays["x_dram"] = np.ascontiguousarray(inputs["L0_attn_x"])
    x_in = nc.dram_tensor("x_dram", (BATCH, SEQ, DIM), F32, kind="ExternalInput").ap()
    x_out = nc.dram_tensor("out_dram", (BATCH, SEQ, DIM), F32, kind="ExternalOutput").ap()
    build(nc, dram, places, x_in, x_out)
    r = run_bass_kernel_spmd(nc, [arrays], core_ids=[0])
    return r.results[0]["out_dram"]
```

```python
from contextlib import ExitStack

import numpy as np

import concourse.bass as bass
from concourse import mybir

P = 128
F32 = mybir.dt.float32
U32 = mybir.dt.uint32
BF16 = mybir.dt.bfloat16
I32 = mybir.dt.int32
ALU = mybir.AluOpType
ACT = mybir.ActivationFunctionType
AX = mybir.AxisListType.X

BATCH, SEQ, DIM = 8, 256, 128
TOKENS = BATCH * SEQ
TILES = TOKENS // P
GROUP = 512
GROUPS = TOKENS // GROUP
NEG = -1.0e30
EPS = 1e-5
MAGIC = 0x5F3759DF

HID0, HEADS0, WIN0, MEM0 = 512, 4, 64, 64
HEADS, HDIM = 16, 8
CHUNKS = HEADS // 4
REG = 5
EXP1, EXP2, FF = 16, 8, 256
INNER, STATE, CONV = 256, 16, 3
LATENT = 32
CLAMP = 10000.0
DEPTH, LHEADS, LDIM, LWIN = 6, 16, 64, 32
LIN = LHEADS * LDIM
GLU = int(DIM * 4 * 2 / 3)
GLU_PARTS = [(0, 128), (128, 128), (256, GLU - 256)]



def rows(v):
    v = np.asarray(v).reshape(1, -1)
    return np.broadcast_to(v, (P, v.shape[1]))


def cols(v):
    return np.asarray(v).reshape(-1, P).T


def chunks(w):
    w = np.asarray(w)
    return w.reshape(-1, P, w.shape[1]).transpose(1, 0, 2).reshape(P, -1)


def spread_heads(w, head_of=None):
    w = np.asarray(w)
    out = np.zeros((w.shape[0], CHUNKS, 4, 32), np.float32)
    for c in range(CHUNKS):
        for g in range(4):
            h = 4 * c + g if head_of is None else head_of(4 * c + g)
            out[:, c, g, :HDIM] = w[:, h * HDIM:(h + 1) * HDIM]
    return out.reshape(w.shape[0], CHUNKS * P)


def spread_rows(w):
    return chunks(spread_heads(np.asarray(w).T).T)


def tall(a):
    a = np.asarray(a)
    out = np.zeros((P, a.shape[1]), np.float32)
    out[:a.shape[0]] = a
    return out


def rotate_columns(w, half):
    w = np.asarray(w)
    k, n = w.shape
    return w.reshape(k, n // (2 * half), 2, half)[:, :, ::-1, :].reshape(k, n)


def pack(parts):
    place, at = {}, 0
    for name, a in parts:
        place[name] = (at, a.shape[1])
        at += a.shape[1]
    return np.ascontiguousarray(np.concatenate([a for _, a in parts], axis=1)), place


def expert_weights(up, gate, down):
    return [piece for e in range(up.shape[0])
            for piece in ((f"gate{e}", np.asarray(gate[e])), (f"up{e}", np.asarray(up[e])),
                          (f"down{e}", chunks(down[e])))]


def layout(i):
    a = {k: np.asarray(v) for k, v in i.items()}
    T = np.transpose
    out = {}
    mem = np.zeros((P, DIM), np.float32)
    mem[P - MEM0:] = a["L0_attn_mem"]
    out["titan"] = [(n, T(a["L0_attn_" + n])) for n in ("wq", "wk", "wv", "wo", "lin1", "lin2", "w1")] + [
        ("w2", a["L0_attn_w2"]), ("w2T", chunks(T(a["L0_attn_w2"]))), ("b1", rows(a["L0_attn_b1"])),
        ("b2", rows(a["L0_attn_b2"])), ("b2col", cols(a["L0_attn_b2"])), ("mem", mem), ("memT", T(mem)),
        ("alpha", rows(a["L0_attn_alpha"])), ("theta", rows(a["L0_attn_theta"]))]
    w = a["L0_ffn_W_qkv"]
    out["split"] = [("wq", w[:, :DIM]), ("wqs", spread_heads(w[:, :DIM])), ("wks", spread_heads(w[:, DIM:2 * DIM])),
                    ("wv", w[:, 2 * DIM:]), ("wo", spread_rows(a["L0_ffn_W_proj"])), ("bo", rows(a["L0_ffn_b_proj"])),
                    ("g", rows(a["L0_ffn_g_info"][0, 0]))]
    out["linear"] = [(n, T(a["L1_attn_" + n])) for n in ("Wq", "Wk", "Wv", "Wo")] + [
        ("bq", cols(a["L1_attn_bq"]))] + [(n, rows(a["L1_attn_" + n])) for n in ("bk", "bv", "bo", "stdp")]
    out["moe1"] = [("router", T(a["L1_ffn_router_w"])), ("rb", rows(a["L1_ffn_router_b"])),
                   ("lng", rows(a["L1_ffn_ln_g"])), ("lnb", tall(a["L1_ffn_ln_b"]))] + expert_weights(
        T(a["L1_ffn_w3"], (0, 2, 1)), T(a["L1_ffn_w1"], (0, 2, 1)), T(a["L1_ffn_w2"], (0, 2, 1)))
    m = "L2_attn_"
    out["mamba"] = [("in", a[m + "in_proj_w"]), ("conv", chunks(a[m + "conv_w"][:, 0, :])),
                    ("convb", cols(a[m + "conv_b"])), ("xp", chunks(a[m + "x_proj_w"])),
                    ("dt", chunks(a[m + "dt_proj_w"])), ("dtb", cols(a[m + "dt_proj_b"])),
                    ("out", chunks(a[m + "out_proj_w"])), ("alog", chunks(a[m + "A_log"])),
                    ("dp", cols(a[m + "D_param"]))]
    m = "L2_ffn_"
    q, k = a[m + "Wq"], a[m + "Wk"]
    kv = lambda h: h // 4
    out["gqa"] = [("ln1", cols(a[m + "ln1_w"])), ("ln2", cols(a[m + "ln2_w"])),
                  ("wqs", spread_heads(q)), ("wqr", spread_heads(rotate_columns(q, 4))),
                  ("wks", spread_heads(k, kv)), ("wkr", spread_heads(rotate_columns(k, 4), kv)),
                  ("wv", a[m + "Wv"]), ("wo", spread_rows(a[m + "Wo"])), ("wr", a[m + "Wr"])] + expert_weights(
        a[m + "Wu"], a[m + "Wg"], a[m + "Wd"])
    m = "L3_attn_"
    out["mla"] = [(n, a[m + n]) for n in ("Wk", "Wv")] + [("Wo", spread_rows(a[m + "Wo"])),
        ("wqs", spread_heads(a[m + "Wq"])), ("down", a[m + "W_down_kv"]),
        ("upk", tall(spread_heads(a[m + "W_up_k"]))), ("upv", tall(a[m + "W_up_v"]))]
    m = "L3_ffn_"
    for l in range(DEPTH):
        qs, ks = a[m + "q_scale"][l], a[m + "k_scale"][l]
        w1, b1 = a[m + "W1"][l], a[m + "b1"][l]
        bias = np.zeros((2, 3 * P), np.float32)
        bias[0, :GLU], bias[1, :GLU] = b1[:GLU], b1[GLU:]
        w2 = np.zeros((3 * P, DIM), np.float32)
        w2[:GLU] = a[m + "W2"][l]
        out[f"layer{l}"] = [("wqkv", a[m + "Wqkv"][l]), ("wo", chunks(a[m + "Wo"][l])), ("w1", w1),
                            ("w2", chunks(w2)), ("b1", cols(bias)), ("b2", cols(a[m + "b2"][l])),
                            ("lng", cols(a[m + "ln_g"][l])), ("lnb", cols(a[m + "ln_b"][l])),
                            ("qs", rows(qs)), ("qsr", rotate_columns(rows(qs), LDIM // 2)),
                            ("ks", rows(ks)), ("ksr", rotate_columns(rows(ks), LDIM // 2))]
    return out


def tables():
    f = np.float32
    q = np.arange(P)[:, None]
    key = np.arange(2 * P)[None, :] - P
    out = [("ident", np.eye(P, dtype=f)), ("ones", np.ones((P, P), f)),
           ("center", (np.eye(P) - 1.0 / DIM).astype(f)), ("mean", np.full((P, P), 1.0 / DIM, f)),
           ("half", np.full((P, 64), -0.5, f))]
    out += [("magic", np.full((P, 1), MAGIC + 1, np.uint32).view(f))]
    window = np.where((key <= q) & (key > q - WIN0), 0, NEG).astype(f)
    out += [("window", window), ("windowmem", np.where((key < P - MEM0) & (q >= P - MEM0), NEG, window).astype(f)),
            ("causal", np.where(key <= q, 0, NEG).astype(f)),
            ("band", np.where((key <= q) & (key >= q - LWIN), 0, NEG).astype(f))]
    reg = np.zeros((P, TILES), f)
    reg[:REG, ::2] = 1
    turn = np.zeros((P, 1), f)
    for g in range(4):
        turn[32 * g + HDIM], turn[32 * g + HDIM + 1] = -1, 1
    block = np.zeros((P, HEADS, 32), f)
    pick = np.zeros((P, REG), f)
    for h in range(HEADS):
        block[h * REG:(h + 1) * REG, h, :HDIM] = 1
        for r in range(REG):
            pick[h * REG + r, r] = 0.5
    block = block.reshape(P, -1)
    out += [("reg", reg), ("turn", turn), ("block", block), ("pick", pick)]
    ch = np.arange(P)[:, None]
    out += [("blockdiag", (ch // HDIM == np.arange(DIM)[None, :] // HDIM).astype(f)),
            ("blockhead", (ch // HDIM == np.arange(HEADS)[None, :]).astype(f)),
            ("iota", np.broadcast_to(np.arange(16, dtype=f), (P, 16)))]
    inv = (f(1.0) / f(10000.0) ** (np.arange(0, HDIM, 2, dtype=f) / f(HDIM))).astype(f)
    fr = np.arange(SEQ, dtype=f)[:, None] * inv
    cos, sin = np.cos(fr).astype(f).T, np.sin(fr).astype(f).T
    ct, st = np.zeros((P, SEQ), f), np.zeros((P, SEQ), f)
    for g in range(4):
        ct[32 * g:32 * g + 4], ct[32 * g + 4:32 * g + 8] = cos, cos
        st[32 * g:32 * g + 4], st[32 * g + 4:32 * g + 8] = -sin, sin
    out += [("cosT", ct), ("sinT", st)]
    pos = np.arange(SEQ, dtype=f)
    decay = np.exp(f(-0.01 * 0.01) * np.abs(pos[:, None] - pos[None, :])).astype(f)
    out += [("decay", chunks(decay))]
    half = np.arange(0, LDIM, 2, dtype=f)
    inv = (f(1.0) / f(10000.0) ** (half / f(LDIM))).astype(f)
    t = np.arange(SEQ, dtype=f)
    fr = t[:, None] * inv[None, :]
    fr = np.concatenate([fr, fr], -1)
    base = ((half + f(0.4 * LDIM)) / f(1.4 * LDIM)).astype(f)
    sc = base[None, :] ** ((t - SEQ // 2) / f(LWIN // 2))[:, None]
    sc = np.concatenate([sc, sc], -1).astype(f)
    sign = np.concatenate([-np.ones(LDIM // 2, f), np.ones(LDIM // 2, f)])
    c, s = np.cos(fr).astype(f), np.sin(fr).astype(f)
    inv = f(1.0) / sc
    out += [("rqc", chunks(c * sc)), ("rqs", chunks(s * sc * sign)), ("rkc", chunks(c * inv)),
            ("rks", chunks(s * inv * sign))]
    return [(n, a.astype(f)) for n, a in out]



class Engine:

    def __init__(self, engine, sem):
        self.engine, self.sem, self.count, self.waited = engine, sem, 0, {}

    def wait(self, after):
        need = {}
        for sem, value in flat(after):
            need[sem.name] = (sem, max(value, need.get(sem.name, (sem, 0))[1]))
        for name, (sem, value) in need.items():
            if value > self.waited.get(name, 0):
                self.engine.wait_ge(sem, value)
                self.waited[name] = value

    def __call__(self, after, issue, *args, **kw):
        self.wait(after)
        return self.mark(issue(*args, **kw))

    def mark(self, instruction):
        instruction.then_inc(self.sem, 1)
        self.count += 1
        return [(self.sem, self.count)]


def flat(tokens):
    out = []
    for t in tokens:
        if isinstance(t, list):
            out += flat(t)
        elif t is not None:
            out.append(t)
    return out


class Slot:

    def __init__(self, ap, free=()):
        self.ap, self.free = ap, list(free)


class Ring:
    def __init__(self, slots):
        self.slots, self.at = slots, 0

    def take(self):
        for _ in self.slots:
            slot = self.slots[self.at % len(self.slots)]
            self.at += 1
            if slot.free is not None:
                break
        assert slot.free is not None, "taken before its release was written down"
        free, slot.free = slot.free, None
        return slot, free

    def get(self):
        while all(slot.free is None for slot in self.slots):
            yield
        return self.take()


def pipeline(units, beside=None, rate=0):
    running, units = [], iter(units)
    more = True
    while more or running:
        nxt = next(units, None) if more else None
        if nxt is None:
            more = False
        else:
            running.append(nxt)
        left, n = [], len(running)
        for i, u in enumerate(running):
            if next(u, "end") != "end":
                left.append(u)
            for _ in range((i + 1) * rate // n - i * rate // n):
                beside()
        running = left


class Machine:
    def __init__(self, nc, ctx, dram, places, sizes):
        self.nc, self.ctx, self.dram, self.places = nc, ctx, dram, places
        sem = lambda n: ctx.enter_context(nc.semaphore(n))
        self.sem = sem
        self.pe = Engine(nc.tensor, sem("pe_done"))
        self.act = Engine(nc.scalar, sem("act_done"))
        self.dve = Engine(nc.vector, sem("dve_done"))
        self.pool = Engine(nc.gpsimd, sem("pool_done"))
        self.sp = Engine(nc.sync, sem("sp_done"))
        sb = lambda n, s: ctx.enter_context(nc.sbuf_tensor(n, s, F32))[:]
        self.x = sb("x", [P, TILES, DIM])
        self.xn = sb("xn", [P, TILES, DIM])
        self.xnT = sb("xnT", [P, TOKENS])
        self.y = sb("y", [P, TILES, DIM])
        self.table = sb("table", [P, sizes["table"]])
        self.weights = [sb("weights0", [P, sizes["w0"]]), sb("weights1", [P, sizes["w1"]])]
        self.scratch = sb("scratch", [P, sizes["scratch"]])
        self.scratch_size = sizes["scratch"]
        self.stats = sb("stats", [P, 512])
        self.psum = ctx.enter_context(nc.psum_tensor("psum", [P, 8, 512], F32))[:]
        self.bank = [Slot(self.psum[:, i, :]) for i in range(8)]
        self.loaded = {}
        self.used = 0

    def c(self, name, n=None):
        at, width = self.places["table"][name]
        return self.table[:, at:at + (n or width)]

    def load(self, name, region, after=()):
        n = self.dram[name].shape[1]
        buf = self.table if region is None else self.weights[region]
        sem = self.sem("loaded_" + name)
        self.sp.wait(after)
        half = (n // 2) if n > 2048 else n
        k = 0
        for a, b in ((0, half), (half, n)):
            if b > a:
                self.nc.sync.dma_start(buf[:, a:b], self.dram[name][:, a:b]).then_inc(sem, 16)
                k += 1
        self.loaded[name] = ([(sem, 16 * k)], buf)

    def w(self, stage, name):
        at, n = self.places[stage][name]
        return self.loaded[stage][1][:, at:at + n]

    def everything(self):
        return [(e.sem, e.count) for e in (self.pe, self.act, self.dve, self.pool) if e.count]

    def begin(self, after_all):
        self.used, self.extra = 0, []
        for e in (self.pe, self.act, self.dve, self.pool):
            e.wait(after_all)
        for b in self.bank:
            b.free = []

    def alloc(self, *shape):
        n = int(np.prod(shape))
        if self.used + n <= self.scratch_size:
            ap = self.scratch[:, self.used:self.used + n]
            self.used += n
        else:
            place = next(e for e in self.extra if e[2] + n <= e[1])
            ap = place[0][:, place[2]:place[2] + n]
            place[2] += n
        if len(shape) == 2:
            ap = ap.rearrange("p (a b) -> p a b", a=shape[0])
        if len(shape) == 3:
            ap = ap.rearrange("p (a b c) -> p a b c", a=shape[0], b=shape[1])
        return ap

    def ring(self, n, *shape):
        return Ring([Slot(self.alloc(*shape)) for _ in range(n)])

    def mm(self, after, groups):
        self.pe.wait(after)
        last = None
        for out, pairs in groups:
            for i, (a, b) in enumerate(pairs):
                last = self.nc.tensor.matmul(out, a, b, start=(i == 0), stop=(i == len(pairs) - 1))
        return self.pe.mark(last)

    def transposes(self, after, pairs):
        self.pe.wait(after)
        last = None
        for out, src in pairs:
            k = src.shape[0]
            last = self.nc.tensor.transpose(out, src, self.c("ident")[0:k, 0:k])
        return self.pe.mark(last)

    def copy(self, eng, after, out, src):
        if eng is self.act:
            return eng(after, self.nc.scalar.copy, out, src)
        e = self.nc.vector if eng is self.dve else self.nc.gpsimd
        return eng(after, e.tensor_copy, out, src)

    def rsqrt(self, after, x, y, t):
        nc, dve = self.nc, self.dve
        n = x.shape[1]
        k = dve(after, nc.vector.tensor_scalar, y.bitcast(U32), x.bitcast(U32), 1, 0xFFFFFFFF,
                ALU.logical_shift_right, ALU.bitwise_xor)
        k = dve(k, nc.vector.tensor_tensor, y.bitcast(I32), y.bitcast(I32),
                self.c("magic").bitcast(I32).broadcast_to([P, n]), ALU.add)
        for _ in range(3):
            k = dve(k, nc.vector.tensor_tensor, t, x, y, ALU.mult)
            k = dve(k, nc.vector.scalar_tensor_tensor, t, t, -0.5, y, ALU.mult, ALU.mult)
            k = dve(k, nc.vector.scalar_tensor_tensor, y, t, 1.5, y, ALU.add, ALU.mult)
        return k

    def moments(self, after, tiles, n, at):
        nc, dve = self.nc, self.dve
        st = self.stats[:, at:at + 6 * n].rearrange("p (t s) -> p t s", s=6)
        r = self.stats[:, at + 6 * n:at + 12 * n].rearrange("p (k t) -> p k t", k=6)
        t = None
        for i, tile in enumerate(tiles):
            t = dve(after, nc.vector.bn_stats, st[:, i, :], tile)
        tt = nc.vector.tensor_tensor
        s = dve(t, tt, r[:, 0, :], st[:, :, 1], st[:, :, 4], ALU.add)
        d = dve([], tt, r[:, 1, :], st[:, :, 1], st[:, :, 4], ALU.subtract)
        v = dve([], tt, r[:, 2, :], st[:, :, 2], st[:, :, 5], ALU.add)
        mean = dve(s, nc.vector.tensor_scalar, r[:, 0, :], r[:, 0, :], 0.5, None, ALU.mult)
        d = dve(d, tt, r[:, 3, :], r[:, 1, :], r[:, 1, :], ALU.mult)
        v = dve(v, nc.vector.tensor_scalar, r[:, 2, :], r[:, 2, :], 1.0 / DIM, EPS, ALU.mult, ALU.add)
        v = dve([v, d], nc.vector.scalar_tensor_tensor, r[:, 4, :], r[:, 3, :], 0.25, r[:, 2, :], ALU.mult, ALU.add)
        if n == TILES:
            rstd = self.rsqrt(v, r[:, 4, :], r[:, 5, :], r[:, 3, :])
        else:
            rstd = self.pool(v, nc.gpsimd.tensor_tensor, r[:, 5, :], r[:, 4, :], self.c("half", n), ALU.pow)
        return r[:, 0, :], r[:, 5, :], [mean, rstd]

    def normalise(self, after, src, out, at=0):
        mean, rstd, ready = self.moments(after, [src[:, t, :] for t in range(TILES)], TILES, at)
        return [self.dve(ready, self.nc.vector.tensor_scalar, out[:, t, :], src[:, t, :], mean[:, t:t + 1],
                         rstd[:, t:t + 1], ALU.subtract, ALU.mult) for t in range(TILES)]

    def turn(self, after, src, dst, banks, scale=None):
        done = []
        for g in range(GROUPS):
            bank, free = banks.take()
            t = self.transposes([free, [after[4 * g + k] for k in range(4)]],
                                [(bank.ap[:, P * k:P * k + P], src[:, 4 * g + k, :]) for k in range(4)])
            out = dst[:, GROUP * g:GROUP * (g + 1)]
            if scale is None:
                t = self.copy(self.act if g % 2 else self.dve, t, out, bank.ap)
            else:
                t = self.dve(t, self.nc.vector.tensor_scalar, out, bank.ap, scale, None, ALU.mult)
            bank.free = t
            done.append(t)
        return done

    def attend(self, rings, heads, dv, scale, tile_of, finish):
        nc = self.nc
        c0 = min(col for col, _ in tile_of["segments"])
        blocks = sorted({k // P for col, n in tile_of["segments"] for k in (col, col + n - 1)})
        per = min(heads, 4 * P // max(dv, 32))
        order = tile_of["order"]
        shared, passed, summed = {}, {}, {}

        def over(step, token):
            passed.setdefault(step, []).append(token)
            if len(passed[step]) == len(order):
                if step == "divided":
                    shared["small"].free = passed[step]
                else:
                    tile_of[step](passed[step])

        def pair(n, hs):
            cols = slice(hs[0], hs[1] + 1, hs[1] - hs[0])
            if n == 0:
                shared["small"], shared["free"] = yield from rings["small"].get()
            while "small" not in shared:
                yield
            small = shared["small"].ap
            bank, free = yield from rings["S"].get()
            s = bank.ap.rearrange("p (h k) -> p h k", h=2)
            scored = [free, tile_of["ready"]]
            one = [[(s[:, i, col:col + n_], [(tile_of["q"](hs[i]), tile_of["k"](hs[i], (col, n_)))])
                    for col, n_ in tile_of["segments"]] for i in range(2)]
            if tile_of.get("apart"):
                scored = self.mm(self.mm(scored, one[0]), one[1])
            else:
                scored = self.mm(scored, one[0] + one[1])
            over("scored", scored)
            yield
            probs, pfree = yield from rings["P"].get()
            p = probs.ap
            m, top, factor = small[:, 0, cols], None, scale
            if tile_of["mask"] is None:
                top = self.dve([scored, shared["free"]], nc.vector.tensor_reduce, m, s[:, :, c0:], AX, ALU.max)
                src = s
            elif tile_of.get("clip"):
                lim = tile_of["clip"]
                t = self.dve([scored, pfree, shared["free"]], nc.vector.tensor_scalar, p, s, lim, -lim, ALU.min, ALU.max)
                bank.free = t
                for i in range(2):
                    top = self.dve(t, nc.vector.tensor_tensor_reduce, p[:, i, :], p[:, i, :], tile_of["mask"], 1.0,
                                   -3.0e38, ALU.mult, ALU.max, small[:, 0, hs[i]:hs[i] + 1])
                src = p
            else:
                for i in range(2):
                    bias = self.dve([scored, pfree, shared["free"]], nc.vector.tensor_tensor_reduce, p[:, i, c0:],
                                    s[:, i, c0:], tile_of["mask"][:, c0:], -scale, 3.0e38, ALU.add, ALU.min,
                                    small[:, 1, hs[i]:hs[i] + 1])
                bank.free = bias
                src, factor = p, -1.0
            if top is not None:
                bias = self.dve(top, nc.vector.tensor_scalar, small[:, 1, cols], m, -scale, None, ALU.mult)
            yield
            for i in range(2):
                h = hs[i]
                e = self.act([bias, pfree], nc.scalar.activation, p[:, i, c0:], src[:, i, c0:], ACT.Exp,
                             bias=small[:, 1, h:h + 1], scale=factor, accum_out=small[:, 2, h:h + 1])
            if tile_of["mask"] is None:
                bank.free = e
            yield
            r = self.dve(e, nc.vector.reciprocal, small[:, 0, cols], small[:, 2, cols])
            if n % 8 in rings["on_pool"]:
                divider, issue = self.pool, nc.gpsimd.tensor_tensor
            else:
                divider, issue = self.dve, nc.vector.tensor_tensor
            d = divider(r, issue, p[:, :, c0:], p[:, :, c0:],
                   small[:, 0, cols].unsqueeze(2).broadcast_to([P, 2, 2 * P - c0]), ALU.mult)
            over("divided", d)
            yield
            bank, free = yield from rings["T"].get()
            tp = bank.ap.rearrange("p (h b k) -> p h b k", h=2, b=2)
            turned = self.transposes([free, d], [(tp[:, i, b, :], p[:, i, P * b:P * b + P])
                                                 for i in range(2) for b in blocks])
            probs.free = turned
            yield
            pt, free = yield from rings["PT"].get()
            ptv = pt.ap.rearrange("p (h b k) -> p h b k", h=2, b=2)
            b0, b1 = blocks[0], blocks[-1] + 1
            eng = self.act if n % 8 in rings["on_act"] else self.dve
            t = self.copy(eng, [turned, free], ptv[:, :, b0:b1, :], tp[:, :, b0:b1, :])
            bank.free = t
            yield
            group = n // (per // 2)
            if n % (per // 2) == 0:
                shared["O", group], shared["ofree"] = yield from rings["O"].get()
            while ("O", group) not in shared:
                yield
            obank = shared["O", group]
            pad = max(dv, 32)
            out = lambda h: obank.ap[h * pad % P:h * pad % P + pad, h % per * pad // P * P:h % per * pad // P * P + P]
            t = self.mm([t, shared["ofree"], tile_of["vready"]],
                        [(out(h), [(tile_of["v"](h, blk), ptv[:, i, blk, :]) for blk in blocks]) for i, h in enumerate(hs)])
            pt.free = t
            over("valued", t)
            summed.setdefault(group, []).append(t)
            if len(summed[group]) == per // 2:
                t = summed[group]
                width = per * pad // P * P
                yield
                attn, free = yield from rings["A"].get()
                t = self.copy(self.act, [t, free], attn.ap[:, 0:width], obank.ap[:, 0:width])
                obank.free = t
                yield
                yield from finish(attn, t, group)

        return [pair(n, hs) for n, hs in enumerate(order)]

    def attention_rings(self, s=3, t=2, o=1, on_pool=(), on_act=(2, 5)):
        b = self.bank
        return {"S": Ring(b[0:s]), "T": Ring(b[s:s + t]), "O": Ring(b[s + t:s + t + o]),
                "P": self.ring(5, 2, 256), "PT": self.ring(3, 512), "small": self.ring(8, 3, 16), "on_pool": on_pool,
                "on_act": on_act}



def stage_titan(M, ready):
    nc, c, w = M.nc, M.c, lambda n: M.w("titan", n)
    wait_w = M.loaded["titan"][0]
    banks = Ring(M.bank)
    NT = TILES + 1
    ext = NT * P
    xT = M.alloc(ext)
    swaT = M.alloc(ext)
    turned = M.turn(ready, M.xn, xT, banks)
    mem = M.copy(M.pool, [wait_w], xT[:, TOKENS:], w("memT"))
    tile_ready = [turned[t // 4] for t in range(TILES)] + [mem]
    at = M.used
    q, k, v = M.alloc(ext), M.alloc(ext), M.alloc(NT, DIM)
    qk = {}
    spans = [(g * GROUP, GROUP) for g in range(GROUPS)] + [(TOKENS, P)]
    for i, (s, n) in enumerate(spans):
        for name, dst in (("wq", q), ("wk", k)):
            bank, free = banks.take()
            t = M.mm([free, wait_w, tile_ready[s // P]], [(bank.ap[:, 0:n], [(w(name), xT[:, s:s + n])])])
            t = M.copy(M.act if name == "wq" else M.dve, t, dst[:, s:s + n], bank.ap[:, 0:n])
            bank.free = t
            qk[name, i] = t
        bank, free = banks.take()
        t = M.mm(free, [(bank.ap[:, j:j + P], [(xT[:, s + j:s + j + P], w("wv"))]) for j in range(0, n, P)])
        t = M.copy(M.act, t, v[:, s // P:(s + n) // P, :], bank.ap[:, 0:n].rearrange("p (t d) -> p t d", d=DIM))
        bank.free = t
        qk["v", i] = t
    of = lambda t: [qk["wq", t // 4], qk["wk", t // 4]]
    rings = M.attention_rings(3, 2, 1)
    rings["A"] = M.ring(2, DIM)
    last = Ring(M.bank[6:8])
    hd = DIM // HEADS0
    swa_done = [None] * NT

    def units():
        for t in [TILES] + list(range(TILES)):
            prev = TILES if t % 2 == 0 else t - 1
            if t == TILES:
                segments, mask = [(P, P)], c("windowmem")
            elif t % 2:
                segments, mask = [(P - WIN0, WIN0 + P)], c("window")
            else:
                segments, mask = [(P - WIN0, WIN0), (P, P)], c("window")
            src = lambda col, t=t, prev=prev: t if col >= P else prev

            def finish(attn, done, g, t=t):
                bank, free = last.take()
                pr = M.mm([free, done], [(bank.ap[:, 0:P], [(w("wo"), attn.ap)])])
                attn.free = pr
                yield
                cp = M.copy(M.act, pr, swaT[:, t * P:t * P + P], bank.ap[:, 0:P])
                bank.free = cp
                swa_done[t] = cp

            tile = {"order": [(0, 1), (2, 3)], "apart": True, "valued": lambda token: None,
                    "scored": lambda token: None, "ready": [of(t), of(prev)],
                    "vready": [qk["v", t // 4], qk["v", prev // 4]],
                    "segments": segments, "mask": mask,
                    "q": lambda h, t=t: q[hd * h:hd * h + hd, t * P:t * P + P],
                    "k": lambda h, sg, src=src: k[hd * h:hd * h + hd,
                                                  src(sg[0]) * P + sg[0] % P:src(sg[0]) * P + sg[0] % P + sg[1]],
                    "v": lambda h, blk, src=src: v[:, src(blk * P), hd * h:hd * h + hd]}
            yield from M.attend(rings, HEADS0, hd, 1.0 / float(np.sqrt(hd)), tile, finish)

    for r in rings["P"].slots:
        r.free = M.pool([], nc.gpsimd.memset, r.ap, 0.0)
    pipeline(units())
    attention_end = M.everything()
    for e in (M.pe, M.act, M.dve, M.pool):
        e.wait(attention_end)
    M.used = at
    for b in M.bank:
        b.free = []
    ones = c("ones")
    g1, g2, gb1, gb2 = (M.bank[i].ap for i in range(4))
    banks = Ring(M.bank[4:8])
    nw1, nw2, nb1, nb2, keep = M.alloc(HID0), M.alloc(HID0), M.alloc(HID0), M.alloc(1), M.alloc(1)
    gradient_room = M.used
    sig, h, hT, dT, dtok, dh = (M.ring(3, HID0), M.ring(3, HID0), M.ring(2, HID0), M.ring(2, P), M.ring(2, P),
                                M.ring(2, HID0))
    grads = []

    def gradient(t):
        tok = w("mem") if t == TILES else M.xn[:, t, :]
        xt, first, final = xT[:, t * P:t * P + P], t == 0, t == TILES
        s, sfree = yield from sig.get()
        hs, hfree = yield from h.get()
        zb, free = yield from banks.get()
        z = M.mm([free, tile_ready[t]], [(zb.ap, [(xt, w("w1")), (ones[0:1, :], w("b1")[0:1, :])])])
        yield
        st = M.act([z, sfree], nc.scalar.activation, s.ap, zb.ap, ACT.Sigmoid)
        ht = M.dve([st, hfree], nc.vector.tensor_tensor, hs.ap, zb.ap, s.ap, ALU.mult)
        zb.free = ht
        yield
        tb, free = yield from banks.get()
        tr = M.transposes([free, ht], [(tb.ap[:, j:j + P], hs.ap[:, j:j + P]) for j in range(0, HID0, P)])
        yield
        hTs, free = yield from hT.get()
        cp = M.copy(M.act, [tr, free], hTs.ap, tb.ap)
        yield
        pr = M.mm(cp, [(tb.ap[:, 0:P], [(w("w2T")[:, j * P:j * P + P], hTs.ap[:, j * P:j * P + P]) for j in range(4)])])
        hTs.free = pr
        yield
        d, free = yield from dT.get()
        dt = M.dve([pr, free], nc.vector.scalar_tensor_tensor, d.ap, tb.ap[:, 0:P], w("b2col"),
                   swaT[:, t * P:t * P + P], ALU.add, ALU.subtract)
        if final:
            dt = M.dve(dt, nc.vector.tensor_scalar, d.ap[:, P - MEM0:], d.ap[:, P - MEM0:], float(BATCH), None, ALU.mult)
            dt = M.dve(dt, nc.vector.memset, d.ap[:, 0:P - MEM0], 0.0)
        tb.free = dt
        yield
        db, free = yield from banks.get()
        tr = M.transposes([free, dt], [(db.ap[:, 0:P], d.ap)])
        hb, free = yield from banks.get()
        dz = M.mm(free, [(hb.ap, [(d.ap, w("w2"))])])
        d.free = dz
        yield
        dk, free = yield from dtok.get()
        dc = M.copy(M.act, [tr, free], dk.ap, db.ap[:, 0:P])
        db.free = dc
        e, free = yield from dh.get()
        a = M.dve([free, st, ht], nc.vector.scalar_tensor_tensor, e.ap, s.ap, 1.0, hs.ap, ALU.subtract, ALU.mult)
        a = M.dve(a, nc.vector.tensor_tensor, e.ap, s.ap, e.ap, ALU.subtract)
        s.free = a
        a = M.dve([a, dz], nc.vector.tensor_tensor, e.ap, hb.ap, e.ap, ALU.mult)
        hb.free = a
        yield
        pe = M.pe
        assert len(grads) == t
        pe.wait([a, dc])
        mm = nc.tensor.matmul
        kw = dict(start=first, stop=final, skip_group_check=True)
        mm(g1, tok, e.ap, **kw)
        for j in range(4):
            mm(g2[:, j * P:j * P + P], hs.ap[:, j * P:j * P + P], dk.ap, start=first and j == 0, stop=final,
               skip_group_check=True)
        mm(gb1[0:1, :], ones[:, 0:1], e.ap, **kw)
        end = pe.mark(mm(gb2[:, 0:1], dk.ap, ones[:, 0:1], **kw))
        for x in (e, hs, dk):
            x.free = end
        grads.append(end)

    pipeline(gradient(t) for t in range(NT))
    k1 = M.dve([], nc.vector.tensor_scalar, keep, w("alpha"), -1.0, 1.0, ALU.mult, ALU.add)

    def step(out, p, g, parts):
        t = M.dve([grads[-1]], nc.vector.tensor_scalar, out, g, w("theta")[0:parts], None, ALU.mult)
        return M.dve([t, k1], nc.vector.scalar_tensor_tensor, out, p, keep[0:parts], out, ALU.mult, ALU.subtract)

    updated = [step(nw1, w("w1"), g1, P), step(nw2, w("w2T"), g2, P), step(nb1[0:1, :], w("b1")[0:1, :], gb1[0:1, :], 1),
               step(nb2, w("b2col"), gb2[:, 0:1], P)]
    for b in M.bank:
        b.free = updated
    banks = Ring(M.bank)
    M.used = gradient_room
    hid, outm, gate1, gate2 = M.ring(2, 4, GROUP), M.ring(2, GROUP), M.ring(2, GROUP), M.ring(2, GROUP)
    done = []
    for g in range(GROUPS):
        sl = slice(g * GROUP, (g + 1) * GROUP)
        hs, hfree = hid.take()
        ts = []
        for j in range(4):
            b, free = banks.take()
            t = M.mm([free, updated], [(b.ap, [(nw1[:, j * P:j * P + P], xT[:, sl]),
                                               (nb1[0:1, j * P:j * P + P], ones512(M)[0:1, :])])])
            t2 = M.act([t, hfree], nc.scalar.activation, hs.ap[:, j, :], b.ap, ACT.Sigmoid)
            t2 = M.dve(t2, nc.vector.tensor_tensor, hs.ap[:, j, :], b.ap, hs.ap[:, j, :], ALU.mult)
            b.free = t2
            ts.append(t2)
        b, free = banks.take()
        t = M.mm([free, ts], [(b.ap, [(nw2[:, j * P:j * P + P], hs.ap[:, j, :]) for j in range(4)])])
        hs.free = t
        om, free = outm.take()
        t = M.dve([t, free], nc.vector.tensor_scalar, om.ap, b.ap, nb2, None, ALU.add)
        b.free = t
        b2, free = banks.take()
        t2 = M.mm([free, t], [(b2.ap, [(w("lin2"), om.ap)])])
        b1, free = banks.take()
        t1 = M.mm(free, [(b1.ap, [(w("lin1"), swaT[:, sl])])])
        a, free = gate1.take()
        t1 = M.act([t1, free], nc.scalar.activation, a.ap, b1.ap, ACT.Sigmoid)
        b1.free = t1
        z, free = gate2.take()
        t2 = M.act([t2, free], nc.scalar.activation, z.ap, b2.ap, ACT.Sigmoid)
        b2.free = t2
        t1 = M.dve(t1, nc.vector.tensor_tensor, a.ap, a.ap, swaT[:, sl], ALU.mult)
        t2 = M.dve(t2, nc.vector.tensor_tensor, z.ap, z.ap, om.ap, ALU.mult)
        om.free = t2
        t = M.dve([t1, t2], nc.vector.tensor_tensor, a.ap, a.ap, z.ap, ALU.add)
        z.free = t
        b, free = banks.take()
        tr = M.transposes([free, t], [(b.ap[:, j:j + P], a.ap[:, j:j + P]) for j in range(0, GROUP, P)])
        a.free = tr
        t = M.copy(M.act, tr, M.y[:, 4 * g:4 * g + 4, :], b.ap.rearrange("p (t d) -> p t d", d=DIM))
        b.free = t
        done += [t] * 4
    return done


def ones512(M):
    return M.c("ones")[:, 0:1].broadcast_to([P, GROUP])


def attention_heads8(M, stage, rings, batch_state, kv_pick, mask_of, clip, scale, finish_tile, b):
    st = batch_state[b]
    qT, kT, v = st["q"], st["k"], st["v"]
    out = []
    for half in range(2):
        t = 2 * b + half
        mask = mask_of(half)
        if mask is not None and not clip:
            segments = [(P, P)] if half == 0 else [(0, 2 * P)]
            block = lambda col, half=half: half if col >= P else 0
        else:
            segments = [(0, 2 * P)]
            block = lambda col: col // P
        def scored(token, st=st):
            both(st, "scored", token, st["slots"][0])

        def valued(token, st=st):
            both(st, "valued", token, st["slots"][1])

        tile = {"order": [(h, h + 4) for h in (0, 1, 2, 3, 8, 9, 10, 11)], "scored": scored, "valued": valued,
                "ready": st["ready"], "vready": st["vready"], "segments": segments, "mask": mask, "clip": clip,
                "q": lambda h, half=half: qT[32 * (h % 4):32 * (h % 4) + 32, h // 4, half * P:half * P + P],
                "k": lambda h, sg, block=block: kT[32 * (h % 4):32 * (h % 4) + 32, h // 4,
                                                   block(sg[0]) * P:block(sg[0]) * P + sg[1]],
                "v": lambda h, blk, block=block: v[:, block(blk * P), 32 * kv_pick(h):32 * kv_pick(h) + 32]}
        out += M.attend(rings, HEADS, HDIM, scale, tile, lambda attn, done, g, t=t: finish_tile(attn, done, t))
    return out


def both(state, step, token, *slots):
    state.setdefault(step, []).append(token)
    if len(state[step]) == 2:
        for slot in slots:
            slot.free = state[step]


def run_batches(prepare, pairs, rate=2):
    for _ in prepare(0):
        pass

    following = [iter(())]

    def units():
        for b in range(BATCH):
            following[0] = prepare(b + 1) if b + 1 < BATCH else iter(())
            for p in pairs(b):
                yield p
            for _ in following[0]:
                pass

    pipeline(units(), lambda: next(following[0], None), rate)


def project_out(M, banks, wo, wait_w, done_y, bias=None):
    def finish(attn, done, t):
        bank, free = banks.take()
        pairs = [(attn.ap[:, k * P:k * P + P], wo[:, k * P:k * P + P]) for k in range(CHUNKS)]
        if bias is not None:
            pairs.append((M.c("ones")[0:1, :], bias[0:1, :]))
        pr = M.mm([free, done, wait_w], [(bank.ap[:, 0:P], pairs)])
        attn.free = pr
        yield
        cp = M.copy(M.act, pr, M.y[:, t, :], bank.ap[:, 0:P])
        bank.free = cp
        done_y[t] = cp
    return finish


def zero_ring(M, n, *shape):
    ring = M.ring(n, *shape)
    for s in ring.slots:
        s.free = M.pool([], M.nc.gpsimd.memset, s.ap, 0.0)
    return ring


def stage_split(M, ready):
    nc, c, w = M.nc, M.c, lambda n: M.w("split", n)
    wait_w = M.loaded["split"][0]
    tt, ts, stt = nc.vector.tensor_tensor, nc.vector.tensor_scalar, nc.vector.scalar_tensor_tensor
    banks = Ring(M.bank)
    turned = M.turn(ready, M.xn, M.xnT, banks)
    heads = lambda ap: ap.rearrange("p (h d) -> p h d", d=HDIM)
    gn, gsq, gl = M.alloc(DIM), M.alloc(DIM), M.alloc(HEADS)
    t = M.dve(wait_w, tt, gsq, w("g"), w("g"), ALU.mult)
    t = M.dve(t, nc.vector.tensor_reduce, gl, heads(gsq), AX, ALU.add)
    t = M.pool(t, nc.gpsimd.tensor_tensor, gl, gl, c("half", HEADS), ALU.pow)
    guide = M.dve(t, tt, heads(gn), heads(w("g")), gl.unsqueeze(2).broadcast_to([P, HEADS, HDIM]), ALU.mult)
    dots, lens = M.alloc(TILES, HEADS), M.alloc(TILES, HEADS)
    tmp, tmp2 = M.ring(2, GROUP), M.ring(2, GROUP)
    ts_ = []
    four = lambda ap: ap.rearrange("p (t h d) -> p t h d", t=4, d=HDIM)
    for g in range(GROUPS):
        bank, free = banks.take()
        t = M.mm([free, turned[g], wait_w], [(bank.ap[:, P * k:P * k + P],
                                              [(M.xnT[:, GROUP * g + P * k:GROUP * g + P * k + P], w("wq"))]) for k in range(4)])
        a, free = tmp.take()
        t1 = M.dve([t, free, guide], tt, a.ap.rearrange("p (t d) -> p t d", t=4),
                   bank.ap.rearrange("p (t d) -> p t d", t=4), gn.unsqueeze(1).broadcast_to([P, 4, DIM]), ALU.mult)
        s, free = tmp2.take()
        t2 = M.act([t1, free], nc.scalar.activation, s.ap, bank.ap, ACT.Square)
        bank.free = [t1, t2]
        a.free = M.dve(t1, nc.vector.tensor_reduce, dots[:, 4 * g:4 * g + 4, :], four(a.ap), AX, ALU.add)
        s.free = M.dve(t2, nc.vector.tensor_reduce, lens[:, 4 * g:4 * g + 4, :], four(s.ap), AX, ALU.add)
        ts_ += [a.free, s.free]
    flat2 = lambda ap: ap.rearrange("p t h -> p (t h)")
    inverse, room = M.alloc(TILES, HEADS), M.alloc(TILES, HEADS)
    t = M.rsqrt(ts_, flat2(lens), flat2(inverse), flat2(room))
    t = M.dve(t, tt, dots, dots, inverse, ALU.mult)
    sim, lo, ext, ext2 = M.alloc(TILES), M.alloc(TILES), M.alloc(2), M.alloc(2)
    t = M.dve(t, nc.vector.tensor_reduce, sim, dots, AX, ALU.add)
    sim_t = M.dve(t, ts, sim, sim, 1.0 / HEADS, None, ALU.mult)
    t = M.dve(sim_t, stt, lo, c("reg"), NEG, sim, ALU.mult, ALU.add)
    t = M.dve(t, nc.vector.tensor_reduce, ext[:, 0:1], lo, AX, ALU.max)
    t = M.dve(t, stt, lo, c("reg"), NEG, sim, ALU.mult, ALU.subtract)
    t = M.dve(t, nc.vector.tensor_reduce, ext[:, 1:2], lo, AX, ALU.max)
    t = M.pool(t, nc.gpsimd.partition_all_reduce, ext2, ext, P, bass.bass_isa.ReduceOp.max)
    rng, up, pos, neg = M.alloc(1), M.alloc(TILES), M.alloc(TILES), M.alloc(TILES)
    t = M.dve(t, ts, rng, ext2[:, 0:1], ext2[:, 1:2], 0.9, ALU.add, ALU.mult)
    t = M.dve(t, ts, up, sim, ext2[:, 1:2], rng, ALU.add, ALU.is_gt)
    notreg = M.alloc(TILES)
    a = M.dve([], ts, notreg, c("reg"), -1.0, 1.0, ALU.mult, ALU.add)
    kpos, kneg = M.alloc(TILES), M.alloc(TILES)
    b0 = M.dve([t, a], tt, kpos, up, notreg, ALU.mult)
    b1 = M.dve(b0, tt, kneg, notreg, kpos, ALU.subtract)
    b2 = M.dve(b0, tt, pos, kpos, c("reg"), ALU.add)
    b3 = M.dve(b2, ts, neg, pos, -1.0, 1.0, ALU.mult, ALU.add)
    extra = M.alloc(2, TILES, 2)
    fills = [M.dve(b3, ts, extra[:, 0, :, 0], pos, 1.0, None, ALU.mult), M.dve(b3, ts, extra[:, 0, :, 1], neg, 1.0, None, ALU.mult),
             M.dve(b3, ts, extra[:, 1, :, 0], kneg, NEG, None, ALU.mult), M.dve(b3, ts, extra[:, 1, :, 1], kpos, NEG, None, ALU.mult)]
    spread = M.ring(2, 2, P)
    for s in spread.slots:
        s.free = M.pool([], nc.gpsimd.memset, s.ap, 0.0)
    qx = M.ring(2, 4, HEADS * REG)
    for s in qx.slots:
        s.free = M.pool([], nc.gpsimd.memset, s.ap, 0.0)
    rings = M.attention_rings(3, 2, 1, on_pool=(0, 1, 2, 4, 5, 6))
    rings["A"] = M.ring(2, 4 * P)
    gen = Ring(M.bank[6:8])
    start = M.everything()
    for b in M.bank:
        b.free = start
    M.extra = [[M.xn.rearrange("p t d -> p (t d)"), TILES * DIM, 0]]
    kq = M.ring(2, 2, 4, SEQ)
    vs, exs = zero_ring(M, 3, 2, 4 * P), M.ring(2, 2, SEQ)
    regs = M.ring(3, 4 * REG)
    small = M.ring(2, 4)
    pr_, prT, orr = M.ring(2, SEQ), M.ring(2, 2 * HEADS * REG), M.ring(2, 4 * P)
    spread_v = lambda v: v.rearrange("p b (h d) -> p b h d", h=HEADS)[:, :, :, 0:HDIM]
    state, done_y = {}, [None] * TILES
    NR = HEADS * REG

    def prepare(b):
        sl = slice(b * SEQ, (b + 1) * SEQ)
        g = b // 2
        ex, xfree = exs.take()
        bank, free = gen.take()
        trs = []
        for half in range(2):
            sp, free2 = spread.take()
            v = sp.ap.rearrange("p s (g r) -> p s g r", g=4)[:, :, :, HDIM:HDIM + 2]
            src = extra[:, :, 2 * b + half, :].unsqueeze(2).broadcast_to([P, 2, 4, 2])
            t1 = M.pool([fills, free2], nc.gpsimd.tensor_copy, v[:, 0], src[:, 0])
            t1 = M.pool([], nc.gpsimd.tensor_copy, v[:, 1], src[:, 1])
            t1 = M.transposes([free, t1], [(bank.ap[:, s * SEQ + half * P:s * SEQ + half * P + P], sp.ap[:, s, :]) for s in range(2)])
            sp.free = t1
        yield
        ext_t = M.copy(M.act, [t1, xfree], ex.ap, bank.ap.rearrange("p (s n) -> p s n", s=2))
        bank.free = ext_t
        yield
        slot, kfree = kq.take()
        outs = []
        for which, name in enumerate(("wqs", "wks")):
            for pairc in range(2):
                bank, free = gen.take()
                t = M.mm([free, turned[g], wait_w], [(bank.ap[:, i * SEQ:(i + 1) * SEQ],
                         [(w(name)[:, (2 * pairc + i) * P:(2 * pairc + i + 1) * P], M.xnT[:, sl])]) for i in range(2)])
                yield
                t = M.dve([t, kfree, ext_t], tt, slot.ap[:, which, 2 * pairc:2 * pairc + 2, :],
                          bank.ap.rearrange("p (c n) -> p c n", c=2),
                          ex.ap[:, which, :].unsqueeze(1).broadcast_to([P, 2, SEQ]), ALU.add)
                bank.free = t
                outs.append(t)
        ex.free = outs
        bank, free = gen.take()
        v, vfree = vs.take()
        t = M.mm([free], [(bank.ap[:, i * P:i * P + P], [(M.xnT[:, b * SEQ + i * P:b * SEQ + (i + 1) * P], w("wv"))]) for i in range(2)])
        yield
        vt = None
        for i in range(2):
            vt = M.copy(M.act, [t, vfree], spread_v(v.ap)[:, i], bank.ap[:, i * P:i * P + P].rearrange("p (h d) -> p h d", h=HEADS))
        bank.free = vt
        q = slot.ap[:, 0]
        k = slot.ap[:, 1]
        x, xf = qx.take()
        for gg in range(4):
            dst = x.ap[32 * gg:32 * gg + 32].rearrange("p c (h r) -> p c h r", r=REG)
            for cc in range(4):
                t = M.dve([xf, outs], ts, dst[:, cc, 4 * cc + gg, :], q[32 * gg:32 * gg + 32, cc, 0:REG],
                          c("turn")[32 * gg:32 * gg + 32], None, ALU.add)
        yield
        bank, free = gen.take()
        t = M.mm([free, t], [(bank.ap[0:NR, 0:SEQ], [(x.ap[:, cc, :], k[:, cc, :]) for cc in range(4)])])
        x.free = t
        yield
        sm, sf = small.take()
        s = sm.ap[0:NR]
        t = M.dve([t, sf], nc.vector.tensor_reduce, s[:, 0:1], bank.ap[0:NR, 0:SEQ], AX, ALU.max)
        t = M.dve(t, ts, s[:, 1:2], s[:, 0:1], -(HDIM ** -0.5), None, ALU.mult)
        p_, pf = pr_.take()
        yield
        e = M.act([t, pf], nc.scalar.activation, p_.ap[0:NR], bank.ap[0:NR, 0:SEQ], ACT.Exp, bias=s[:, 1:2],
                  scale=HDIM ** -0.5, accum_out=s[:, 2:3])
        bank.free = e
        yield
        bank, free = gen.take()
        t = M.transposes([e, free], [(bank.ap[:, i * NR:(i + 1) * NR], p_.ap[0:NR, i * P:i * P + P]) for i in range(2)])
        p_.free = t
        yield
        pT, pf = prT.take()
        t = M.copy(M.act, [t, pf], pT.ap, bank.ap[:, 0:2 * NR])
        yield
        bank.free = t
        bank, free = gen.take()
        t = M.mm([t, vt, free], [(bank.ap[0:NR], [(pT.ap[:, i * NR:(i + 1) * NR], v.ap[:, i, :]) for i in range(2)])])
        pT.free = t
        yield
        r = M.dve(e, nc.vector.reciprocal, s[:, 3:4], s[:, 2:3])
        o, of_ = orr.take()
        t = M.dve([t, r, of_], stt, o.ap[0:NR], bank.ap[0:NR], s[:, 3:4], c("block")[0:NR], ALU.mult, ALU.mult)
        sm.free = t
        yield
        t = M.mm(t, [(bank.ap[:, k_ * REG:(k_ + 1) * REG], [(o.ap[0:NR, k_ * P:k_ * P + P], c("pick")[0:NR, :])])
                     for k_ in range(CHUNKS)])
        o.free = t
        yield
        rg, rf = regs.take()
        t = M.copy(M.act, [t, rf], rg.ap, bank.ap[:, 0:4 * REG])
        bank.free = t
        state[b] = {"q": q, "k": k, "v": v.ap, "ready": outs, "vready": vt, "reg": rg, "regt": t, "slots": (slot, v)}

    out = project_out(M, gen, w("wo"), wait_w, done_y, bias=w("bo"))

    def finish(attn, done, t):
        if t % 2 == 0:
            st = state[t // 2]
            both = attn.ap.rearrange("p (c n) -> p c n", c=CHUNKS)[:, :, 0:REG]
            done = M.dve([done, st["regt"]], stt, both, both, 0.5, st["reg"].ap.rearrange("p (c n) -> p c n", c=CHUNKS),
                         ALU.mult, ALU.add)
            st["reg"].free = done
        yield from out(attn, done, t)

    def pairs(b):
        yield from attention_heads8(M, "split", rings, state, lambda h: h, lambda half: None, None, HDIM ** -0.5, finish, b)

    run_batches(prepare, pairs)
    return done_y


def stage_linear(M, ready):
    nc, c, w = M.nc, M.c, lambda n: M.w("linear", n)
    wait_w = M.loaded["linear"][0]
    tt, ts, stt = nc.vector.tensor_tensor, nc.vector.tensor_scalar, nc.vector.scalar_tensor_tensor
    banks = Ring(M.bank)
    turned = M.turn(ready, M.xn, M.xnT, banks)
    ones = c("ones")
    gate = M.alloc(HEADS)
    gt = M.act(wait_w, nc.scalar.activation, gate, w("stdp"), ACT.Sigmoid)
    qT = M.alloc(TOKENS)
    kk, vv = M.alloc(TILES, DIM), M.alloc(TILES, DIM)
    ex = M.ring(3, GROUP)
    kv = M.ring(2, DIM + HEADS)
    an, aT, rd = M.ring(2, DIM), M.ring(2, DIM), M.ring(2, HEADS)

    def phi(after, bank, out, bias=None):
        e, free = ex.take()
        z = bank.ap
        if bias is None:
            t = M.dve([after, free], ts, e.ap, z, 0.0, None, ALU.min)
        else:
            t = M.dve([after, free], ts, e.ap, z, bias, 0.0, ALU.add, ALU.min)
        t = M.act(t, nc.scalar.activation, e.ap, e.ap, ACT.Exp)
        if bias is None:
            t = M.dve(t, stt, out, z, 0.0, e.ap, ALU.max, ALU.add)
        else:
            t1 = M.dve([after], ts, out, z, bias, 0.0, ALU.add, ALU.max)
            t = M.dve([t, t1], tt, out, out, e.ap, ALU.add)
        bank.free = t
        e.free = t
        return t

    qd, kd, vd = {}, {}, {}
    for g in range(GROUPS):
        sl = slice(g * GROUP, (g + 1) * GROUP)
        b, free = banks.take()
        t = M.mm([free, turned[g], wait_w], [(b.ap, [(w("Wq"), M.xnT[:, sl])])])
        qd[g] = phi(t, b, qT[:, sl], w("bq"))
        for name, bias, dst in (("Wk", "bk", kk), ("Wv", "bv", vv)):
            b, free = banks.take()
            t = M.mm([free], [(b.ap[:, P * i:P * i + P], [(M.xnT[:, g * GROUP + i * P:g * GROUP + (i + 1) * P], w(name)),
                                                          (ones[0:1, :], w(bias)[0:1, :])]) for i in range(4)])
            d = dst[:, 4 * g:4 * g + 4, :].rearrange("p t d -> p (t d)")
            if name == "Wk":
                kd[g] = phi(t, b, d)
            else:
                vd[g] = M.copy(M.act, t, d, b.ap)
                b.free = vd[g]
    done = []
    for bt in range(BATCH):
        g = bt // 2
        b, free = banks.take()
        t = M.mm([free, kd[g], vd[g]], [(b.ap[:, 0:P], [(kk[:, 2 * bt + i, :], vv[:, 2 * bt + i, :]) for i in range(2)]),
                                        (b.ap[:, P:P + 1], [(kk[:, 2 * bt + i, :], ones[:, 0:1]) for i in range(2)])])
        s, free = kv.take()
        t1 = M.dve([t, free], tt, s.ap[:, 0:P], b.ap[:, 0:P], c("blockdiag"), ALU.mult)
        t2 = M.dve([], ts, s.ap[:, P:], c("blockhead"), b.ap[:, P:P + 1], None, ALU.mult)
        b.free = [t1, t2]
        for i in range(2):
            tile = 2 * bt + i
            b, free = banks.take()
            t = M.mm([free, t1, t2, qd[g]], [(b.ap[:, 0:P + HEADS], [(qT[:, tile * P:tile * P + P], s.ap)])])
            s.free = t
            r, free = rd.take()
            t3 = M.dve([t, free], ts, r.ap, b.ap[:, P:P + HEADS], 1e-6, None, ALU.add)
            t3 = M.dve(t3, nc.vector.reciprocal, r.ap, r.ap)
            t3 = M.dve([t3, gt], tt, r.ap, r.ap, gate, ALU.mult)
            a, free = an.take()
            t4 = M.dve([t3, free], tt, a.ap.rearrange("p (h d) -> p h d", d=HDIM),
                       b.ap[:, 0:P].rearrange("p (h d) -> p h d", d=HDIM),
                       r.ap.unsqueeze(2).broadcast_to([P, HEADS, HDIM]), ALU.mult)
            r.free = t4
            t5 = M.transposes(t4, [(b.ap[:, 256:384], a.ap)])
            a.free = t5
            x, free = aT.take()
            t5 = M.copy(M.act, [t5, free], x.ap, b.ap[:, 256:384])
            t5 = M.mm(t5, [(b.ap[:, 384:512], [(x.ap, w("Wo")), (ones[0:1, :], w("bo")[0:1, :])])])
            x.free = t5
            t5 = M.copy(M.act, t5, M.y[:, tile, :], b.ap[:, 384:512])
            b.free = t5
            done.append(t5)
    return done


def top_two(M, after, logits, E):
    nc = M.nc
    tt, ts = nc.vector.tensor_tensor, nc.vector.tensor_scalar
    B3 = lambda ap: ap.broadcast_to([P, TILES, E])
    red, coef = M.alloc(TILES), M.alloc(TILES, E)
    t = M.dve(after, nc.vector.tensor_reduce, red, logits, AX, ALU.max)
    t = M.dve(t, tt, logits, logits, B3(red.unsqueeze(2)), ALU.subtract)
    t = M.act(t, nc.scalar.activation, logits, logits, ACT.Exp)
    t = M.dve(t, nc.vector.tensor_reduce, red, logits, AX, ALU.add)
    t = M.dve(t, nc.vector.reciprocal, red, red)
    t = M.dve(t, tt, logits, logits, B3(red.unsqueeze(2)), ALU.mult)
    best, index = M.alloc(TILES, 8), M.alloc(TILES, 8)
    fi = M.alloc(TILES, 8)
    for i in range(TILES):
        u = M.dve(t, nc.vector.max, best[:, i, :], logits[:, i, :])
        v = M.dve(u, nc.vector.max_index, index[:, i, :].bitcast(U32), best[:, i, :], logits[:, i, :])
    v = M.dve(v, nc.vector.tensor_copy, fi, index.bitcast(U32))
    t = M.dve(v, tt, red, best[:, :, 0], best[:, :, 1], ALU.add)
    t = M.dve(t, nc.vector.reciprocal, red, red)
    t = M.dve(t, tt, best[:, :, 0:2], best[:, :, 0:2], red.unsqueeze(2).broadcast_to([P, TILES, 2]), ALU.mult)
    iota = M.c("iota", E).unsqueeze(1)
    hot = M.alloc(TILES, E)
    t0 = M.dve(t, tt, coef, B3(iota), B3(fi[:, :, 0:1]), ALU.is_equal)
    t0 = M.dve(t0, tt, coef, coef, B3(best[:, :, 0:1]), ALU.mult)
    t1 = M.dve(t0, tt, hot, B3(iota), B3(fi[:, :, 1:2]), ALU.is_equal)
    t1 = M.dve(t1, tt, hot, hot, B3(best[:, :, 1:2]), ALU.mult)
    return coef, M.dve(t1, tt, coef, coef, hot, ALU.add)


def experts(M, stage, E, xT, x_ready, coef, coef_ready, norm, first):
    nc, w = M.nc, lambda n: M.w(stage, n)
    wait_w = M.loaded[stage][0]
    tt, ts, stt = nc.vector.tensor_tensor, nc.vector.tensor_scalar, nc.vector.scalar_tensor_tensor
    up, down = Ring(M.bank[0:6]), Ring(M.bank[6:8])
    act, hid = M.ring(4, GROUP), M.ring(3, 2, GROUP)
    mid = M.ring(3, 4, DIM)
    st_at = [0]
    last = [first[t] for t in range(TILES)]

    def unit(e, g):
        sl = slice(g * GROUP, (g + 1) * GROUP)
        gates, ups = [], []
        for f in range(2):
            b, free = up.take()
            t = M.mm([free, wait_w, x_ready], [(b.ap, [(w(f"gate{e}")[:, f * P:f * P + P], xT[:, sl])])])
            gates.append((b, t))
            b, free = up.take()
            t = M.mm([free], [(b.ap, [(w(f"up{e}")[:, f * P:f * P + P], xT[:, sl])])])
            ups.append((b, t))
        yield
        h, hfree = hid.take()
        ts_ = []
        for f in range(2):
            a, free = act.take()
            t = M.act([gates[f][1], free], nc.scalar.activation, a.ap, gates[f][0].ap, ACT.Silu)
            gates[f][0].free = t
            t = M.dve([t, ups[f][1], hfree], tt, h.ap[:, f, :], ups[f][0].ap, a.ap, ALU.mult)
            ups[f][0].free = t
            a.free = t
            ts_.append(t)
        yield
        b, free = down.take()
        yv = b.ap.rearrange("p (t d) -> p t d", t=4)
        t = M.mm([free, ts_], [(yv[:, k, :], [(h.ap[:, f, k * P:k * P + P], w(f"down{e}")[:, f * P:f * P + P])
                                              for f in range(2)]) for k in range(4)])
        h.free = t
        yield
        y = M.y[:, 4 * g:4 * g + 4, :]
        cf = coef[:, 4 * g:4 * g + 4, e]
        if not norm:
            for k in range(4):
                t2 = M.dve([t, coef_ready, last[4 * g]], stt, y[:, k, :], yv[:, k, :], coef[:, 4 * g + k, e:e + 1],
                           y[:, k, :], ALU.mult, ALU.add)
            b.free = t2
            last[4 * g] = t2
            return
        at = 48 * (st_at[0] % 4)
        st_at[0] += 1
        mean, rstd, mt = M.moments([t, stats_free[(st_at[0] - 1) % 4]], [yv[:, k, :] for k in range(4)], 4, at)
        yield
        sc = M.stats[:, 200 + at // 12:204 + at // 12]
        t2 = M.dve([mt, coef_ready], tt, sc, rstd, cf, ALU.mult)
        m, free = mid.take()
        for k in range(4):
            t3 = M.dve([t2, free], ts, m.ap[:, k, :], yv[:, k, :], mean[:, k:k + 1], sc[:, k:k + 1], ALU.subtract, ALU.mult)
        b.free = t3
        stats_free[(st_at[0] - 1) % 4] = t3
        yield
        gain = w("lng")[:, e * DIM:(e + 1) * DIM].unsqueeze(1).broadcast_to([P, 4, DIM])
        t4 = M.pool([t3], nc.gpsimd.tensor_tensor, m.ap, m.ap, gain, ALU.mult)
        t4 = M.pool([t4, last[4 * g]], nc.gpsimd.tensor_tensor, y, y, m.ap, ALU.add)
        m.free = t4
        last[4 * g] = t4

    stats_free = [None] * 4
    pipeline(unit(e, g) for e in range(E) for g in range(GROUPS))
    return [last[4 * (t // 4)] for t in range(TILES)]


def router(M, xT, x_ready, wr, E, banks, bias=None):
    nc = M.nc
    logits = M.alloc(TILES, E)
    b, free = banks.take()
    t = M.mm([free, x_ready], [(b.ap[:, E * i:E * i + E], [(xT[:, P * i:P * i + P], wr)] + (
        [(M.c("ones")[0:1, :], bias[0:1, :])] if bias is not None else [])) for i in range(TILES)])
    t = M.copy(M.dve, t, logits, b.ap[:, 0:E * TILES].rearrange("p (t e) -> p t e", e=E))
    b.free = t
    return top_two(M, t, logits, E)


def stage_moe1(M, ready):
    nc, w = M.nc, lambda n: M.w("moe1", n)
    banks = Ring(M.bank)
    turned = M.turn(ready, M.xn, M.xnT, banks)
    coef, ct = router(M, M.xnT, [turned, M.loaded["moe1"][0]], w("router"), EXP1, banks, w("rb"))
    cT = M.ring(2, 4, P)
    first = []
    for g in range(GROUPS):
        b, free = banks.take()
        t = M.transposes([free, ct], [(b.ap[0:EXP1, P * k:P * k + P], coef[:, 4 * g + k, :]) for k in range(4)])
        s, sf = cT.take()
        t = M.copy(M.act, [t, sf], s.ap[0:EXP1], b.ap[0:EXP1, :].rearrange("p (k n) -> p k n", k=4))
        b.free = t
        b, free = banks.take()
        t = M.mm([free, t], [(b.ap[:, P * k:P * k + P], [(s.ap[0:EXP1, k, :], w("lnb")[0:EXP1, :])]) for k in range(4)])
        s.free = t
        t = M.copy(M.act, t, M.y[:, 4 * g:4 * g + 4, :], b.ap.rearrange("p (k n) -> p k n", k=4))
        b.free = t
        first += [t] * 4
    return experts(M, "moe1", EXP1, M.xnT, turned, coef, ct, True, first)


def stage_mamba(M, ready):
    nc, c, w = M.nc, M.c, lambda n: M.w("mamba", n)
    wait_w = M.loaded["mamba"][0]
    tt, ts, stt = nc.vector.tensor_tensor, nc.vector.tensor_scalar, nc.vector.scalar_tensor_tensor
    banks = Ring(M.bank)
    turned = M.turn(ready, M.xn, M.xnT, banks)
    u, dl = M.alloc(2, TOKENS), M.alloc(2, TOKENS)
    raw = M.ring(1, TOKENS)
    du = M.alloc(2, TOKENS)
    ut = {}
    act1 = M.xn.rearrange("p t d -> p (t d)")
    for h in range(2):
        r, rfree = raw.take()
        seq = lambda ap: ap.rearrange("p (b s) -> p b s", b=BATCH)
        for g in range(GROUPS):
            b, free = banks.take()
            t = M.mm([free, turned[g], wait_w], [(b.ap, [(w("in")[:, h * P:h * P + P], M.xnT[:, g * GROUP:(g + 1) * GROUP])])])
            t = M.copy(M.act, [t, rfree], r.ap[:, g * GROUP:(g + 1) * GROUP], b.ap)
            b.free = t
        tap = lambda k: w("conv")[:, 3 * h + k:3 * h + k + 1]
        o, s = seq(u[:, h, :]), seq(r.ap)
        t = M.dve([t], ts, u[:, h, :], r.ap, tap(1), w("convb")[:, h:h + 1], ALU.mult, ALU.add)
        t = M.dve(t, stt, o[:, :, 1:], s[:, :, :-1], tap(0), o[:, :, 1:], ALU.mult, ALU.add)
        t = M.dve(t, stt, o[:, :, :-1], s[:, :, 1:], tap(2), o[:, :, :-1], ALU.mult, ALU.add)
        r.free = t
        sg = M.act([t, turned] + ([ut[0]] if h else []), nc.scalar.activation, act1, u[:, h, :], ACT.Sigmoid)
        ut[h] = M.dve(sg, tt, u[:, h, :], u[:, h, :], act1, ALU.mult)
    NX, NB = INNER + 2 * STATE, 2 * STATE
    parts = M.alloc(TOKENS // 2).bitcast(BF16)[0:3 * NB]
    rest = M.ring(2, GROUP)
    xd = du
    for g in range(GROUPS):
        sl = slice(g * GROUP, (g + 1) * GROUP)
        for m0, mn, dst in ((0, P, xd[:, 0, sl]), (P, P, xd[:, 1, sl]), (2 * P, 2 * STATE, None)):
            b, free = banks.take()
            t = M.mm([free, ut[0], ut[1]], [(b.ap[0:mn, :], [(w("xp")[:, h * NX + m0:h * NX + m0 + mn], u[:, h, sl])
                                                             for h in range(2)])])
            if m0 < 2 * P:
                t = xdt = M.copy(M.act, t, dst, b.ap[0:mn, :])
            else:
                r, free = rest.take()
                hi, mid, lo = (parts[k * NB:(k + 1) * NB, sl] for k in range(3))
                t = M.copy(M.act, t, hi, b.ap[0:NB, :])
                t = M.dve([t, free], tt, r.ap[0:NB], b.ap[0:NB, :], hi, ALU.subtract)
                b.free = t
                t = M.dve(t, nc.vector.tensor_copy, mid, r.ap[0:NB])
                t = r.free = M.dve(t, tt, lo, r.ap[0:NB], mid, ALU.subtract)
                continue
            b.free = t
    selectors = M.alloc(STATE).bitcast(BF16)[0:3 * NB]
    sel_t = M.dve([], tt, selectors, c("ident")[0:3 * NB, 0:NB], c("ident")[0:3 * NB, NB:2 * NB], ALU.add)
    sel_t = M.dve(sel_t, tt, selectors, selectors, c("ident")[0:3 * NB, 2 * NB:3 * NB], ALU.add)
    ready_d, projected = [], {}
    for h in range(2):
        for g in range(GROUPS):
            sl = slice(g * GROUP, (g + 1) * GROUP)
            b, free = banks.take()
            t = M.mm([free, xdt], [(b.ap, [(w("dt")[:, k * INNER + h * P:k * INNER + h * P + P], xd[:, k, sl])
                                           for k in range(2)])])
            t = M.dve(t, ts, dl[:, h, sl], b.ap, w("dtb")[:, h:h + 1], None, ALU.add)
            b.free = t
            projected[h, g] = t
    dt_used = t
    N = TOKENS // 2
    halves = lambda ap, after: Ring([Slot(ap[:, 0:N], after), Slot(ap[:, N:], after)])
    expo, sums, logs = (halves(act1, ut[1]), halves(raw.slots[0].ap, raw.slots[0].free),
                        halves(M.y.rearrange("p t d -> p (t d)"), []))

    def softplus(h, part):
        d = dl[:, h, part * N:(part + 1) * N]
        x, xfree = expo.take()
        y, yfree = sums.take()
        l, lfree = logs.take()
        t = M.dve([projected[h, 2 * part + 1], xfree], stt, x.ap, d, -1.0, d, ALU.mult, ALU.min)
        t = M.act(t, nc.scalar.activation, x.ap, x.ap, ACT.Exp)
        yield
        t = M.dve([t, yfree], ts, y.ap, x.ap, 1.0, None, ALU.add)
        c_ = M.dve(t, stt, x.ap, y.ap, -1.0, x.ap, ALU.add, ALU.subtract)
        t = M.act([t, lfree], nc.scalar.activation, l.ap, y.ap, ACT.Ln)
        t = M.act([t, c_], nc.scalar.activation, y.ap, l.ap, ACT.Exp, scale=-1.0)
        yield
        t = M.dve([t, c_], tt, x.ap, x.ap, y.ap, ALU.mult)
        y.free = t
        t = M.dve(t, tt, l.ap, l.ap, x.ap, ALU.subtract)
        x.free = t
        t = M.dve(t, stt, d, d, 0.0, l.ap, ALU.max, ALU.add)
        l.free = t
        ready_d.append(t)

    pipeline(softplus(h, part) for h in range(2) for part in range(2))
    for h in range(2):
        t = M.dve([ready_d, dt_used], tt, du[:, h, :], dl[:, h, :], u[:, h, :], ALU.mult)
    du_t = t
    am = M.alloc(2 * STATE)
    t = M.dve([], ts, am, w("alog"), 88.7, None, ALU.min)
    t = M.act(t, nc.scalar.activation, am, am, ACT.Exp)
    a_t = M.dve(t, ts, am, am, -1.0, None, ALU.mult)
    start = M.everything()
    for b_ in M.bank:
        b_.free = start
    fr = [M.xn.rearrange("p t d -> p (t d)"), raw.slots[0].ap]
    big = [fr[0][:, 0:N], fr[0][:, N:], fr[1][:, 0:N], fr[1][:, N:]]
    yv = M.y.rearrange("p t d -> p (t d)")
    big += [yv[:, 0:N], yv[:, N:]]
    decay, inp = Ring([Slot(x, start) for x in big[0:2]]), Ring([Slot(x, start) for x in big[2:4]])
    hs = Ring([Slot(x, start) for x in big[4:6]])
    hc, csb = M.ring(2, N), M.ring(2, N)
    bk = Ring([Slot(M.psum[:, 2 * i:2 * i + 2, :].rearrange("p a b -> p (a b)"), start) for i in range(3)])
    ybank = M.psum[:, 6:8, :].rearrange("p a b -> p (a b)")
    yfree = start
    gated = {}

    def unit(h, part, s, ctx_):
        sl = slice(part * N, (part + 1) * N)
        spread = lambda k: [(b.ap[:, j:j + GROUP], [(selectors[:, k:k + 1].broadcast_to([3 * NB, P]),
                                                     parts[:, part * N + j:part * N + j + GROUP])])
                            for j in range(0, N, GROUP)]
        b, free = bk.take()
        bt = M.mm([free, sel_t], spread(s))
        dc, free = decay.take()
        d = M.dve([free, a_t, du_t], ts, dc.ap, dl[:, h, sl], am[:, h * STATE + s:h * STATE + s + 1],
                  -1e4, ALU.mult, ALU.max)
        d = M.dve(d, nc.vector.memset, dc.ap.rearrange("p (b n) -> p b n", n=SEQ)[:, :, 0:1], -1e4)
        d = M.act(d, nc.scalar.activation, dc.ap, dc.ap, ACT.Exp)
        yield
        i, free = inp.take()
        t = M.dve([bt, free, du_t], tt, i.ap, du[:, h, sl], b.ap, ALU.mult)
        b.free = t
        b, free = bk.take()
        ct = M.mm([free], spread(STATE + s))
        hh, free = hs.take()
        t = M.dve([t, d, free], nc.vector.tensor_tensor_scan, hh.ap, dc.ap, i.ap, 0.0, ALU.mult, ALU.add)
        dc.free = t
        i.free = t
        yield
        cs, free = csb.take()
        ct = M.copy(M.act, [ct, free], cs.ap, b.ap)
        b.free = ct
        yield
        o, free = hc.take()
        t = M.pool([t, ct, free], nc.gpsimd.tensor_tensor, o.ap, hh.ap, cs.ap, ALU.mult)
        hh.free = t
        cs.free = t
        yield
        M.pe.wait([t, ctx_["yfree"]] if s == 0 else t)
        for j in range(0, N, GROUP):
            m = nc.tensor.matmul(ybank[:, j:j + GROUP], c("ident"), o.ap[:, j:j + GROUP], start=(s == 0), stop=(s == STATE - 1),
                                 skip_group_check=True)
        t = M.pe.mark(m)
        o.free = t
        if s == STATE - 1:
            yield
            t = M.dve([t], stt, u[:, h, sl], u[:, h, sl], w("dp")[:, h:h + 1], ybank, ALU.mult, ALU.add)
            ctx_["next"]["yfree"] = t
            gated[h, part] = t

    ctxs = [{"yfree": start}]
    us = []
    for h in range(2):
        for part in range(2):
            ctxs.append({})
            ctxs[-2]["next"] = ctxs[-1]
            us += [unit(h, part, s, ctxs[-2]) for s in range(STATE)]
    pipeline(us)
    end = M.everything()
    for b_ in M.bank:
        b_.free = end
    banks = Ring(M.bank)
    ya = Ring([Slot(big[0][:, 0:GROUP], end), Slot(big[0][:, GROUP:], end)])
    done = []
    gt = {}
    for g in range(GROUPS):
        sl = slice(g * GROUP, (g + 1) * GROUP)
        for h in range(2):
            b, free = banks.take()
            t = M.mm([free], [(b.ap, [(w("in")[:, INNER + h * P:INNER + h * P + P], M.xnT[:, sl])])])
            s, free = ya.take()
            t1 = M.act([t, free], nc.scalar.activation, s.ap, b.ap, ACT.Silu)
            b.free = t1
            t = M.dve([t1, gated[h, g // 2]], tt, u[:, h, sl], u[:, h, sl], s.ap, ALU.mult)
            s.free = t
            gt[h] = t
        b, free = banks.take()
        t = M.mm([free, gt[0], gt[1]], [(b.ap[:, P * k:P * k + P],
                                         [(u[:, h, g * GROUP + k * P:g * GROUP + k * P + P],
                                           w("out")[:, h * P:h * P + P]) for h in range(2)]) for k in range(4)])
        t = M.copy(M.act, [t, end], M.y[:, 4 * g:4 * g + 4, :], b.ap.rearrange("p (k n) -> p k n", k=4))
        b.free = t
        done += [t] * 4
    return done


def stage_gqa(M, ready):
    nc, c, w = M.nc, M.c, lambda n: M.w("gqa", n)
    wait_w = M.loaded["gqa"][0]
    tt, ts, stt = nc.vector.tensor_tensor, nc.vector.tensor_scalar, nc.vector.scalar_tensor_tensor
    banks = Ring(M.bank)

    def rms(after, src, out, sq):
        ss = M.stats[:, 400:400 + TILES]
        t = M.act([after, wait_w], nc.scalar.activation, sq, src, ACT.Square)
        M.dve.wait(wait_w)
        t = M.dve(t, nc.vector.tensor_reduce, ss, sq, AX, ALU.add)
        t = M.dve(t, ts, ss, ss, 1.0 / DIM, EPS, ALU.mult, ALU.add)
        inv = M.stats[:, 432:432 + TILES]
        t = M.rsqrt(t, ss, inv, M.stats[:, 464:464 + TILES])
        return [M.dve(t, ts, out[:, i, :], src[:, i, :], inv[:, i:i + 1], None, ALU.mult) for i in range(TILES)]

    h1 = M.y
    at = M.used
    sq = M.alloc(TILES, DIM)
    n1 = rms(ready, M.xn, h1, sq)
    turned = M.turn(n1, h1, M.xnT, banks, scale=w("ln1"))
    M.used = at
    start = M.everything()
    for b in M.bank:
        b.free = start
    rings = M.attention_rings(3, 2, 1, on_pool=(0, 1, 2, 4, 5, 6))
    rings["A"] = M.ring(2, 4 * P)
    gen = Ring(M.bank[6:8])
    for r in [*rings["P"].slots, *rings["PT"].slots]:
        r.free = start
    kq, vs = M.ring(2, 2, 4, SEQ), M.ring(3, 2, P)
    rot, cs = M.ring(2, 2, SEQ), M.ring(2, 2, SEQ)
    for ring_ in (kq, rot, cs, rings["A"], rings["small"]):
        for s in ring_.slots:
            s.free = start
    for s in vs.slots:
        s.free = M.pool(start, nc.gpsimd.memset, s.ap, 0.0)
    state, done_y = {}, [None] * TILES

    def prepare(b):
        sl = slice(b * SEQ, (b + 1) * SEQ)
        slot, kfree = kq.take()
        outs = []
        for which, (name, rname) in enumerate((("wqs", "wqr"), ("wks", "wkr"))):
            for pc in range(2):
                parts = []
                for nm, tab, ring_ in ((name, "cosT", cs), (rname, "sinT", rot)):
                    bank, free = gen.take()
                    t = M.mm([free, turned[b // 2], wait_w], [(bank.ap[:, i * SEQ:(i + 1) * SEQ],
                             [(w(nm)[:, (2 * pc + i) * P:(2 * pc + i + 1) * P], M.xnT[:, sl])]) for i in range(2)])
                    yield
                    s, free = ring_.take()
                    t = M.dve([t, free], tt, s.ap, bank.ap.rearrange("p (c n) -> p c n", c=2),
                              c(tab).unsqueeze(1).broadcast_to([P, 2, SEQ]), ALU.mult)
                    bank.free = t
                    parts.append((s, t))
                t = M.pool([parts[0][1], parts[1][1], kfree], nc.gpsimd.tensor_tensor, slot.ap[:, which, 2 * pc:2 * pc + 2, :],
                           parts[0][0].ap, parts[1][0].ap, ALU.add)
                parts[0][0].free = t
                parts[1][0].free = t
                outs.append(t)
        bank, free = gen.take()
        v, vfree = vs.take()
        t = M.mm([free], [(bank.ap[:, i * 32:i * 32 + 32], [(M.xnT[:, b * SEQ + i * P:b * SEQ + (i + 1) * P], w("wv"))]) for i in range(2)])
        yield
        for i in range(2):
            vt = M.copy(M.act, [t, vfree], v.ap[:, i, :].rearrange("p (h d) -> p h d", h=4)[:, :, 0:HDIM],
                        bank.ap[:, i * 32:i * 32 + 32].rearrange("p (h d) -> p h d", h=4))
        bank.free = vt
        state[b] = {"q": slot.ap[:, 0], "k": slot.ap[:, 1], "v": v.ap, "ready": outs, "vready": vt, "slots": (slot, v)}

    out = project_out(M, gen, w("wo"), wait_w, done_y)

    def finish(attn, done, t):
        yield from out(attn, done, t)

    run_batches(prepare, rate=1, pairs=lambda b: attention_heads8(M, "gqa", rings, state, lambda h: h // 4, lambda half: c("causal"), None,
                                                    HDIM ** -0.5, finish, b))
    end = M.everything()
    for e in (M.pe, M.act, M.dve, M.pool):
        e.wait(end)
    for b in M.bank:
        b.free = []
    banks = Ring(M.bank)
    M.used = at
    h2, sq = M.alloc(TILES, DIM), M.alloc(TILES, DIM)
    t = M.dve(done_y, tt, M.xn, M.xn, M.y, ALU.add)
    t = M.dve(t, ts, M.xn, M.xn, 100.0, -100.0, ALU.min, ALU.max)
    n2 = rms(t, M.xn, h2, sq)
    turned = M.turn(n2, h2, M.xnT, banks, scale=w("ln2"))
    M.used = at
    coef, ct = router(M, M.xnT, [turned, n2, wait_w], w("wr"), EXP2, banks)
    y0 = M.dve([], nc.vector.tensor_copy, M.y, M.xn)
    done = experts(M, "gqa", EXP2, M.xnT, turned, coef, ct, False, [y0] * TILES)
    clipped = [M.dve(done[4 * g], ts, M.y[:, 4 * g:4 * g + 4, :], M.y[:, 4 * g:4 * g + 4, :], 100.0, -100.0, ALU.min, ALU.max)
               for g in range(GROUPS)]
    return [clipped[t // 4] for t in range(TILES)]


def stage_mla(M, ready):
    nc, c, w = M.nc, M.c, lambda n: M.w("mla", n)
    wait_w = M.loaded["mla"][0]
    banks = Ring(M.bank)
    turned = M.turn(ready, M.xn, M.xnT, banks)
    start = M.everything()
    for b in M.bank:
        b.free = start
    rings = M.attention_rings(3, 2, 1, on_pool=(1, 3, 5, 7))
    rings["A"] = M.ring(2, 4 * P)
    gen = Ring(M.bank[6:8])
    kq, kv, lat = M.ring(2, 2, 4, SEQ), M.ring(2, SEQ), M.ring(2, SEQ)
    vs = zero_ring(M, 3, 2, 4 * P)
    spread_v = lambda v: v.rearrange("p b (h d) -> p b h d", h=HEADS)[:, :, :, 0:HDIM]
    state, done_y = {}, [None] * TILES

    def prepare(b):
        sl = slice(b * SEQ, (b + 1) * SEQ)
        slot, kfree = kq.take()
        outs = []
        bank, free = gen.take()
        t = M.mm([free, turned[b // 2], wait_w], [(bank.ap[:, 0:SEQ], [(w("Wk"), M.xnT[:, sl]), (w("Wv"), M.xnT[:, sl])])])
        yield
        s, free = kv.take()
        t = M.copy(M.act, [t, free], s.ap, bank.ap[:, 0:SEQ])
        yield
        t = M.mm(t, [(bank.ap[0:LATENT, SEQ:2 * SEQ], [(w("down"), s.ap)])])
        s.free = t
        yield
        l, free = lat.take()
        lt = M.copy(M.act, [t, free], l.ap[0:LATENT], bank.ap[0:LATENT, SEQ:2 * SEQ])
        bank.free = lt
        yield
        for which in range(2):
            for pc in range(2):
                bank, free = gen.take()
                wt = w("wqs") if which == 0 else w("upk")[0:LATENT]
                src = M.xnT[:, sl] if which == 0 else l.ap[0:LATENT]
                t = M.mm([free, lt], [(bank.ap[:, i * SEQ:(i + 1) * SEQ], [(wt[:, (2 * pc + i) * P:(2 * pc + i + 1) * P], src)])
                                      for i in range(2)])
                yield
                t = M.copy(M.act, [t, kfree], slot.ap[:, which, 2 * pc:2 * pc + 2, :], bank.ap.rearrange("p (c n) -> p c n", c=2))
                bank.free = t
                outs.append(t)
        bank, free = gen.take()
        v, vfree = vs.take()
        t = M.mm([free], [(bank.ap[:, i * P:i * P + P], [(l.ap[0:LATENT, i * P:i * P + P], w("upv")[0:LATENT])]) for i in range(2)])
        l.free = t
        yield
        for i in range(2):
            vt = M.copy(M.act, [t, vfree], spread_v(v.ap)[:, i], bank.ap[:, i * P:i * P + P].rearrange("p (h d) -> p h d", h=HEADS))
        bank.free = vt
        state[b] = {"q": slot.ap[:, 0], "k": slot.ap[:, 1], "v": v.ap, "ready": outs, "vready": vt, "slots": (slot, v)}

    out = project_out(M, gen, w("Wo"), wait_w, done_y)

    def finish(attn, done, t):
        yield from out(attn, done, t)

    scale = float(np.float32(1.0) / (np.sqrt(np.float32(DIM)) + np.float32(1e-8)))
    run_batches(prepare, lambda b: attention_heads8(M, "mla", rings, state, lambda h: h,
                                                    lambda half: c("decay")[:, half * SEQ:(half + 1) * SEQ], CLAMP / scale,
                                                    scale, finish, b))
    return done_y


def stage_local(M, ready):
    nc, c = M.nc, M.c
    tt, ts, stt = nc.vector.tensor_tensor, nc.vector.tensor_scalar, nc.vector.scalar_tensor_tensor
    xT = M.xnT
    turned = M.turn(ready, M.xn, xT, Ring(M.bank))
    start = M.everything()
    for e in (M.pe, M.act, M.dve, M.pool):
        e.wait(start)
    for b in M.bank:
        b.free = []
    layer_width = M.dram["layer0"].shape[1]
    M.extra = [[M.xn.rearrange("p t d -> p (t d)"), TILES * DIM, 0], [M.y.rearrange("p t d -> p (t d)"), TILES * DIM, 0],
               [M.weights[0][:, layer_width:], M.weights[0].shape[1] - layer_width, 0],
               [M.weights[1][:, layer_width:], M.weights[1].shape[1] - layer_width, 0]]
    rings = {"S": Ring(M.bank[0:2]), "T": Ring(M.bank[2:4]), "O": Ring(M.bank[4:5]),
             "P": M.ring(5, 2, 256), "PT": M.ring(3, 512), "on_pool": (1,), "on_act": (2, 3, 6, 7), "small": M.ring(4, 3, 16), "A": M.ring(2, 512)}
    gen = Ring(M.bank[5:8])
    for s in rings["P"].slots:
        s.free = M.pool([], nc.gpsimd.memset, s.ap, 0.0)
    shifted = M.ring(3, SEQ)
    for s in shifted.slots:
        s.free = M.pool([], nc.gpsimd.memset, s.ap, 0.0)
    rope = M.ring(2, 4, 2, LDIM)
    A, B, SQ, NRM = M.ring(5, 512), M.ring(2, 512), M.ring(2, 512), M.ring(2, 3, 32)
    QT, KT, V = M.ring(4, 8, P), M.ring(3, 8, SEQ), M.ring(5, LIN)
    XC, SQ2, XN, AG, GL = M.ring(1, SEQ), M.ring(1, SEQ), M.ring(2, SEQ), M.ring(2, 3, SEQ), M.ring(3, SEQ)
    RAW = M.ring(2, 512)
    VAR, DG = M.ring(2, 3, 2), M.ring(1, 2, P)
    res = [turned[b // 2] for b in range(BATCH)]
    tabs, tile_state = {}, {}
    HB = 8
    WAIT_STEPS, RATE = 6, 5

    def shift(b, after):
        s, free = yield from shifted.get()
        x = xT[:, b * SEQ:(b + 1) * SEQ]
        t1 = M.dve([after, free], nc.vector.tensor_copy, s.ap[0:64], x[0:64])
        t2 = M.dve([], nc.vector.tensor_copy, s.ap[64:P, 1:], x[64:P, :-1])
        return s, [t1, t2]

    def layer_tables(l):
        if l in tabs:
            return
        w = lambda n: M.w(f"layer{l}", n)
        s, free = rope.take()
        t = [free, M.loaded[f"layer{l}"][0]]
        two = lambda ap: ap.rearrange("p (a d) -> p a d", a=2)
        out = [M.pool(t, nc.gpsimd.tensor_tensor, s.ap[:, i], two(c(tab)), w(sc).unsqueeze(1).broadcast_to([P, 2, LDIM]),
                      ALU.mult)
               for i, (tab, sc) in enumerate((("rqc", "qs"), ("rqs", "qsr"), ("rkc", "ks"), ("rks", "ksr")))]
        tabs[l] = (s, out)

    def prepare(n):
        l, b = divmod(n, BATCH)
        layer_tables(l)
        w = lambda nm: M.w(f"layer{l}", nm)
        wt = M.loaded[f"layer{l}"][0]
        tab, tab_t = tabs[l]
        xs, xst = yield from shift(b, res[b])
        yield
        yield
        last = []
        for i in range(2):
            st = {}
            nr, nfree = yield from NRM.get()
            lens, inv, room = nr.ap[:, 0, :], nr.ap[:, 1, :], nr.ap[:, 2, :]
            heads = lambda ap: ap.rearrange("p (h d) -> p h d", d=LDIM)
            bc = lambda ap, k: ap.unsqueeze(1).broadcast_to([P, HB, k])
            hd = LDIM // 2
            parts = []
            for part in range(4):
                which = part // 2
                bank, free = yield from gen.get()
                at = part * 512
                t = M.mm([free, xst, wt], [(bank.ap, [(xs.ap[:, i * P:i * P + P], w("wqkv")[:, at:at + 512])])])
                last.append(t)
                yield
                raw, free = yield from RAW.get()
                t = M.copy(M.act, [t, free], raw.ap, bank.ap)
                bank.free = t
                sq, free = yield from SQ.get()
                t0 = M.act([t, free], nc.scalar.activation, sq.ap, raw.ap, ACT.Square)
                yield
                src = heads(raw.ap)
                ct, st_ = tab.ap[:, 2 * which, i, :], tab.ap[:, 2 * which + 1, i, :]
                a, free = yield from A.get()
                t1 = M.dve([t, free, tab_t], tt, heads(a.ap), src, bc(ct, LDIM), ALU.mult)
                r, free = yield from B.get()
                t2 = M.dve([free], tt, heads(r.ap)[:, :, 0:hd], src[:, :, hd:], bc(st_[:, 0:hd], hd), ALU.mult)
                t3 = M.dve([], tt, heads(r.ap)[:, :, hd:], src[:, :, 0:hd], bc(st_[:, hd:], hd), ALU.mult)
                raw.free = [t0, t3]
                t1 = M.pool([t1, t2, t3], nc.gpsimd.tensor_tensor, a.ap, a.ap, r.ap, ALU.add)
                r.free = t1
                t4 = M.dve([t0, nfree], nc.vector.tensor_reduce, lens[:, 8 * part:8 * part + 8], heads(sq.ap), AX, ALU.add)
                sq.free = t4
                parts.append((a, t1, t4))
            t4 = M.dve([p[2] for p in parts], ts, lens, lens, 1e-24, None, ALU.max)
            t4 = M.rsqrt(t4, lens, inv, room)
            for part, (a, t1, _) in enumerate(parts):
                t1 = M.pool([t4, t1], nc.gpsimd.tensor_tensor, heads(a.ap), heads(a.ap),
                            inv[:, 8 * part:8 * part + 8].unsqueeze(2).broadcast_to([P, HB, LDIM]), ALU.mult)
                parts[part] = (a, t1)
            nr.free = t1
            yield
            v, vfree = yield from V.get()
            outs = []
            for hf in range(2):
                bank, free = yield from gen.get()
                at = 2 * LIN + hf * 512
                t = M.mm([free], [(bank.ap, [(xs.ap[:, i * P:i * P + P], w("wqkv")[:, at:at + 512])])])
                last.append(t)
                yield
                t = M.copy(M.act, [t, vfree], v.ap[:, hf * 512:hf * 512 + 512], bank.ap)
                bank.free = t
                outs.append(t)
            st["v"] = (v, outs)
            tile_state[n, i] = st
            for _ in range(WAIT_STEPS):
                yield
            for part, (a, t1) in enumerate(parts):
                if part == 0:
                    dst, dfree = yield from QT.get()
                if part == 2 and i == 0:
                    keys, kfree = yield from KT.get()
                if part == 2:
                    dst, dfree = keys, kfree
                if part % 2 == 0:
                    outs = []
                bank, free = yield from gen.get()
                t = M.transposes([t1, free], [(bank.ap[:, j:j + P], a.ap[:, j:j + P]) for j in range(0, 512, P)])
                a.free = t
                yield
                hf = part % 2
                place = dst.ap[:, 4 * hf:4 * hf + 4, :] if part < 2 else dst.ap[:, 4 * hf:4 * hf + 4, i * P:(i + 1) * P]
                t = M.copy(M.dve if hf else M.act, [t, dfree], place, bank.ap.rearrange("p (k n) -> p k n", k=4))
                bank.free = t
                outs.append(t)
                st[part // 2] = (dst, outs)
        xs.free = last
        tab.free = last
        prepared.add(n)

    adds, finished, prepared = {}, {}, {0}

    def pairs(n):
        l, b = divmod(n, BATCH)
        w = lambda nm: M.w(f"layer{l}", nm)
        for i in range(2):
            st = tile_state[n, i]
            prev = tile_state[n, 0] if i else None
            segments = [(P - LWIN, LWIN + P)] if i else [(P, P)]
            of = lambda col, st=st, prev=prev: st if col >= P else prev

            def finish(attn, done, g, i=i, st=st, n=n, b=b, w=w):
                bank, free = yield from gen.get()
                t = M.mm([free, done], [(bank.ap[:, 0:P], [(w("wo")[:, (4 * g + k) * DIM:(4 * g + k + 1) * DIM],
                                                            attn.ap[:, k * P:k * P + P]) for k in range(4)])])
                attn.free = t
                yield
                x = xT[:, b * SEQ + i * P:b * SEQ + (i + 1) * P]
                t = M.dve([t, adds.get((n, i))], tt, x, bank.ap[:, 0:P], x, ALU.add)
                bank.free = t
                adds[n, i] = t
                finished[n] = finished.get(n, 0) + 1

            def scored(token, i=i, n=n, st=st):
                st[0][0].free = token
                both(tile_state[n, 0], "scored", token, st[1][0])

            def valued(token, i=i, n=n, st=st):
                both(tile_state[n, 0], "valued", token, tile_state[n, 0]["v"][0], tile_state[n, 1]["v"][0])

            tile = {"order": [(h, h + 2) for h in range(LHEADS) if h % 4 < 2], "scored": scored, "valued": valued,
                    "ready": [st[0][1], st[1][1]] + ([prev[1][1]] if prev else []),
                    "vready": [st["v"][1]] + ([prev["v"][1]] if prev else []), "segments": segments, "mask": c("band"),
                    "q": lambda h, st=st: st[0][0].ap[64 * (h % 2):64 * (h % 2) + 64, h // 2, :],
                    "k": lambda h, sg, st=st, i=i: st[1][0].ap[64 * (h % 2):64 * (h % 2) + 64, h // 2,
                                                               sg[0] - P + i * P:sg[0] - P + i * P + sg[1]],
                    "v": lambda h, blk, of=of: of(blk * P)["v"][0].ap[:, LDIM * h:LDIM * h + LDIM]}
            yield from M.attend(rings, LHEADS, LDIM, 8.0, tile, finish)

    def feed(n):
        l, b = divmod(n, BATCH)
        w = lambda nm: M.w(f"layer{l}", nm)
        while finished.get(n, 0) < 4:
            yield
        xs, t = yield from shift(b, [adds[n, 0], adds[n, 1]])
        yield
        bank, free = yield from gen.get()
        t = M.mm([free, t], [(bank.ap[:, 0:SEQ], [(c("center"), xs.ap)])])
        xs.free = t
        yield
        xc, free = yield from XC.get()
        t1 = M.copy(M.act, [t, free], xc.ap, bank.ap[:, 0:SEQ])
        sq, free = yield from SQ2.get()
        t2 = M.act([free], nc.scalar.activation, sq.ap, bank.ap[:, 0:SEQ], ACT.Square)
        yield
        t = M.mm([t1, t2], [(bank.ap[:, SEQ + i:SEQ + i + 1], [(sq.ap[:, i * P:i * P + P], c("mean")[:, 0:1])]) for i in range(2)])
        sq.free = t
        yield
        v, free = yield from VAR.get()
        t = M.dve([t, free], ts, v.ap[:, 0, :], bank.ap[:, SEQ:SEQ + 2], EPS, None, ALU.add)
        t = M.rsqrt(t, v.ap[:, 0, :], v.ap[:, 1, :], v.ap[:, 2, :])
        dg, free = yield from DG.get()
        for i in range(2):
            t = M.dve([t, free], ts, dg.ap[:, i, :], c("ident"), v.ap[:, 1, i:i + 1], None, ALU.mult)
        v.free = t
        yield
        t = M.mm(t, [(bank.ap[:, SEQ + i * P:SEQ + (i + 1) * P], [(c("ones"), dg.ap[:, i, :])]) for i in range(2)])
        dg.free = t
        yield
        xn, free = yield from XN.get()
        t = M.dve([t, free, t1], tt, xn.ap, xc.ap, bank.ap[:, SEQ:], ALU.mult)
        xc.free = t
        bank.free = t
        t = M.dve(t, ts, xn.ap, xn.ap, w("lng"), w("lnb"), ALU.mult, ALU.add)
        ag, afree = yield from AG.get()
        ready = []
        yield
        gated = []
        for j, (at, m) in enumerate(GLU_PARTS):
            bank, free = yield from gen.get()
            t1 = M.mm([t, free], [(bank.ap[0:m, 0:SEQ], [(w("w1")[:, at:at + m], xn.ap)]),
                                  (bank.ap[0:m, SEQ:], [(w("w1")[:, GLU + at:GLU + at + m], xn.ap)])])
            gl, free = yield from GL.get()
            t2 = M.act([t1, free], nc.scalar.activation, gl.ap[0:m], bank.ap[0:m, SEQ:], ACT.Gelu,
                       bias=w("b1")[0:m, 3 + j:4 + j])
            gated.append((bank, gl, t2))
        yield
        for j, (at, m) in enumerate(GLU_PARTS):
            bank, gl, t2 = gated[j]
            t2 = M.dve([t2, afree], stt, ag.ap[0:m, j, :], bank.ap[0:m, 0:SEQ], w("b1")[0:m, j:j + 1], gl.ap[0:m],
                       ALU.add, ALU.mult)
            bank.free = t2
            gl.free = t2
            ready.append(t2)
        xn.free = t1
        yield
        bank, free = yield from gen.get()
        t = M.mm([free, ready], [(bank.ap[:, 0:SEQ], [(w("w2")[0:m, j * DIM:(j + 1) * DIM], ag.ap[0:m, j, :])
                                                      for j, (at, m) in enumerate(GLU_PARTS)])])
        ag.free = t
        yield
        x = xT[:, b * SEQ:(b + 1) * SEQ]
        t = M.dve(t, stt, x, bank.ap[:, 0:SEQ], w("b2"), x, ALU.add, ALU.add)
        bank.free = t
        res[b] = t
        layer_end.setdefault(l, []).append(t)

    layer_end = {}
    steps = DEPTH * BATCH
    for _ in prepare(0):
        pass

    following = [iter(())]

    def units():
        for n in range(steps):
            nxt = following[0] = prepare(n + 1) if n + 1 < steps else iter(())
            for k, p in enumerate(pairs(n)):
                yield p
                if k == 14 and n:
                    yield feed(n - 1)
                if k == 15 and n and n % BATCH == 4 and n // BATCH + 1 < DEPTH and n >= BATCH:
                    M.load(f"layer{n // BATCH + 1}", (n // BATCH + 1) % 2, layer_end[n // BATCH - 1])
            while n + 1 < steps and n + 1 not in prepared:
                yield iter(())
        yield feed(steps - 1)

    pipeline(units(), lambda: next(following[0], None), RATE)
    end = M.everything()
    for b in M.bank:
        b.free = end
    banks = Ring(M.bank)
    done = []
    for g in range(GROUPS):
        b, free = banks.take()
        t = M.transposes([free], [(b.ap[:, P * k:P * k + P], xT[:, GROUP * g + P * k:GROUP * g + P * k + P]) for k in range(4)])
        t = M.copy(M.act, t, M.y[:, 4 * g:4 * g + 4, :], b.ap.rearrange("p (k n) -> p k n", k=4))
        b.free = t
        done += [t] * 4
    M.extra = []
    return done


STAGES = [("titan", 1, stage_titan), ("split", 0, stage_split), ("linear", 1, stage_linear), ("moe1", 0, stage_moe1),
          ("mamba", 1, stage_mamba), ("gqa", 0, stage_gqa), ("mla", 1, stage_mla), ("layer0", 0, stage_local)]
FIRST, LAST = 0, 8


def build(nc, dram, places, x_in, x_out):
    with ExitStack() as ctx:
        width = lambda n: dram[n].shape[1]
        sizes = {"table": width("table"), "w0": max(width(n) for n in ("split", "moe1", "gqa", "layer0")),
                 "w1": max(width(n) for n in ("titan", "linear", "mamba", "mla", "layer1"))}
        fixed = 4 * TILES * DIM + 512 + sizes["table"] + sizes["w0"] + sizes["w1"]
        sizes["scratch"] = min(22400, 212000 // 4 - fixed)
        M = Machine(nc, ctx, dram, places, sizes)
        tokens = "(t p) d -> p t d"
        src, dst = (a.rearrange("b s d -> (b s) d").rearrange(tokens, p=P) for a in (x_in, x_out))
        x_sem, out_sem = M.sem("x_loaded"), M.sem("out_stored")
        nc.sync.dma_start(M.x, src).then_inc(x_sem, 16)
        stages = STAGES[FIRST:LAST]
        M.load("table", None)
        for name, region, _ in stages[:2]:
            M.load(name, region)
        if len(stages) == 1 and stages[0][0] == "layer0":
            M.load("layer1", 1)
        M.extra = []
        x_ready, ends = [(x_sem, 16)], [[]]
        for e in (M.pe, M.act, M.dve, M.pool):
            e.wait(M.loaded["table"][0])
        for i, (name, _, stage) in enumerate(stages):
            if i >= 1 and i + 1 < len(stages):
                M.load(stages[i + 1][0], stages[i + 1][1], M.everything())
            if i >= 1 and i == len(stages) - 1 and name == "layer0":
                M.load("layer1", 1, M.everything())
            M.begin(M.everything())
            ready = M.normalise(x_ready, M.x, M.xn)
            done = stage(M, ready)
            t = M.normalise([done, M.everything()], M.y, M.y)
            add = lambda eng, issue, sl: eng([t, x_ready], issue, M.x[:, sl, :], M.x[:, sl, :], M.y[:, sl, :], ALU.add)
            split = 11
            x_ready = [add(M.dve, nc.vector.tensor_tensor, slice(0, split)),
                       add(M.pool, nc.gpsimd.tensor_tensor, slice(split, TILES))]
        M.sp.wait(x_ready)
        nc.sync.dma_start(dst, M.x).then_inc(out_sem, 16)
        nc.sync.wait_ge(out_sem, 16)


def kernel(**inputs):
    from concourse import bacc
    from concourse.bass_utils import run_bass_kernel_spmd

    nc = bacc.Bacc("TRN2", target_bir_lowering=False, num_devices=1)
    arrays, dram, places = {}, {}, {}
    packs = {"table": tables(), **layout(inputs)}
    for name, parts in packs.items():
        arrays[name + "_dram"], places[name] = pack(parts)
        dram[name] = nc.dram_tensor(name + "_dram", arrays[name + "_dram"].shape, F32, kind="ExternalInput").ap()
    arrays["x_dram"] = np.ascontiguousarray(inputs["L0_attn_x"])
    x_in = nc.dram_tensor("x_dram", (BATCH, SEQ, DIM), F32, kind="ExternalInput").ap()
    x_out = nc.dram_tensor("out_dram", (BATCH, SEQ, DIM), F32, kind="ExternalOutput").ap()
    build(nc, dram, places, x_in, x_out)
    r = run_bass_kernel_spmd(nc, [arrays], core_ids=[0])
    return r.results[0]["out_dram"]
```
